# Optimizing a Trainium2 kernel written in Bass

```python
import numpy as np
import jax
import jax.numpy as jnp

def _softmax(x, axis=-1):
    return jax.nn.softmax(x, axis=axis)

def _gelu(x):
    return jax.nn.gelu(x, approximate=True)

def _silu(x):
    return jax.nn.silu(x)

def _sigmoid(x):
    return jax.nn.sigmoid(x)

def _layernorm(x, axis=-1, eps=1e-05):
    m = jnp.mean(x, axis=axis, keepdims=True)
    v = jnp.var(x, axis=axis, keepdims=True)
    return (x - m) / jnp.sqrt(v + eps)

def _scatter_add(tgt, idx, src, axis=0):
    return tgt.at[idx].add(src)

def _segment_sum(src, seg, n):
    return jax.ops.segment_sum(src, seg, n)
kernel_name = 'mk_hybrid_d1_jaxref_r4_206cfa'

def setup_inputs(seed: int=0):
    np.random.seed(seed)
    _w = jnp.asarray

    def _L0_attn_a_setup():
        import jax, jax.numpy as jnp
        import numpy as np
        EPS = 1e-05

        def rwkv6_scan(q, k, v, w, u):
            B, H, T, K = q.shape
            V = v.shape[-1]
            h0 = jnp.zeros((B, H, K, V), jnp.float32)

            def step(h, xs):
                qi, ki, vi, wi = xs
                kv = ki[..., :, None] * vi[..., None, :]
                oi = jnp.einsum('bhk,bhkv->bhv', qi, h + u[None, :, :, None] * kv)
                h = h * jnp.exp(wi)[..., None] + kv
                return (h, oi)
            xs = tuple((jnp.moveaxis(a, 2, 0) for a in (q, k, v, w)))
            _, o = jax.lax.scan(step, h0, xs)
            return jnp.moveaxis(o, 0, 2)
        key = jax.random.key(seed)
        ks = jax.random.split(key, 20)
        B, T, D = (2, 512, 256)
        H, Dk, Dv = (4, 128, 64)
        KD, VD = (H * Dk, H * Dv)
        R5, LR = (5 * 32, 64)
        s = 0.02
        rn = lambda k, shp: jax.random.normal(k, shp, dtype=jnp.float32) * s
        return {'hidden_states': jax.random.normal(ks[0], (B, T, D), dtype=jnp.float32), 'xp_mu': rn(ks[1], (D,)), 'xp_W1': rn(ks[2], (R5, D)), 'xp_W2': rn(ks[3], (D, R5)), 'x_bias': rn(ks[4], (5, D)), 'r_W': rn(ks[5], (KD, D)), 'w_A': rn(ks[6], (LR, D)), 'w_B': rn(ks[7], (KD, LR)), 'w_b': rn(ks[8], (KD,)), 'k_W': rn(ks[9], (KD, D)), 'v_W': rn(ks[10], (VD, D)), 'g_A': rn(ks[11], (LR, D)), 'g_B': rn(ks[12], (VD, LR)), 'g_b': rn(ks[13], (VD,)), 'bonus': rn(ks[14], (H, Dk)), 'gn_w': jnp.ones((VD,), jnp.float32), 'gn_b': jnp.zeros((VD,), jnp.float32), 'o_W': rn(ks[15], (D, VD))}
    _L0_attn_a_in = _L0_attn_a_setup()

    def _L0_attn_b_setup():
        import jax, jax.numpy as jnp
        import numpy as np
        import math
        D_MODEL = 256
        NUM_HEADS = 16
        HEAD_DIM = D_MODEL // NUM_HEADS
        LN_EPS = 1e-05

        def _layer_norm(x, g, b):
            mu = jnp.mean(x, axis=-1, keepdims=True)
            var = jnp.mean(jnp.square(x - mu), axis=-1, keepdims=True)
            return (x - mu) * jax.lax.rsqrt(var + LN_EPS) * g + b

        def _rope_tables(seq_len, dim, dtype):
            inv_freq = 1.0 / 10000.0 ** (jnp.arange(0, dim, 2, dtype=jnp.float32) / dim)
            t = jnp.arange(seq_len, dtype=jnp.float32)
            freqs = t[:, None] * inv_freq[None, :]
            emb = jnp.concatenate([freqs, freqs], axis=-1)
            return (jnp.cos(emb).astype(dtype), jnp.sin(emb).astype(dtype))

        def _rotate_half(x):
            x1, x2 = jnp.split(x, 2, axis=-1)
            return jnp.concatenate([-x2, x1], axis=-1)
        key = jax.random.key(seed)
        ks = jax.random.split(key, 8)
        B, S, D = (2, 512, D_MODEL)
        s_in = 1.0 / math.sqrt(D)
        return {'x': jax.random.normal(ks[0], (B, S, D), jnp.float32), 'ln1_g': jnp.ones((D,), jnp.float32), 'ln1_b': jnp.zeros((D,), jnp.float32), 'Wqkv': jax.random.normal(ks[1], (D, 3 * D), jnp.float32) * s_in, 'bqkv': jnp.zeros((3 * D,), jnp.float32), 'Wo': jax.random.normal(ks[2], (D, D), jnp.float32) * s_in, 'bo': jnp.zeros((D,), jnp.float32), 'ln2_g': jnp.ones((D,), jnp.float32), 'ln2_b': jnp.zeros((D,), jnp.float32), 'W1': jax.random.normal(ks[3], (D, 4 * D), jnp.float32) * s_in, 'b1': jnp.zeros((4 * D,), jnp.float32), 'W2': jax.random.normal(ks[4], (4 * D, D), jnp.float32) / math.sqrt(4 * D), 'b2': jnp.zeros((D,), jnp.float32)}
    _L0_attn_b_in = _L0_attn_b_setup()

    def _L0_ffn_setup():
        import jax, jax.numpy as jnp
        import numpy as np
        D_MODEL = 256
        EXPANSION = 4
        D_HIDDEN = D_MODEL * EXPANSION
        NUM_STAGES = int(np.log2(D_HIDDEN))

        def butterfly(y, weights, dim):
            lead = y.shape[:-1]
            for stage in range(weights.shape[0]):
                s = 2 ** stage
                nb = dim // (2 * s)
                yr = y.reshape(*lead, nb, 2, s)
                a = yr[..., 0, :]
                b = yr[..., 1, :]
                w = weights[stage].reshape(nb, s, 2, 2)
                na = w[..., 0, 0] * a + w[..., 0, 1] * b
                nb2 = w[..., 1, 0] * a + w[..., 1, 1] * b
                y = jnp.stack([na, nb2], axis=-2).reshape(*lead, dim)
            return y
        key = jax.random.key(seed)
        ks = jax.random.split(key, 6)
        B, S = (4, 512)
        x = jax.random.normal(ks[0], (B, S, D_MODEL), jnp.float32)
        W_exp = jax.random.normal(ks[1], (D_MODEL, D_HIDDEN), jnp.float32) * 0.02
        b_exp = jnp.zeros((D_HIDDEN,), jnp.float32)
        up_weights = jax.random.normal(ks[2], (NUM_STAGES, D_HIDDEN // 2, 2, 2), jnp.float32) * 0.02
        up_bias = jnp.zeros((D_HIDDEN,), jnp.float32)
        down_weights = jax.random.normal(ks[3], (NUM_STAGES, D_HIDDEN // 2, 2, 2), jnp.float32) * 0.02
        W_con = jax.random.normal(ks[4], (D_HIDDEN, D_MODEL), jnp.float32) * 0.02
        b_con = jnp.zeros((D_MODEL,), jnp.float32)
        down_bias = jnp.zeros((D_MODEL,), jnp.float32)
        return dict(x=x, W_exp=W_exp, b_exp=b_exp, up_weights=up_weights, up_bias=up_bias, down_weights=down_weights, W_con=W_con, b_con=b_con, down_bias=down_bias)
    _L0_ffn_in = _L0_ffn_setup()
    _d = {'L0_attn_a_hidden_states': _L0_attn_a_in['hidden_states'], 'L0_attn_a_xp_mu': _L0_attn_a_in['xp_mu'], 'L0_attn_a_xp_W1': _L0_attn_a_in['xp_W1'], 'L0_attn_a_xp_W2': _L0_attn_a_in['xp_W2'], 'L0_attn_a_x_bias': _L0_attn_a_in['x_bias'], 'L0_attn_a_r_W': _L0_attn_a_in['r_W'], 'L0_attn_a_w_A': _L0_attn_a_in['w_A'], 'L0_attn_a_w_B': _L0_attn_a_in['w_B'], 'L0_attn_a_w_b': _L0_attn_a_in['w_b'], 'L0_attn_a_k_W': _L0_attn_a_in['k_W'], 'L0_attn_a_v_W': _L0_attn_a_in['v_W'], 'L0_attn_a_g_A': _L0_attn_a_in['g_A'], 'L0_attn_a_g_B': _L0_attn_a_in['g_B'], 'L0_attn_a_g_b': _L0_attn_a_in['g_b'], 'L0_attn_a_bonus': _L0_attn_a_in['bonus'], 'L0_attn_a_gn_w': _L0_attn_a_in['gn_w'], 'L0_attn_a_gn_b': _L0_attn_a_in['gn_b'], 'L0_attn_a_o_W': _L0_attn_a_in['o_W'], 'L0_attn_b_ln1_g': _L0_attn_b_in['ln1_g'], 'L0_attn_b_ln1_b': _L0_attn_b_in['ln1_b'], 'L0_attn_b_Wqkv': _L0_attn_b_in['Wqkv'], 'L0_attn_b_bqkv': _L0_attn_b_in['bqkv'], 'L0_attn_b_Wo': _L0_attn_b_in['Wo'], 'L0_attn_b_bo': _L0_attn_b_in['bo'], 'L0_attn_b_ln2_g': _L0_attn_b_in['ln2_g'], 'L0_attn_b_ln2_b': _L0_attn_b_in['ln2_b'], 'L0_attn_b_W1': _L0_attn_b_in['W1'], 'L0_attn_b_b1': _L0_attn_b_in['b1'], 'L0_attn_b_W2': _L0_attn_b_in['W2'], 'L0_attn_b_b2': _L0_attn_b_in['b2'], 'L0_ffn_W_exp': _L0_ffn_in['W_exp'], 'L0_ffn_b_exp': _L0_ffn_in['b_exp'], 'L0_ffn_up_weights': _L0_ffn_in['up_weights'], 'L0_ffn_up_bias': _L0_ffn_in['up_bias'], 'L0_ffn_down_weights': _L0_ffn_in['down_weights'], 'L0_ffn_W_con': _L0_ffn_in['W_con'], 'L0_ffn_b_con': _L0_ffn_in['b_con'], 'L0_ffn_down_bias': _L0_ffn_in['down_bias']}
    _x0 = _d['L0_attn_a_hidden_states']
    _d['L0_attn_a_hidden_states'] = jax.random.normal(jax.random.fold_in(jax.random.key(seed), 1), (8, 512, 256), dtype=_x0.dtype)
    del _x0
    return _d

def reference(L0_attn_a_hidden_states, L0_attn_a_xp_mu, L0_attn_a_xp_W1, L0_attn_a_xp_W2, L0_attn_a_x_bias, L0_attn_a_r_W, L0_attn_a_w_A, L0_attn_a_w_B, L0_attn_a_w_b, L0_attn_a_k_W, L0_attn_a_v_W, L0_attn_a_g_A, L0_attn_a_g_B, L0_attn_a_g_b, L0_attn_a_bonus, L0_attn_a_gn_w, L0_attn_a_gn_b, L0_attn_a_o_W, L0_attn_b_ln1_g, L0_attn_b_ln1_b, L0_attn_b_Wqkv, L0_attn_b_bqkv, L0_attn_b_Wo, L0_attn_b_bo, L0_attn_b_ln2_g, L0_attn_b_ln2_b, L0_attn_b_W1, L0_attn_b_b1, L0_attn_b_W2, L0_attn_b_b2, L0_ffn_W_exp, L0_ffn_b_exp, L0_ffn_up_weights, L0_ffn_up_bias, L0_ffn_down_weights, L0_ffn_W_con, L0_ffn_b_con, L0_ffn_down_bias):

    def _L0_attn_a_ref(hidden_states, xp_mu, xp_W1, xp_W2, x_bias, r_W, w_A, w_B, w_b, k_W, v_W, g_A, g_B, g_b, bonus, gn_w, gn_b, o_W):
        import jax, jax.numpy as jnp
        import numpy as np
        EPS = 1e-05

        def rwkv6_scan(q, k, v, w, u):
            B, H, T, K = q.shape
            V = v.shape[-1]
            h0 = jnp.zeros((B, H, K, V), jnp.float32)

            def step(h, xs):
                qi, ki, vi, wi = xs
                kv = ki[..., :, None] * vi[..., None, :]
                oi = jnp.einsum('bhk,bhkv->bhv', qi, h + u[None, :, :, None] * kv)
                h = h * jnp.exp(wi)[..., None] + kv
                return (h, oi)
            xs = tuple((jnp.moveaxis(a, 2, 0) for a in (q, k, v, w)))
            _, o = jax.lax.scan(step, h0, xs)
            return jnp.moveaxis(o, 0, 2)
        B, T, D = hidden_states.shape
        H = bonus.shape[0]
        x = hidden_states
        shifted = jnp.pad(x, ((0, 0), (1, 0), (0, 0)))[:, :-1]
        delta = shifted - x
        xl = jnp.tanh((x + delta * xp_mu) @ xp_W1.T)
        xl = xl.reshape(B, T, 5, -1)
        W2 = xp_W2.reshape(D, 5, -1)
        x5 = jnp.einsum('blnr,hnr->blnh', xl, W2) + x_bias
        mur, muw, muk, muv, mug = (x5[:, :, i] for i in range(5))
        r = (x + delta * mur) @ r_W.T
        w = jnp.tanh((x + delta * muw) @ w_A.T) @ w_B.T + w_b
        k = (x + delta * muk) @ k_W.T
        v = (x + delta * muv) @ v_W.T
        g = jnp.tanh((x + delta * mug) @ g_A.T) @ g_B.T + g_b
        heads = lambda a: a.reshape(B, T, H, -1).transpose(0, 2, 1, 3)
        r, w, k, v = map(heads, (r, w, k, v))
        w = -jnp.exp(w)
        o = rwkv6_scan(r, k, v, w, bonus)
        o = o.transpose(0, 2, 1, 3).reshape(B, T, -1)
        mu = o.mean(-1, keepdims=True)
        var = ((o - mu) ** 2).mean(-1, keepdims=True)
        o = (o - mu) * jax.lax.rsqrt(var + EPS) * gn_w + gn_b
        o = o * (g * jax.nn.sigmoid(g))
        return o @ o_W.T

    def _L0_attn_b_ref(x, ln1_g, ln1_b, Wqkv, bqkv, Wo, bo, ln2_g, ln2_b, W1, b1, W2, b2):
        import jax, jax.numpy as jnp
        import numpy as np
        import math
        D_MODEL = 256
        NUM_HEADS = 16
        HEAD_DIM = D_MODEL // NUM_HEADS
        LN_EPS = 1e-05

        def _layer_norm(x, g, b):
            mu = jnp.mean(x, axis=-1, keepdims=True)
            var = jnp.mean(jnp.square(x - mu), axis=-1, keepdims=True)
            return (x - mu) * jax.lax.rsqrt(var + LN_EPS) * g + b

        def _rope_tables(seq_len, dim, dtype):
            inv_freq = 1.0 / 10000.0 ** (jnp.arange(0, dim, 2, dtype=jnp.float32) / dim)
            t = jnp.arange(seq_len, dtype=jnp.float32)
            freqs = t[:, None] * inv_freq[None, :]
            emb = jnp.concatenate([freqs, freqs], axis=-1)
            return (jnp.cos(emb).astype(dtype), jnp.sin(emb).astype(dtype))

        def _rotate_half(x):
            x1, x2 = jnp.split(x, 2, axis=-1)
            return jnp.concatenate([-x2, x1], axis=-1)
        B, S, D = x.shape
        H, hd = (NUM_HEADS, HEAD_DIM)
        normed = _layer_norm(x, ln1_g, ln1_b)
        qkv = (normed @ Wqkv + bqkv).reshape(B, S, 3, H, hd)
        qkv = jnp.transpose(qkv, (2, 0, 3, 1, 4))
        q, k, v = (qkv[0], qkv[1], qkv[2])
        cos, sin = _rope_tables(S, hd, q.dtype)
        cos = cos[None, None, :, :]
        sin = sin[None, None, :, :]
        q = q * cos + _rotate_half(q) * sin
        k = k * cos + _rotate_half(k) * sin
        scores = jnp.einsum('bhqd,bhkd->bhqk', q, k) / math.sqrt(hd)
        causal = jnp.triu(jnp.ones((S, S), dtype=bool), k=1)
        scores = jnp.where(causal[None, None], -jnp.inf, scores)
        attn = jax.nn.softmax(scores, axis=-1)
        attn_out = jnp.einsum('bhqk,bhkd->bhqd', attn, v)
        attn_out = jnp.transpose(attn_out, (0, 2, 1, 3)).reshape(B, S, D)
        attn_out = attn_out @ Wo + bo
        x = x + attn_out
        h = _layer_norm(x, ln2_g, ln2_b)
        h = jax.nn.gelu(h @ W1 + b1, approximate=False) @ W2 + b2
        return x + h

    def _L0_ffn_ref(x, W_exp, b_exp, up_weights, up_bias, down_weights, W_con, b_con, down_bias):
        import jax, jax.numpy as jnp
        import numpy as np
        D_MODEL = 256
        EXPANSION = 4
        D_HIDDEN = D_MODEL * EXPANSION
        NUM_STAGES = int(np.log2(D_HIDDEN))

        def butterfly(y, weights, dim):
            lead = y.shape[:-1]
            for stage in range(weights.shape[0]):
                s = 2 ** stage
                nb = dim // (2 * s)
                yr = y.reshape(*lead, nb, 2, s)
                a = yr[..., 0, :]
                b = yr[..., 1, :]
                w = weights[stage].reshape(nb, s, 2, 2)
                na = w[..., 0, 0] * a + w[..., 0, 1] * b
                nb2 = w[..., 1, 0] * a + w[..., 1, 1] * b
                y = jnp.stack([na, nb2], axis=-2).reshape(*lead, dim)
            return y
        h = jnp.einsum('bsd,dh->bsh', x, W_exp) + b_exp
        h = butterfly(h, up_weights, D_HIDDEN)
        h = jax.nn.gelu(h + up_bias, approximate=False)
        h = butterfly(h, down_weights, D_HIDDEN)
        y = jnp.einsum('bsh,hd->bsd', h, W_con) + b_con
        return y + down_bias
    x = L0_attn_a_hidden_states
    x = x + _L0_attn_a_ref(_layernorm(x, axis=-1), L0_attn_a_xp_mu, L0_attn_a_xp_W1, L0_attn_a_xp_W2, L0_attn_a_x_bias, L0_attn_a_r_W, L0_attn_a_w_A, L0_attn_a_w_B, L0_attn_a_w_b, L0_attn_a_k_W, L0_attn_a_v_W, L0_attn_a_g_A, L0_attn_a_g_B, L0_attn_a_g_b, L0_attn_a_bonus, L0_attn_a_gn_w, L0_attn_a_gn_b, L0_attn_a_o_W)
    x = x + _L0_ffn_ref(_layernorm(x, axis=-1), L0_ffn_W_exp, L0_ffn_b_exp, L0_ffn_up_weights, L0_ffn_up_bias, L0_ffn_down_weights, L0_ffn_W_con, L0_ffn_b_con, L0_ffn_down_bias)
    x = x + _L0_attn_b_ref(_layernorm(x, axis=-1), L0_attn_b_ln1_g, L0_attn_b_ln1_b, L0_attn_b_Wqkv, L0_attn_b_bqkv, L0_attn_b_Wo, L0_attn_b_bo, L0_attn_b_ln2_g, L0_attn_b_ln2_b, L0_attn_b_W1, L0_attn_b_b1, L0_attn_b_W2, L0_attn_b_b2)
    x = x + _L0_ffn_ref(_layernorm(x, axis=-1), L0_ffn_W_exp, L0_ffn_b_exp, L0_ffn_up_weights, L0_ffn_up_bias, L0_ffn_down_weights, L0_ffn_W_con, L0_ffn_b_con, L0_ffn_down_bias)
    return x

_drawn_inputs = setup_inputs


def setup_inputs(seed=0):
    import zlib

    import numpy as np

    out = dict(_drawn_inputs(seed))
    spreads = {'L0_attn_a_gn_w': (1.0, 0.6),
     'L0_attn_a_gn_b': (0.0, 0.8),
     'L0_attn_b_ln1_g': (1.0, 0.6),
     'L0_attn_b_ln1_b': (0.0, 0.1),
     'L0_attn_b_bqkv': (0.0, 0.1),
     'L0_attn_b_bo': (0.0, 0.1),
     'L0_attn_b_ln2_g': (1.0, 0.2),
     'L0_attn_b_ln2_b': (0.0, 0.421),
     'L0_attn_b_b1': (0.0, 0.414),
     'L0_attn_b_b2': (0.0, 0.278),
     'L0_ffn_b_exp': (0.0, 0.1),
     'L0_ffn_up_bias': (0.0, 0.1),
     'L0_ffn_b_con': (0.0, 0.1),
     'L0_ffn_down_bias': (0.0, 0.1)}
    factors = {'L0_attn_a_xp_mu': 8.0,
     'L0_attn_a_xp_W1': 8.0,
     'L0_attn_a_xp_W2': 8.0,
     'L0_attn_a_x_bias': 8.0,
     'L0_attn_a_r_W': 6.725,
     'L0_attn_a_w_A': 8.0,
     'L0_attn_a_w_B': 8.0,
     'L0_attn_a_w_b': 8.0,
     'L0_attn_a_k_W': 6.721,
     'L0_attn_a_v_W': 6.734,
     'L0_attn_a_g_A': 7.27,
     'L0_attn_a_g_B': 7.287,
     'L0_attn_a_g_b': 8.0,
     'L0_attn_a_bonus': 8.0,
     'L0_attn_a_o_W': 6.655}
    for name, (base, spread) in spreads.items():
        noise = np.random.default_rng([zlib.crc32(name.encode()), seed]).standard_normal(out[name].shape)
        drawn = base * np.exp(spread * noise) if base else spread * noise
        out[name] = jnp.asarray(drawn.astype(out[name].dtype))
    for name, factor in factors.items():
        out[name] = (out[name] * factor).astype(out[name].dtype)
    return out
```

```python
from contextlib import ExitStack

import numpy as np

import concourse.bass as bass
from concourse import mybir

F32 = mybir.dt.float32
F32R = mybir.dt.float32r
BF16 = mybir.dt.bfloat16
U16 = mybir.dt.uint16
ALU = mybir.AluOpType
ACT = mybir.ActivationFunctionType
AX_X = mybir.AxisListType.X

P = 128
B, T, D = 8, 512, 256
NT = T // P
NC = D // P
H, DK, DV = 4, 128, 64
LR = 64
NMIX, RMIX = 5, 32
NH, HD = 16, 16
HG = 4
NG = NH // HG
FF = 1024
NF = FF // P
EPS = 1e-5
STAGES = 10
LOW = 7
LEVELS = [0, 1, 2, 4, 8, 16, 32, 64]
MIX_ORDER = [1, 2, 0, 3, 4]
RING = 6
NEG = -1e30

COLS = {}
_at = 0
for _name, _n in (("mu", NC), ("xbias", NMIX * NC), ("w_b", H), ("bonus", H), ("gn_w", NC), ("gn_b", NC),
                  ("ln1_g", NC), ("ln1_b", NC), ("ln2_g", NC), ("ln2_b", NC), ("bq", NG), ("bk", NG),
                  ("b1", NF), ("up_b", NF), ("minus_row", 1)):
    COLS[_name] = _at
    _at += _n
NCOLS = _at


def psum_order():
    o = [("zt", "A", c) for c in range(NC)] + [("xl", 0), ("xl", 1)]

    def project(n):
        if n == 1:
            return [("wa",)] + [("w", h) for h in range(H)]
        if n == 2:
            return [("k", h) for h in range(H)]
        if n == 0:
            return [("r", h) for h in range(H)]
        if n == 3:
            return [("v", t) for t in range(2)]
        return [("ga",)] + [("g", c) for c in range(NC)]

    for a, n in enumerate(MIX_ORDER):
        o += [("x5", n, c) for c in range(NC)]
        if a >= 1:
            o += project(MIX_ORDER[a - 1])
    o += project(MIX_ORDER[-1])
    o += [("A", lv, h) for lv in range(len(LEVELS)) for h in range(H)]
    o += [("kt", h) for h in range(H)] + [("s", c) for c in range(NT - 1)]
    o += [("o", t) for t in range(2)] + [("ogt", c) for c in range(NC)] + [("ao", t) for t in range(2)]

    def ffn(tag):
        return ([("zt", tag, c) for c in range(NC)] + [("up", tag, m) for m in range(NF)]
                + [("dn", tag, t) for t in range(2)])

    o += ffn("F")
    o += [("zt", "B", c) for c in range(NC)]
    o += [("q", 0), ("kk", 0)]
    for t in range(NG):
        if t + 1 < NG:
            o += [("q", t + 1), ("kk", t + 1)]
        o += [("qf", t), ("kf", t)]
    o += [("vb", t) for t in range(2)]
    o += [("S", 0, g, i) for g in range(HG) for i in range(3)]
    for t in range(NG):
        o += [("mt", t)]
        for g in range(HG):
            if t + 1 < NG:
                o += [("S", t + 1, g, i) for i in range(3)]
            o += [("ST", t, g, i) for i in range(3)]
    o += [("aot", c) for c in range(NC)] + [("wo", t) for t in range(2)]
    o += ffn("M")
    o += ffn("G")
    return o


def hybrid_kernel(nc, io, out):
    order = psum_order()
    bank_of, use_of, uses = {}, {}, [0] * RING
    for n, key in enumerate(order):
        bank_of[key] = n % RING
        use_of[key] = uses[n % RING]
        uses[n % RING] += 1

    with ExitStack() as ctx:
        def sb(name, shape, dt=F32):
            return ctx.enter_context(nc.sbuf_tensor(name, shape, dt))

        class Sem:

            def __init__(self, name, per):
                self.h = ctx.enter_context(nc.semaphore(name))
                self.name, self.per, self.made = name, per, 0

        sems = []

        def sem(name, per=0):
            s = Sem(name, per)
            sems.append(s)
            return s

        def one(s):
            s.made += 1
            return s.h, 1

        w1 = sb("w_mix1", [P, NC, NMIX * RMIX])
        w2a = sb("w_mix2a", [P, D])
        w2b = sb("w_mix2b", [RMIX, D])
        wr = sb("w_r", [P, NC, H * DK])
        wk = sb("w_k", [P, NC, H * DK])
        wv = sb("w_v", [P, NC, H * DV])
        wwa = sb("w_decay_a", [P, NC, LR])
        wwb = sb("w_decay_b", [LR, H * DK])
        wga = sb("w_gate_a", [P, NC, LR])
        wgb = sb("w_gate_b", [LR + 1, D])
        wo = sb("w_mixer_out", [P, NC, D])
        wup = sb("w_up", [P, NC, FF])
        wdn = sb("w_down", [P, NF, D])
        wq_b = sb("w_q", [P, NC, NG * P])
        wk_b = sb("w_kk", [P, NC, NG * P])
        wv_b = sb("w_vv", [P, NC, D])
        wo_b = sb("w_attn_out", [P, NC, D])
        wm1 = sb("w_mlp1", [P, NC, FF])
        wm2 = sb("w_mlp2", [P, NF, D])
        cols = sb("cols", [P, NCOLS])
        upb = sb("up_bias", [P, NF])
        bias_f = sb("bias_ffn", [P, D])
        bias_o = sb("bias_attn_out", [P, D])
        bias_m = sb("bias_mlp", [P, D])
        bias_v = sb("bias_v", [P, D])
        ident = sb("ident", [P, P])
        masks = sb("masks", [P, 3 + len(LEVELS), P], BF16)
        identb = masks[:, 0, :]
        future = masks[:, 1, :]
        future_t = masks[:, 2, :]
        lmask = masks[:, 3:, :]
        fold = sb("fold", [P, P])
        rope = sb("rope", [P, T])

        x = sb("x", [P, NT, D])
        z = sb("z", [P, NT, D])
        xb = sb("x_plus_bias", [P, NT, D])
        x2 = sb("x_block", [P, NT, D])
        zt = sb("z_t", [P, NC, T + 1])
        delta = sb("delta", [P, NC, T])
        mix = sb("mix", [P, 3, NC, T])
        xl0 = sb("xl0", [P, T])
        xl1 = sb("xl1", [RMIX, T])
        stats = sb("stats", [P, NT, 6])
        mv = sb("mean_var", [P, NT, 2])
        rstd = sb("rstd", [P, 3, NT])
        power = sb("eps_and_power", [P, 2, NT])
        big = sb("big", [P, 16, T])
        dec = sb("decay", [P, H, T])
        dtree = sb("decay_blocks", [P, H, T])
        wat = sb("wa_t", [LR, T])
        gat = sb("ga_t", [LR + 1, T])
        v = sb("v", [P, NT, H * DV])
        scores = sb("scores_t", [P, H, NT, P])
        state = sb("state", [P, NT - 1, H, DV])
        gate = sb("gate", [P, NC, T])
        rqk = sb("qk_rounded", [P, 2, 2, T], F32R)
        vaug = sb("v_ones", [P, NT, NH, HD + 1])
        maxes = sb("maxes", [P, 2, NT, P])
        rden = sb("rden", [P, NT, HG])

        qf, qu, kg = big[:, 0:4], big[:, 4:8], big[:, 8:12]
        kt = big[:, 12:16].rearrange("p h (c k) -> p h c k", c=NT)
        gelu = big[:, 0:8]
        qp, kp = big[:, 0:4], big[:, 4:8]
        NPT = 3
        pt = big[:, 8:16].rearrange("p a t -> p (a t)")[:, 0:NPT * 1280].rearrange("p (r n) -> p r n", r=NPT)
        on = mix[:, 0].rearrange("p c t -> p (c t)").rearrange("p (t d) -> p t d", t=NT)
        ogate = mix[:, 1]
        gtanh = mix[:, 2]
        qh = mix[:, 1:3].rearrange("p a c t -> p (a c) t")
        attn = mix[:, 0].rearrange("p c t -> p (c t)").rearrange("p (t d) -> p t d", t=NT)
        attn_t = delta[:, :, :]
        z2 = on

        dblk, at = {0: dec[:, :, :]}, 0
        for lv in range(1, 8):
            n = T >> lv
            dblk[lv] = dtree[:, :, at:at + n]
            at += n

        ring = [ctx.enter_context(nc.psum_tensor(f"ring{i}", [P, T], F32)) for i in range(RING)]
        obank = [ctx.enter_context(nc.psum_tensor(f"attn_out{i}", [P, T], F32)) for i in range(2)]

        wload = sem("weights_loaded")
        full = [sem(f"bank_full{i}", uses[i]) for i in range(RING)]
        x_in = sem("x_loaded", 16)
        x_out = sem("x_stored", 16)
        x_ready = sem("x_ready", 2 * 4)
        x2_ready = sem("x2_ready", 2)
        lns = sem("ln_steps", 5 * 2 * NT)
        lnb = sem("ln_block_steps", 2)
        rs_step = sem("rstd_step", 7)
        rs_ready = sem("rstd_ready", 7)
        z_ready = sem("z_ready", 5 * NT)
        z2_ready = sem("z2_ready", NT)
        zt_ready = sem("zt_ready", 5 * NC)
        delta_ready = sem("delta_ready", NC)
        mix0_ready = sem("mix0_ready", NC)
        xl_ready = sem("xl_ready", 2)
        mixd_ready = sem("mix_delta_ready", NMIX * NC)
        mix_ready = sem("mix_ready", NMIX * NC)
        wa_ready = sem("wa_ready", 1)
        ga_ready = sem("ga_ready", 1)
        ew_ready = sem("exp_w_ready", H)
        dec_ready = sem("decay_ready", H)
        tree_ready = sem("tree_ready", 7)
        kg_ready = sem("k_ready", H)
        qf_ready = sem("q_ready", H)
        qu_ready = sem("q_bonus_ready", H)
        kg_level = sem("k_level", 7 * H)
        qf_level = sem("q_level", 7 * H)
        v_ready = sem("v_ready", 2)
        gt_ready = sem("gate_tanh", NC)
        gate_ready = sem("gate_ready", NC)
        a_copied = sem("scores_copied", len(LEVELS) * H)
        gating = sem("dve_gate", 0)
        pool_gate = sem("pool_gate", 0)
        sp_gate = sem("sp_gate", 0)
        kt_ready = sem("k_rows_ready", H)
        state_ready = sem("state_ready", NT - 1)
        gstat = sem("gn_steps", 2 * NT)
        on_ready = sem("o_normed", NT)
        oaff_ready = sem("o_affine", NC)
        og_ready = sem("o_gated", NC)
        xb_ready = sem("xb_ready", 4)
        xs_step = sem("xs_step", 1)
        gelu_ready = sem("gelu_ready", 3 * NF)
        qh_ready = sem("qh_ready", 2 * NG)
        qp_ready = sem("qp_ready", 2 * NG)
        rqk_ready = sem("rounded_ready", 2 * NG)
        vaug_ready = sem("vaug_ready", 2)
        maxs = sem("max_steps", NG * HG * 4)
        qm_ready = sem("q_shifted", NG)
        pt_ready = sem("p_ready", NH * 3)
        pt_used = sem("p_used", NH)
        rden_ready = sem("rden_ready", NG)
        attn_ready = sem("attn_ready", NG)
        at_ready = sem("attn_t_ready", NC)
        def copied(key):
            kind, a = key[0], key[1:]
            if kind in ("zt", "dn"):
                layer = "AFBMG".index(a[0])
                return (zt_ready, layer * NC + a[1] + 1) if kind == "zt" else \
                    (x_ready, {1: 2, 3: 4, 4: 6}[layer] + a[1] + 1)
            return {
                "xl": lambda i: (xl_ready, i + 1),
                "x5": lambda n, c: (mixd_ready, MIX_ORDER.index(n) * NC + c + 1),
                "wa": lambda: (wa_ready, 1),
                "w": lambda h: (ew_ready, h + 1),
                "k": lambda h: (kg_ready, h + 1),
                "r": lambda h: (qf_ready, h + 1),
                "v": lambda t: (v_ready, t + 1),
                "ga": lambda: (ga_ready, 1),
                "g": lambda c: (gate_ready, c + 1),
                "A": lambda lv, h: (a_copied, lv * H + h + 1),
                "kt": lambda h: (kt_ready, h + 1),
                "s": lambda c: (state_ready, c + 1),
                "o": lambda t: (on_ready, 2 * t + 2),
                "ogt": lambda c: (oaff_ready, c + 1),
                "ao": lambda t: (x_ready, t + 1),
                "up": lambda tag, m: (gelu_ready, "FMG".index(tag) * NF + m + 1),
                "q": lambda t: (qh_ready, 2 * t + 1),
                "kk": lambda t: (qh_ready, 2 * t + 2),
                "qf": lambda t: (qp_ready, 2 * t + 1),
                "kf": lambda t: (qp_ready, 2 * t + 2),
                "vb": lambda t: (vaug_ready, t + 1),
                "S": lambda t, g, b: (maxs, (t * HG + g) * 4 + (1, 3, 4)[b]),
                "mt": lambda t: (qm_ready, t + 1),
                "ST": lambda t, g, i: (pt_ready, (t * HG + g) * 3 + i + 1),
                "aot": lambda c: (at_ready, c + 1),
                "wo": lambda t: (x2_ready, t + 1),
            }[kind](*a)

        consts = sem("constants_set")
        bl_in = sem("butterfly_tile_in")
        bl_cols = sem("butterfly_cols")
        bl_diag = sem("butterfly_diag")
        bl_mat = sem("butterfly_matrix")
        bl_mm = [sem("butterfly_mm_up"), sem("butterfly_mm_down")]
        bl_ev = [sem("butterfly_evac_up"), sem("butterfly_evac_down")]
        bh_t = sem("butterfly_high_same")
        bh_s = sem("butterfly_high")
        bt_mm = sem("w_up_turned")
        bt_ev = sem("w_up_copied")
        pre = sem("biases_ready")
        seeded = sem("seeded")

        flat = big[:, :, :].rearrange("p a t -> p (a t)")
        UW = D + 1
        y_up = flat[:, 0:NF * UW].rearrange("p (t n) -> p t n", t=NF)
        y_up2 = flat[:, NF * UW:2 * NF * UW].rearrange("p (t n) -> p t n", t=NF)
        dflat = mix[:, :, :, :].rearrange("p a c t -> p (a c t)")
        y_dn = flat[:, 2 * NF * UW:2 * NF * UW + NF * D].rearrange("p (t n) -> p t n", t=NF)
        masks_in = flat[:, 2 * NF * UW + NF * D:2 * NF * UW + NF * D + (3 + len(LEVELS)) * P]
        bw = dflat[:, 0:3 * 2 * NF * STAGES].rearrange("p (k w t s) -> p k w t s", k=3, w=2, t=NF)
        perm = dflat[:, 512:512 + LOW * P].rearrange("p (s n) -> p s n", s=LOW)
        bcol = dflat[:, 1408:1408 + 6 * STAGES].rearrange("p (k w s) -> p k w s", k=3, w=2)
        diag = dflat[:, 1536:1536 + 4 * P].rearrange("p (r n) -> p r n", r=4)
        bmat = dflat[:, 2048:2048 + 4 * P].rearrange("p (r n) -> p r n", r=4)
        ystep = v[:, :, :].rearrange("p a b -> p (a b)")[:, 0:4 * D].rearrange("p (r n) -> p r n", r=4)
        y_st = [sb("y_step_up", [P, 2, UW]), ystep[:, 0:2, :]]
        tmp_h = sb("tmp_high", [P, UW])
        bdn = scores[:, :, :, :].rearrange("p h c n -> p (h c n)")[:, 0:NF * D].rearrange("p (t n) -> p t n", t=NF)

        def col(name, i=0):
            return cols[:, COLS[name] + i:COLS[name] + i + 1]

        block = ctx.enter_context(nc.Block())
        dflt = io

        small_loads = [
            (cols[:, :], dflt["cols"]), (ident[:, :], dflt["ident"]), (perm, dflt["perm"]),
            (masks_in, dflt["masks"].rearrange("p s n -> p (s n)")), (bw, dflt["bw"]), (y_dn, dflt["w_con"].rearrange("(t p) n -> p t n", p=P)),
        ]

        def chunked(a):
            return a.rearrange("(c p) n -> p c n", p=P)

        loads = [
            (w1[:, :, :], chunked(dflt["w1"])), (w2a[:, :], dflt["w2"][0:P, :]),
            (w2b[:, :], dflt["w2"][P:P + RMIX, :]), (wr[:, :, :], chunked(dflt["wr"])),
            (wk[:, :, :], chunked(dflt["wk"])), (wv[:, :, :], chunked(dflt["wv"])),
            (wwa[:, :, :], chunked(dflt["wwa"])), (wwb[:, :], dflt["wwb"]),
            (wga[:, :, :], chunked(dflt["wga"])), (wgb[:, :], dflt["wgb"]),
            (wo[:, :, :], chunked(dflt["wo"])), (wq_b[:, :, :], chunked(dflt["wq_b"])),
            (wk_b[:, :, :], chunked(dflt["wk_b"])), (wv_b[:, :, :], chunked(dflt["wv_b"])),
            (wo_b[:, :, :], chunked(dflt["wo_b"])), (wm1[:, :, :], chunked(dflt["wm1"])),
            (wm2[:, :, :], chunked(dflt["wm2"])), (fold[:, :], dflt["fold"]), (rope[:, :], dflt["rope"]),
        ]
        for tile, name in ((bias_f, "b_con"), (xb[:, 0, :], "down_b"), (bias_o, "bo"), (bias_m, "b2"),
                           (bias_v, "bv")):
            dst = tile[:, :] if name != "down_b" else tile
            loads.append((dst, dflt[name].rearrange("(a n) -> a n", a=1).to_broadcast([P, D])))
        N_SMALL, N_LOADS = len(small_loads), len(loads)
        w_up_dram = dflt["w_exp_t"].rearrange("(t p) n -> t p n", p=P)
        x_dram = dflt["x"].rearrange("b (t p) d -> b p t d", p=P)
        out_dram = out.rearrange("b (t p) d -> b p t d", p=P)

        @block.sync
        def _(sp):
            for dst, src in small_loads:
                sp.dma_start(dst, src).then_inc(wload.h, 16)
            with sp.Fori(0, NF) as t:
                sp.wait_ge(bl_ev[0].h, t * LOW + 1)
                sp.dma_start(y_st[0][:, 0, :], w_up_dram[t]).then_inc(bl_in.h, 16)
            with sp.Fori(0, B) as it:
                sp.dma_start(x[:, :, :], x_dram[it]).then_inc(x_in.h, 16)
                sp.wait_ge(x_ready.h, it * x_ready.per + 8)
                sp.dma_start(out_dram[it], x[:, :, :]).then_inc(x_out.h, 16)
                sp.wait_ge(x_out.h, it * 16 + 16)
                sp.sem_inc(sp_gate.h, 1)

        @block.gpsimd
        def _(pool):
            for n, (dst, src) in enumerate(loads):
                pool.dma_start(dst, src).then_inc(pre.h, 16)
            nc.gpsimd.memset(zt[:, :, :], 0.0).then_inc(*one(consts))
            nc.gpsimd.memset(scores[:, :, :, :], 0.0).then_inc(*one(consts))
            nc.gpsimd.memset(maxes[:, :, :, :], 0.0).then_inc(*one(consts))
            nc.gpsimd.memset(vaug[:, :, :, :], 1.0).then_inc(*one(consts))
            nc.gpsimd.memset(gat[:, :], 1.0).then_inc(*one(consts))
            nc.gpsimd.memset(power[:, 0, :], EPS).then_inc(*one(consts))
            nc.gpsimd.memset(power[:, 1, :], -0.5).then_inc(*one(consts))
            pool.wait_ge(pre.h, 16 * N_LOADS)
            nc.gpsimd.tensor_tensor(bias_f[:, :], bias_f[:, :], xb[:, 0, :], ALU.add).then_inc(*one(consts))
            pool.wait_ge(consts.h, 8)
            pool.wait_ge(bt_ev.h, NC * NF)
            with pool.Fori(0, B) as it:
                def after(s, k):
                    return s.h, it * s.per + k

                def bank_full(key):
                    return after(full[bank_of[key]], use_of[key] + 1)

                def rsqrt(ready, var, dst):
                    pool.wait_ge(*ready)
                    nc.gpsimd.tensor_tensor(rstd[:, dst, :], var, power[:, 0, :], ALU.add).then_inc(*one(rs_step))
                    pool.wait_ge(*after(rs_step, rs_step.made))
                    nc.gpsimd.tensor_tensor(rstd[:, dst, :], rstd[:, dst, :], power[:, 1, :], ALU.pow) \
                        .then_inc(*one(rs_ready))

                rsqrt(after(lns, 2 * NT), mv[:, :, 1], 0)
                for c in range(NC):
                    pool.wait_ge(*after(zt_ready, c + 1))
                    nc.gpsimd.tensor_tensor(delta[:, c, :], zt[:, c, 0:T], zt[:, c, 1:T + 1],
                                            ALU.subtract).then_inc(*one(delta_ready))
                for a, n in enumerate(MIX_ORDER):
                    for c in range(NC):
                        pool.wait_ge(*after(mixd_ready, a * NC + c + 1))
                        nc.gpsimd.tensor_tensor(mix[:, a % 3, c, :], mix[:, a % 3, c, :], zt[:, c, 1:T + 1],
                                                ALU.add).then_inc(*one(mix_ready))
                    if n == 1:
                        for lv in range(1, 8):
                            if lv == 1:
                                pool.wait_ge(*after(dec_ready, H))
                            else:
                                pool.wait_ge(*after(tree_ready, lv - 1))
                            pairs = dblk[lv - 1].rearrange("p h (m two) -> p h m two", two=2)
                            nc.gpsimd.tensor_tensor(dblk[lv], pairs[:, :, :, 0], pairs[:, :, :, 1],
                                                    ALU.mult).then_inc(*one(tree_ready))
                for h in range(H):
                    pool.wait_ge(*after(qf_ready, h + 1))
                    pool.sem_inc(pool_gate.h, 1)
                    nc.gpsimd.tensor_scalar(qu[:, h, :], qf[:, h, :], col("bonus", h), None,
                                            ALU.mult).then_inc(*one(qu_ready))
                pool.wait_ge(*after(tree_ready, 7))
                for lv in range(1, 8):
                    s = LEVELS[lv]
                    for h in range(H):
                        pool.wait_ge(*bank_full(("A", lv, h)))
                        if lv > 1:
                            pool.wait_ge(*after(kg_level, (lv - 2) * H + h + 1))
                        kv = kg[:, h, :].rearrange("p (m two s) -> p m two s", two=2, s=s)[:, :, 0, :]
                        dv = dblk[lv - 1][:, h, :].rearrange("p (m two) -> p m two", two=2)[:, :, 1]
                        nc.gpsimd.tensor_tensor(kv, kv, dv.unsqueeze(2).to_broadcast([P, T // (2 * s), s]),
                                                ALU.mult).then_inc(*one(kg_level))
                rsqrt(after(gstat, 2 * NT), mv[:, :, 1], 0)
                for c in range(NC):
                    pool.wait_ge(*after(oaff_ready, c + 1))
                    pool.wait_ge(*after(gate_ready, c + 1))
                    nc.gpsimd.tensor_tensor(ogate[:, c, :], ogate[:, c, :], gate[:, c, :],
                                            ALU.mult).then_inc(*one(og_ready))

                def plus(out_, a_, bias):
                    return nc.gpsimd.tensor_tensor(out_, a_, bias[:, :].unsqueeze(1).to_broadcast([P, NT, D]),
                                                   ALU.add)

                pool.wait_ge(*after(x_ready, 2))
                rsqrt(after(lns, 4 * NT), mv[:, :, 1], 0)
                plus(xb[:, :, :], x[:, :, :], bias_f).then_inc(*one(xb_ready))
                rsqrt(after(lns, 6 * NT), mv[:, :, 1], 0)
                rsqrt(after(lnb, 2), rstd[:, 1, :], 2)
                pool.wait_ge(*after(z_ready, 3 * NT))
                pool.wait_ge(*after(x_ready, 4))
                plus(xb[:, :, :], z[:, :, :], bias_o).then_inc(*one(xb_ready))
                for t in range(NG):
                    for i, src in enumerate((qp, kp)):
                        pool.wait_ge(*after(qp_ready, 2 * t + i + 1))
                        if t >= 2:
                            pool.wait_ge(*bank_full(("S", t - 2, HG - 1, 2)))
                        pool.sem_inc(pool_gate.h, 1)
                        nc.gpsimd.tensor_copy(rqk[:, t % 2, i, :], src[:, t, :]).then_inc(*one(rqk_ready))
                pool.wait_ge(*after(x2_ready, 2))
                rsqrt(after(lns, 8 * NT), mv[:, :, 1], 0)
                nc.gpsimd.tensor_tensor(xb[:, :, :], x[:, :, :], x2[:, :, :], ALU.add).then_inc(*one(xs_step))
                pool.wait_ge(*after(xs_step, 1))
                plus(xb[:, :, :], xb[:, :, :], bias_m).then_inc(*one(xb_ready))
                pool.wait_ge(*after(x_ready, 6))
                rsqrt(after(lns, 10 * NT), mv[:, :, 1], 0)
                plus(xb[:, :, :], x[:, :, :], bias_f).then_inc(*one(xb_ready))

        @block.scalar
        def _(act):
            with act.Fori(0, NF) as t:
                act.wait_ge(bl_cols.h, t + 1)
                for s in range(LOW):
                    n = t * (2 * LOW) + 2 * s
                    act.wait_ge(bl_mat.h, n + 1)
                    nc.scalar.activation(diag[:, (2 * s) % 4, :], ident[:, :], ACT.Copy,
                                         scale=bcol[:, 0, 0, s:s + 1]).then_inc(bl_diag.h, 1)
                    act.wait_ge(bl_mat.h, n + 2)
                    nc.scalar.activation(diag[:, (2 * s + 1) % 4, :], ident[:, :], ACT.Copy,
                                         scale=bcol[:, 0, 1, LOW - 1 - s:LOW - s]).then_inc(bl_diag.h, 1)
                    act.wait_ge(bl_mm[0].h, t * LOW + s + 1)
                    if s < LOW - 1:
                        nc.scalar.activation(y_st[0][:, (s + 1) % 2, :], ring[s % 2][:, 0:UW],
                                             ACT.Copy).then_inc(bl_ev[0].h, 1)
                    else:
                        nc.scalar.activation(y_up[:, bass.ds(t, 1), :], ring[s % 2][:, 0:UW].unsqueeze(1),
                                             ACT.Copy).then_inc(bl_ev[0].h, 1)
            for m in range(NF):
                for c in range(NC):
                    n = m * NC + c
                    act.wait_ge(bt_mm.h, n + 1)
                    nc.scalar.activation(wup[:, c, m * P:(m + 1) * P], ring[n % 4][:, 0:P],
                                         ACT.Copy).then_inc(*one(bt_ev))
            act.wait_ge(pre.h, 16 * N_LOADS)
            with act.Fori(0, B) as it:
                def after(s, k):
                    return s.h, it * s.per + k

                def bank_full(key):
                    return after(full[bank_of[key]], use_of[key] + 1)

                def bank(key):
                    return ring[bank_of[key]]

                def turned(tag, scale=None, bias=None):
                    for c in range(NC):
                        act.wait_ge(*bank_full(("zt", tag, c)))
                        if scale is None:
                            ins = nc.scalar.activation(zt[:, c, 1:T + 1], bank(("zt", tag, c))[:, :], ACT.Copy)
                        else:
                            ins = nc.scalar.activation(zt[:, c, 1:T + 1], bank(("zt", tag, c))[:, :],
                                                       ACT.Identity, scale=col(scale, c), bias=col(bias, c))
                        ins.then_inc(*one(zt_ready))

                def evac(key, dst, done, func=ACT.Copy, rows=P, **kw):
                    act.wait_ge(*bank_full(key))
                    nc.scalar.activation(dst, bank(key)[0:rows, :], func, **kw).then_inc(*one(done))

                turned("A")
                evac(("xl", 0), xl0[:, :], xl_ready, ACT.Tanh)
                evac(("xl", 1), xl1[:, :], xl_ready, ACT.Tanh, rows=RMIX)
                evac(("wa",), wat[:, :], wa_ready, ACT.Tanh, rows=LR)
                for h in range(H):
                    evac(("w", h), dec[:, h, :], ew_ready, ACT.Exp, bias=col("w_b", h))
                    act.wait_ge(*after(ew_ready, h + 1))
                    nc.scalar.activation(dec[:, h, :], dec[:, h, :], ACT.Exp, scale=-1.0).then_inc(*one(dec_ready))
                for h in range(H):
                    evac(("k", h), kg[:, h, :], kg_ready)
                for h in range(H):
                    evac(("r", h), qf[:, h, :], qf_ready)
                for t in range(2):
                    evac(("v", t), v[:, 2 * t:2 * t + 2, :].rearrange("p a b -> p (a b)"), v_ready)
                evac(("ga",), gat[0:LR, :], ga_ready, ACT.Tanh, rows=LR)
                for c in range(NC):
                    act.wait_ge(*bank_full(("g", c)))
                    nc.scalar.activation(gtanh[:, c, :], bank(("g", c))[:, :], ACT.Tanh,
                                         scale=0.5).then_inc(*one(gt_ready))
                for h in range(H):
                    act.wait_ge(*bank_full(("kt", h)))
                    nc.scalar.activation(kt[:, h, 0:NT - 1, :],
                                         bank(("kt", h))[:, 0:(NT - 1) * P].rearrange("p (c k) -> p c k", k=P),
                                         ACT.Copy).then_inc(*one(kt_ready))
                for c in range(NC):
                    evac(("ogt", c), ogate[:, c, :], oaff_ready, ACT.Identity, scale=col("gn_w", c),
                         bias=col("gn_b", c))

                def gelus(tag, bias):
                    for m in range(NF):
                        evac(("up", tag, m), gelu[:, m, :], gelu_ready, ACT.Gelu, bias=bias(m))

                turned("F")
                gelus("F", lambda m: upb[:, m:m + 1])
                for t in range(NT):
                    act.wait_ge(*after(z_ready, 2 * NT + t + 1))
                    act.wait_ge(*after(rs_ready, 5))
                    if t == 0:
                        act.wait_ge(*after(og_ready, NC))
                    nc.scalar.activation(z2[:, t, :], z[:, t, :], ACT.Copy,
                                         scale=rstd[:, 2, t:t + 1]).then_inc(*one(z2_ready))
                turned("B", "ln1_g", "ln1_b")
                for t in range(NG):
                    evac(("qf", t), qp[:, t, :], qp_ready)
                    evac(("kf", t), kp[:, t, :], qp_ready, ACT.Identity, bias=col("minus_row"))
                for t in range(NG):
                    for g in range(HG):
                        n = t * HG + g
                        if n >= NPT:
                            act.wait_ge(*after(pt_used, n - NPT + 1))
                        for i, (lo, hi) in enumerate(((0, 512), (512, 1024), (1024, 1280))):
                            key = ("ST", t, g, i)
                            act.wait_ge(*bank_full(key))
                            nc.scalar.activation(pt[:, n % NPT, lo:hi], bank(key)[:, 0:hi - lo], ACT.Exp,
                                                 scale=HD ** -0.5).then_inc(*one(pt_ready))
                for c in range(NC):
                    evac(("aot", c), attn_t[:, c, :], at_ready)
                turned("M", "ln2_g", "ln2_b")
                gelus("M", lambda m: col("b1", m))
                turned("G")
                gelus("G", lambda m: upb[:, m:m + 1])

        @block.vector
        def _(dve):
            for i in range(3):
                dve.sem_inc(bl_mat.h, 1)
            dve.wait_ge(wload.h, 16 * N_SMALL)
            nc.vector.tensor_copy(masks[:, :, :].rearrange("p s n -> p (s n)"), masks_in).then_inc(*one(seeded))
            high = [0]

            def high_stage(src, dst, width, which, kind, s):
                m = 1 << (s - LOW)
                for t in range(NF):
                    if high[0] >= 1:
                        dve.wait_ge(bh_s.h, high[0])
                    high[0] += 1
                    nc.vector.tensor_scalar(tmp_h[:, 0:width], src[:, t, 0:width], bw[:, 0, which, t, s:s + 1], None,
                                            ALU.mult).then_inc(bh_t.h, 1)
                    dve.wait_ge(bh_t.h, high[0])
                    nc.vector.scalar_tensor_tensor(out=dst[:, t, 0:width], in0=src[:, t ^ m, 0:width],
                                                   scalar=bw[:, kind, which, t, s:s + 1], in1=tmp_h[:, 0:width],
                                                   op0=ALU.mult, op1=ALU.add).then_inc(bh_s.h, 1)

            dn_tmp = y_up
            dn_cur = y_dn
            for s in range(STAGES - 1, LOW - 1, -1):
                nxt = {STAGES - 1: dn_tmp, STAGES - 2: y_dn, LOW: bdn}[s]
                if s == LOW:
                    dve.wait_ge(consts.h, 2)
                high_stage(dn_cur, nxt, D, 1, 2, s)
                dn_cur = nxt
            dve.wait_ge(bh_s.h, high[0])
            HDN = high[0]
            dve.sem_inc(bl_ev[0].h, 1)
            with dve.Fori(0, NF) as t:
                nc.vector.tensor_copy(bcol.rearrange("p k w s -> p (k w) s"),
                                      bw.rearrange("p k w t s -> p (k w) t s")[:, :, bass.ds(t, 1), :]
                                      .rearrange("p k t s -> p k (t s)")).then_inc(bl_cols.h, 1)
                dve.wait_ge(bl_cols.h, t + 1)
                for s in range(LOW):
                    for w in range(2):
                        n = 2 * s + w
                        st = s if w == 0 else LOW - 1 - s
                        dve.wait_ge(bl_diag.h, t * 2 * LOW + n + 1)
                        if w == 0:
                            if s >= 2:
                                dve.wait_ge(bl_mm[0].h, t * LOW + s - 1)
                        nc.vector.scalar_tensor_tensor(out=bmat[:, n % 4, :], in0=perm[:, st, :],
                                                       scalar=bcol[:, 2 if w == 0 else 1, w, st:st + 1],
                                                       in1=diag[:, n % 4, :], op0=ALU.mult,
                                                       op1=ALU.add).then_inc(bl_mat.h, 1)
                    dve.wait_ge(bl_mm[1].h, t * LOW + s + 1)
                    if s < LOW - 1:
                        nc.vector.tensor_copy(y_st[1][:, (s + 1) % 2, :],
                                              ring[2 + s % 2][:, 0:D]).then_inc(bl_ev[1].h, 1)
                    else:
                        nc.vector.tensor_copy(wdn[:, bass.ds(t, 1), :],
                                              ring[2 + s % 2][:, 0:D].unsqueeze(1)).then_inc(bl_ev[1].h, 1)
            dve.wait_ge(bl_ev[0].h, NF * LOW + 1)
            high_stage(y_up, y_up2, UW, 0, 1, LOW)
            high_stage(y_up2, y_up, UW, 0, 1, LOW + 1)
            high_stage(y_up, y_up2, UW, 0, 1, LOW + 2)
            dve.wait_ge(bh_s.h, high[0])
            for m in range(NF):
                ins = nc.vector.tensor_tensor(upb[:, m:m + 1], y_up2[:, m, D:UW], col("up_b", m), ALU.add)
            ins.then_inc(*one(seeded))
            dve.wait_ge(bt_ev.h, NC * NF)
            dve.wait_ge(consts.h, 8)
            dve.wait_ge(pre.h, 16 * N_LOADS)

            with dve.Fori(0, B) as it:
                def after(s, k):
                    return s.h, it * s.per + k

                def bank_full(key):
                    return after(full[bank_of[key]], use_of[key] + 1)

                def bank(key):
                    return ring[bank_of[key]]

                nln = [0]

                def layer_norm(src, ready, block=False):
                    base = nln[0] * 2 * NT
                    for t in range(NT):
                        dve.wait_ge(*ready(t))
                        nc.vector.bn_stats(stats[:, t, :], src[:, t, :]).then_inc(*one(lns))
                    dve.wait_ge(*after(lns, base + NT))
                    dve.sem_inc(gating.h, 1)
                    for t in range(NT):
                        nc.vector.bn_aggr(mv[:, t, :], stats[:, t, :]).then_inc(*one(lns))
                    dve.wait_ge(*after(rs_ready, (1, 3, 4, 6, 7)[nln[0]]))
                    for t in range(NT):
                        nc.vector.tensor_scalar(z[:, t, :], src[:, t, :], mv[:, t, 0:1], rstd[:, 0, t:t + 1],
                                                ALU.subtract, ALU.mult).then_inc(*one(z_ready))
                    if block:
                        nc.vector.tensor_tensor(rstd[:, 1, :], rstd[:, 0, :], rstd[:, 0, :],
                                                ALU.mult).then_inc(*one(lnb))
                        dve.wait_ge(*after(lnb, 1))
                        nc.vector.tensor_tensor(rstd[:, 1, :], rstd[:, 1, :], mv[:, :, 1],
                                                ALU.mult).then_inc(*one(lnb))
                    nln[0] += 1

                def add_back(keys, res, dst, done):
                    for t, key in enumerate(keys):
                        dve.wait_ge(*bank_full(key))
                        nc.vector.tensor_tensor(dst[:, 2 * t:2 * t + 2, :].rearrange("p a b -> p (a b)"),
                                                bank(key)[:, :],
                                                res[:, 2 * t:2 * t + 2, :].rearrange("p a b -> p (a b)"),
                                                ALU.add).then_inc(*one(done))

                layer_norm(x, lambda t: after(x_in, 16))
                for c in range(NC):
                    dve.wait_ge(*after(delta_ready, c + 1))
                    nc.vector.scalar_tensor_tensor(out=mix[:, 2, c, :], in0=delta[:, c, :], scalar=col("mu", c),
                                                   in1=zt[:, c, 1:T + 1], op0=ALU.mult,
                                                   op1=ALU.add).then_inc(*one(mix0_ready))
                for a, n in enumerate(MIX_ORDER):
                    for c in range(NC):
                        key = ("x5", n, c)
                        dve.wait_ge(*bank_full(key))
                        if a == 3:
                            dve.wait_ge(*bank_full(("w", 0)))
                        if a == 4:
                            dve.wait_ge(*bank_full(("k", H - 1)))
                        nc.vector.scalar_tensor_tensor(out=mix[:, a % 3, c, :], in0=bank(key)[:, :],
                                                       scalar=col("xbias", n * NC + c), in1=delta[:, c, :],
                                                       op0=ALU.add, op1=ALU.mult).then_inc(*one(mixd_ready))
                for c in range(NC):
                    dve.wait_ge(*after(gt_ready, c + 1))
                    nc.vector.scalar_tensor_tensor(out=gate[:, c, :], in0=gtanh[:, c, :], scalar=1.0,
                                                   in1=bank(("g", c))[:, :], op0=ALU.add,
                                                   op1=ALU.mult).then_inc(*one(gate_ready))
                dve.wait_ge(*after(tree_ready, 7))
                for lv, s in enumerate(LEVELS):
                    for h in range(H):
                        key = ("A", lv, h)
                        dve.wait_ge(*bank_full(key))
                        if lv >= 1:
                            dve.wait_ge(*after(a_copied, (lv - 1) * H + h + 1))
                        dve.sem_inc(gating.h, 1)
                        nc.vector.copy_predicated(scores[:, h, :, :],
                                                  lmask[:, lv, :].bitcast(U16).unsqueeze(1).to_broadcast([P, NT, P]),
                                                  bank(key)[:, :].rearrange("p (c n) -> p c n", c=NT)) \
                            .then_inc(*one(a_copied))
                        if lv >= 1:
                            if lv > 1:
                                dve.wait_ge(*after(qf_level, (lv - 2) * H + h + 1))
                            qv = qf[:, h, :].rearrange("p (m two s) -> p m two s", two=2, s=s)[:, :, 1, :]
                            dv = dblk[lv - 1][:, h, :].rearrange("p (m two) -> p m two", two=2)[:, :, 0]
                            nc.vector.tensor_tensor(qv, qv, dv.unsqueeze(2).to_broadcast([P, T // (2 * s), s]),
                                                    ALU.mult).then_inc(*one(qf_level))
                for c in range(NT - 1):
                    key = ("s", c)
                    dve.wait_ge(*bank_full(key))
                    if c == 0:
                        nc.vector.tensor_copy(state[:, 0, :, :].rearrange("p h v -> p (h v)"),
                                              bank(key)[:, 0:H * DV]).then_inc(*one(state_ready))
                    else:
                        dve.wait_ge(*after(state_ready, c))
                        for h in range(H):
                            ins = nc.vector.scalar_tensor_tensor(
                                out=state[:, c, h, :], in0=state[:, c - 1, h, :], scalar=dblk[7][:, h, c:c + 1],
                                in1=bank(key)[:, h * DV:(h + 1) * DV], op0=ALU.mult, op1=ALU.add)
                        ins.then_inc(*one(state_ready))
                for t in range(NT):
                    dve.wait_ge(*bank_full(("o", t // 2)))
                    nc.vector.bn_stats(stats[:, t, :], bank(("o", t // 2))[:, (t % 2) * D:(t % 2 + 1) * D]) \
                        .then_inc(*one(gstat))
                dve.wait_ge(*after(gstat, NT))
                dve.sem_inc(gating.h, 1)
                for t in range(NT):
                    nc.vector.bn_aggr(mv[:, t, :], stats[:, t, :]).then_inc(*one(gstat))
                dve.wait_ge(*after(rs_ready, 2))
                for t in range(NT):
                    nc.vector.tensor_scalar(on[:, t, :], bank(("o", t // 2))[:, (t % 2) * D:(t % 2 + 1) * D],
                                            mv[:, t, 0:1], rstd[:, 0, t:t + 1], ALU.subtract,
                                            ALU.mult).then_inc(*one(on_ready))
                for t in range(2):
                    key = ("ao", t)
                    dve.wait_ge(*bank_full(key))
                    xv = x[:, 2 * t:2 * t + 2, :].rearrange("p a b -> p (a b)")
                    nc.vector.scalar_tensor_tensor(out=xv, in0=bank(key)[:, :], scalar=0.5, in1=xv, op0=ALU.mult,
                                                   op1=ALU.add).then_inc(*one(x_ready))

                layer_norm(x, lambda t: after(x_ready, t // 2 + 1))
                dve.wait_ge(*after(xb_ready, 1))
                add_back([("dn", "F", t) for t in range(2)], xb, x, x_ready)

                layer_norm(x, lambda t: after(x_ready, 2 + t // 2 + 1), block=True)
                for t in range(NG):
                    for i, (name, b) in enumerate((("q", "bq"), ("kk", "bk"))):
                        n = 2 * t + i
                        dve.wait_ge(*bank_full((name, t)))
                        if n == 0:
                            dve.wait_ge(*after(zt_ready, 3 * NC))
                        if n >= 4:
                            dve.wait_ge(*bank_full(("qf" if i == 0 else "kf", t - 2)))
                        nc.vector.scalar_tensor_tensor(out=qh[:, n % 4, :], in0=bank((name, t))[:, :],
                                                       scalar=col(b, t), in1=rope[:, :], op0=ALU.add,
                                                       op1=ALU.mult).then_inc(*one(qh_ready))
                for t in range(2):
                    dve.wait_ge(*bank_full(("vb", t)))
                    for a in range(2):
                        ins = nc.vector.tensor_tensor(
                            vaug[:, 2 * t + a, :, 0:HD],
                            bank(("vb", t))[:, a * D:(a + 1) * D].rearrange("p (h d) -> p h d", d=HD),
                            bias_v[:, :].rearrange("p (h d) -> p h d", d=HD), ALU.add)
                    ins.then_inc(*one(vaug_ready))

                def row_max(t, g):
                    c = 32 * g + HD
                    n = (t * HG + g) * 4
                    if t >= 2 and g == 0:
                        dve.wait_ge(*bank_full(("mt", t - 2)))
                    for i, (qt, lo, hi) in enumerate(((3, 0, 512), (2, 0, 384), (0, 384, 512), (1, 0, 256))):
                        b = (0, 1, 1, 2)[i]
                        key = ("S", t, g, b)
                        dve.wait_ge(*bank_full(key))
                        nc.vector.tensor_reduce(maxes[:, t % 2, qt, c:c + 1], bank(key)[:, lo:hi], AX_X,
                                                ALU.max).then_inc(*one(maxs))

                def normalised(t):
                    dve.wait_ge(*after(pt_used, HG * (t + 1)))
                    ob = obank[t % 2][:, 0:NT * HG * (HD + 1)].rearrange("p (q g e) -> p q g e", q=NT, g=HG)
                    if t >= 1:
                        dve.wait_ge(*after(attn_ready, t))
                    nc.vector.reciprocal(rden[:, :, :], ob[:, :, :, HD]).then_inc(*one(rden_ready))
                    dve.wait_ge(*after(rden_ready, t + 1))
                    nc.vector.tensor_tensor(
                        attn[:, :, 64 * t:64 * t + 64].rearrange("p q (g d) -> p q g d", g=HG), ob[:, :, :, 0:HD],
                        rden[:, :, :].unsqueeze(3).to_broadcast([P, NT, HG, HD]), ALU.mult) \
                        .then_inc(*one(attn_ready))

                for g in range(HG):
                    row_max(0, g)
                for t in range(NG):
                    dve.wait_ge(*bank_full(("mt", t)))
                    nc.vector.tensor_tensor(qp[:, t, :], bank(("mt", t))[:, :], qp[:, t, :],
                                            ALU.add).then_inc(*one(qm_ready))
                    if t >= 1:
                        normalised(t - 1)
                    if t + 1 < NG:
                        for g in range(HG):
                            row_max(t + 1, g)
                normalised(NG - 1)
                dve.wait_ge(*after(xb_ready, 2))
                add_back([("wo", t) for t in range(2)], xb, x2, x2_ready)
                layer_norm(x2, lambda t: after(x2_ready, t // 2 + 1))
                dve.wait_ge(*after(xb_ready, 3))
                add_back([("dn", "M", t) for t in range(2)], xb, x, x_ready)
                layer_norm(x, lambda t: after(x_ready, 4 + t // 2 + 1))
                dve.wait_ge(*after(xb_ready, 4))
                add_back([("dn", "G", t) for t in range(2)], xb, x, x_ready)

        @block.tensor
        def _(pe):
            mm = nc.tensor.matmul
            with pe.Fori(0, NF) as t:
                for s in range(LOW):
                    pe.wait_ge(bl_mat.h, t * 2 * LOW + 2 * s + 3 + 1)
                    if s == 0:
                        pe.wait_ge(bl_in.h, t * 16 + 16)
                    pe.wait_ge(bl_ev[0].h, t * LOW + s + 1)
                    mm(ring[s % 2][:, 0:UW], bmat[:, (2 * s) % 4, :], y_st[0][:, s % 2, :], start=True,
                       stop=True).then_inc(bl_mm[0].h, 1)
                    pe.wait_ge(bl_mat.h, t * 2 * LOW + 2 * s + 3 + 2)
                    if s:
                        pe.wait_ge(bl_ev[1].h, t * LOW + s)
                        src = y_st[1][:, s % 2, :]
                    else:
                        src = bdn[:, bass.ds(t, 1), :].rearrange("p a n -> p (a n)")
                    mm(ring[2 + s % 2][:, 0:D], bmat[:, (2 * s + 1) % 4, :], src, start=True,
                       stop=True).then_inc(bl_mm[1].h, 1)
            pe.wait_ge(bh_s.h, 2 * 3 * NF)
            for m in range(NF):
                for c in range(NC):
                    n = m * NC + c
                    if n >= 4:
                        pe.wait_ge(bt_ev.h, n - 3)
                    nc.tensor.transpose(ring[n % 4][:, 0:P], y_up2[:, m, c * P:(c + 1) * P],
                                        ident[:, :]).then_inc(*one(bt_mm))
            pe.wait_ge(seeded.h, 2)
            pe.wait_ge(pre.h, 16 * N_LOADS)
            pe.wait_ge(consts.h, 8)

            with pe.Fori(0, B) as it:
                def after(s, k):
                    return s.h, it * s.per + k

                count = [0]

                def take(key):
                    assert order[count[0]] == key, (order[count[0]], key)
                    count[0] += 1
                    if count[0] > RING:
                        pe.wait_ge(*after(*copied(order[count[0] - 1 - RING])))
                    return ring[bank_of[key]]

                def filled(key):
                    return one(full[bank_of[key]])

                nln = [0]

                def turn(tag, src, ready):
                    for c in range(NC):
                        ps = take(("zt", tag, c))
                        for t in range(NT):
                            if c == 0:
                                pe.wait_ge(*ready(t))
                            ins = nc.tensor.transpose(ps[:, t * P:(t + 1) * P], src[:, t, c * P:(c + 1) * P],
                                                      ident[:, :])
                        ins.then_inc(*filled(("zt", tag, c)))

                def dense(key, w, lo, hi, src, rows=P):
                    ps = take(key)
                    for c in range(NC):
                        ins = mm(ps[0:hi - lo, :], w[:, c, lo:hi], src[:, c, :], start=(c == 0), stop=(c == NC - 1))
                    ins.then_inc(*filled(key))

                def dense_rows(keys, src, w, nk):
                    for t2, key in enumerate(keys):
                        ps = take(key)
                        for t in range(2):
                            tok = (2 * t2 + t) * P
                            for c in range(nk):
                                ins = mm(ps[:, t * D:(t + 1) * D], src[:, c, tok:tok + P], w[:, c, :],
                                         start=(c == 0), stop=(c == nk - 1))
                        ins.then_inc(*filled(key))

                turn("A", z, lambda t: after(z_ready, t + 1))
                for i in range(2):
                    if i == 0:
                        pe.wait_ge(*after(mix0_ready, NC))
                    dense(("xl", i), w1, i * P, P + i * RMIX, mix[:, 2])

                def low_rank(a, n):
                    pe.wait_ge(*after(xl_ready, 1 if n < 4 else 2))
                    for c in range(NC):
                        ps = take(("x5", n, c))
                        if n < 4:
                            ins = mm(ps[:, :], w2a[32 * n:32 * n + 32, c * P:(c + 1) * P], xl0[32 * n:32 * n + 32, :],
                                     start=True, stop=True)
                        else:
                            ins = mm(ps[:, :], w2b[:, c * P:(c + 1) * P], xl1[:, :], start=True, stop=True)
                        ins.then_inc(*filled(("x5", n, c)))

                def project(a, n):
                    pe.wait_ge(*after(mix_ready, (a + 1) * NC))
                    src = mix[:, a % 3]
                    if n == 1:
                        dense(("wa",), wwa, 0, LR, src)
                        pe.wait_ge(*after(wa_ready, 1))
                        for h in range(H):
                            ps = take(("w", h))
                            mm(ps[:, :], wwb[:, h * DK:(h + 1) * DK], wat[:, :], start=True, stop=True) \
                                .then_inc(*filled(("w", h)))
                    elif n == 2:
                        for h in range(H):
                            dense(("k", h), wk, h * DK, (h + 1) * DK, src)
                    elif n == 0:
                        for h in range(H):
                            dense(("r", h), wr, h * DK, (h + 1) * DK, src)
                    elif n == 3:
                        dense_rows([("v", t) for t in range(2)], src, wv, NC)
                    else:
                        dense(("ga",), wga, 0, LR, src)
                        pe.wait_ge(*after(ga_ready, 1))
                        for c in range(NC):
                            ps = take(("g", c))
                            mm(ps[:, :], wgb[:, c * P:(c + 1) * P], gat[:, :], start=True, stop=True) \
                                .then_inc(*filled(("g", c)))

                for a, n in enumerate(MIX_ORDER):
                    low_rank(a, n)
                    if a >= 1:
                        project(a - 1, MIX_ORDER[a - 1])
                project(NMIX - 1, MIX_ORDER[-1])

                for lv in range(len(LEVELS)):
                    for h in range(H):
                        if lv == 0:
                            pe.wait_ge(*after(kg_ready, h + 1))
                            pe.wait_ge(*after(qu_ready, h + 1))
                        if lv >= 2:
                            pe.wait_ge(*after(kg_level, (lv - 2) * H + h + 1))
                            pe.wait_ge(*after(qf_level, (lv - 2) * H + h + 1))
                        ps = take(("A", lv, h))
                        q = qu if lv == 0 else qf
                        for c in range(NT):
                            tok = slice(c * P, (c + 1) * P)
                            ins = mm(ps[:, tok], kg[:, h, tok], q[:, h, tok], start=True, stop=True)
                        ins.then_inc(*filled(("A", lv, h)))
                for h in range(H):
                    pe.wait_ge(*after(kg_level, 6 * H + h + 1))
                    ps = take(("kt", h))
                    for c in range(NT - 1):
                        ins = nc.tensor.transpose(ps[:, c * P:(c + 1) * P], kg[:, h, c * P:(c + 1) * P], ident[:, :])
                    ins.then_inc(*filled(("kt", h)))
                pe.wait_ge(*after(v_ready, 2))
                for c in range(NT - 1):
                    ps = take(("s", c))
                    for h in range(H):
                        if c == 0:
                            pe.wait_ge(*after(kt_ready, h + 1))
                        ins = mm(ps[:, h * DV:(h + 1) * DV], kt[:, h, c, :], v[:, c, h * DV:(h + 1) * DV],
                                 start=True, stop=True)
                    ins.then_inc(*filled(("s", c)))
                pe.wait_ge(*after(a_copied, len(LEVELS) * H))
                pe.wait_ge(*after(qf_level, 7 * H))
                for c in range(NT):
                    if c % 2 == 0:
                        ps = take(("o", c // 2))
                    if c >= 1:
                        pe.wait_ge(*after(state_ready, c))
                    for h in range(H):
                        dst = ps[:, (c % 2) * D + h * DV:(c % 2) * D + (h + 1) * DV]
                        ins = mm(dst, scores[:, h, c, :], v[:, c, h * DV:(h + 1) * DV], start=True, stop=(c == 0))
                        if c >= 1:
                            ins = mm(dst, qf[:, h, c * P:(c + 1) * P], state[:, c - 1, h, :], start=False, stop=True)
                    if c % 2:
                        ins.then_inc(*filled(("o", c // 2)))
                for c in range(NC):
                    ps = take(("ogt", c))
                    for t in range(NT):
                        if c == 0:
                            pe.wait_ge(*after(on_ready, t + 1))
                        ins = nc.tensor.transpose(ps[:, t * P:(t + 1) * P], on[:, t, c * P:(c + 1) * P], ident[:, :])
                    ins.then_inc(*filled(("ogt", c)))
                pe.wait_ge(*after(og_ready, NC))
                dense_rows([("ao", t) for t in range(2)], ogate, wo, NC)

                nffn = [0]

                def ffn(tag, src, ready, wu, wd):
                    n = {"F": 1, "M": 3, "G": 4}[tag]
                    turn(tag, src, ready)
                    for m in range(NF):
                        if m == 0:
                            pe.wait_ge(*after(zt_ready, (n + 1) * NC))
                        dense(("up", tag, m), wu, m * P, (m + 1) * P, zt[:, :, 1:T + 1])
                    pe.wait_ge(*after(gelu_ready, (nffn[0] + 1) * NF))
                    nffn[0] += 1
                    dense_rows([("dn", tag, t) for t in range(2)], gelu, wd, NF)

                ffn("F", z, lambda t: after(z_ready, NT + t + 1), wup, wdn)

                turn("B", z2, lambda t: after(z2_ready, t + 1))
                pe.wait_ge(*after(zt_ready, 3 * NC))
                nrm = zt[:, :, 1:T + 1]
                dense(("q", 0), wq_b, 0, P, nrm)
                dense(("kk", 0), wk_b, 0, P, nrm)
                for t in range(NG):
                    if t + 1 < NG:
                        dense(("q", t + 1), wq_b, (t + 1) * P, (t + 2) * P, nrm)
                        dense(("kk", t + 1), wk_b, (t + 1) * P, (t + 2) * P, nrm)
                    for i, name in enumerate(("qf", "kf")):
                        pe.wait_ge(*after(qh_ready, 2 * t + i + 1))
                        ps = take((name, t))
                        mm(ps[:, :], fold[:, :], qh[:, (2 * t + i) % 4, :], start=True, stop=True) \
                            .then_inc(*filled((name, t)))
                dense_rows([("vb", t) for t in range(2)], nrm, wv_b, NC)

                def s_max(t, g):
                    r = slice(32 * g, 32 * g + 32)
                    if g == 0:
                        pe.wait_ge(*after(rqk_ready, 2 * t + 2))
                    for b, parts in enumerate((((3, 0),), ((2, 0), (0, 384)), ((1, 0),))):
                        ps = take(("S", t, g, b))
                        for qt, lo in parts:
                            n = (qt + 1) * P
                            mm(ps[:, lo:lo + n], rqk[r, t % 2, 0, qt * P:(qt + 1) * P], rqk[r, t % 2, 1, 0:n],
                               start=True, stop=False)
                            ins = mm(ps[:, lo + n - P:lo + n], identb, future, start=False, stop=True)
                        ins.then_inc(*filled(("S", t, g, b)))

                def s_exp(t, g):
                    r = slice(32 * g, 32 * g + 32)
                    for b, parts in enumerate((((0, 0),), ((1, 0), (3, 384)), ((2, 0),))):
                        ps = take(("ST", t, g, b))
                        for jt, lo in parts:
                            n = T - jt * P
                            mm(ps[:, lo:lo + n], kp[r, t, jt * P:(jt + 1) * P], qp[r, t, jt * P:T],
                               start=True, stop=False)
                            ins = mm(ps[:, lo:lo + P], identb, future_t, start=False, stop=True)
                        ins.then_inc(*filled(("ST", t, g, b)))

                def pv(t, g):
                    n = t * HG + g
                    if g == 0 and t >= 2:
                        pe.wait_ge(*after(attn_ready, t - 1))
                    pe.wait_ge(*after(pt_ready, 3 * n + 3))
                    base = {0: 0, 1: 512, 3: 896, 2: 1024}
                    for qt in range(NT):
                        lo = (qt * HG + g) * (HD + 1)
                        for jt in range(qt + 1):
                            c = base[jt] + (qt - jt) * P
                            ins = mm(obank[t % 2][:, lo:lo + HD + 1], pt[:, n % NPT, c:c + P],
                                     vaug[:, jt, n, :], start=(jt == 0), stop=(jt == qt))
                    ins.then_inc(*one(pt_used))

                for g in range(HG):
                    s_max(0, g)
                pe.wait_ge(*after(vaug_ready, 2))
                for t in range(NG):
                    pe.wait_ge(*after(maxs, 4 * HG * (t + 1)))
                    ps = take(("mt", t))
                    for qt in range(NT):
                        ins = nc.tensor.transpose(ps[:, qt * P:(qt + 1) * P], maxes[:, t % 2, qt, :], ident[:, :])
                    ins.then_inc(*filled(("mt", t)))
                    if t >= 1:
                        pv(t - 1, HG - 1)
                    for g in range(HG):
                        if t + 1 < NG:
                            s_max(t + 1, g)
                        if g == 0:
                            pe.wait_ge(*after(qm_ready, t + 1))
                        s_exp(t, g)
                        if g >= 1:
                            pv(t, g - 1)
                pv(NG - 1, HG - 1)
                pe.wait_ge(*after(attn_ready, NG))
                for c in range(NC):
                    ps = take(("aot", c))
                    for t in range(NT):
                        ins = nc.tensor.transpose(ps[:, t * P:(t + 1) * P], attn[:, t, c * P:(c + 1) * P], ident[:, :])
                    ins.then_inc(*filled(("aot", c)))
                pe.wait_ge(*after(at_ready, NC))
                dense_rows([("wo", t) for t in range(2)], attn_t, wo_b, NC)
                ffn("M", z, lambda t: after(z_ready, 3 * NT + t + 1), wm1, wm2)
                ffn("G", z, lambda t: after(z_ready, 4 * NT + t + 1), wup, wdn)
                assert count[0] == len(order)

        for s in sems:
            assert not s.per or s.made in (s.per, 0), (s.name, s.per, s.made)


def layouts(i):
    def c(a):
        return np.ascontiguousarray(a)

    def tiles(a, n):
        return a.reshape(n, P).T

    A, Bk, Fn = "L0_attn_a_", "L0_attn_b_", "L0_ffn_"
    i = {k: np.asarray(v) for k, v in i.items()}
    f = np.float32
    o = {"x": i[A + "hidden_states"]}
    o["w1"] = c(i[A + "xp_W1"].T)
    o["w2"] = c(i[A + "xp_W2"].T)
    o["wr"], o["wk"], o["wv"] = c(i[A + "r_W"].T), c(i[A + "k_W"].T), c(i[A + "v_W"].T)
    o["wwa"], o["wwb"] = c(i[A + "w_A"].T), c(i[A + "w_B"].T)
    o["wga"] = c(i[A + "g_A"].T)
    o["wgb"] = c(np.concatenate([i[A + "g_B"].T, i[A + "g_b"][None, :]], 0))
    o["wo"] = c(i[A + "o_W"].T)
    src = np.array([h * HD + d if r == 0 else h * HD + (d + HD // 2) % HD
                    for h in range(NH) for r in range(2) for d in range(HD)])
    W, bb = i[Bk + "Wqkv"], i[Bk + "bqkv"]
    o["wq_b"], o["wk_b"], o["wv_b"] = c(W[:, src]), c(W[:, D + src]), c(W[:, 2 * D:3 * D])
    o["bv"], o["bo"], o["b2"] = c(bb[2 * D:3 * D]), i[Bk + "bo"], i[Bk + "b2"]
    o["wo_b"], o["wm1"], o["wm2"] = i[Bk + "Wo"], i[Bk + "W1"], i[Bk + "W2"]
    minus = np.zeros((P, 1), f)
    minus[HD::32] = -1.0
    o["cols"] = c(np.concatenate([
        tiles(i[A + "xp_mu"], NC), tiles(i[A + "x_bias"], NMIX * NC), tiles(i[A + "w_b"], H), i[A + "bonus"].T,
        tiles(i[A + "gn_w"], NC), tiles(i[A + "gn_b"], NC), tiles(i[Bk + "ln1_g"], NC), tiles(i[Bk + "ln1_b"], NC),
        tiles(i[Bk + "ln2_g"], NC), tiles(i[Bk + "ln2_b"], NC), tiles(bb[src], NG), tiles(bb[D + src], NG),
        tiles(i[Bk + "b1"], NF), tiles(i[Fn + "up_bias"], NF), minus], 1))
    o["b_con"], o["down_b"], o["w_con"] = i[Fn + "b_con"], i[Fn + "down_bias"], i[Fn + "W_con"]
    o["w_exp_t"] = c(np.concatenate([i[Fn + "W_exp"].T, i[Fn + "b_exp"][:, None]], 1))
    n = np.arange(FF)
    parts = []
    for kind in range(3):
        for name in ("up_weights", "down_weights"):
            w = i[Fn + name]
            byst = []
            for s in range(STAGES):
                S = 1 << s
                bit = (n >> s) & 1
                k = (n // (2 * S)) * S + n % S
                a_, b_ = ((bit, bit), (bit, 1 - bit), (1 - bit, bit))[kind]
                byst.append(w[s][k, a_, b_])
            parts.append(np.stack(byst, 1).reshape(NF, P, STAGES).transpose(1, 0, 2))
    o["bw"] = c(np.stack(parts, 1).reshape(P, 3, 2, NF, STAGES))
    q = np.arange(P)
    o["ident"] = np.eye(P, dtype=f)
    o["perm"] = c(np.stack([(q[:, None] == (q[None, :] ^ (1 << s))).astype(f) for s in range(LOW)], 1))
    o["fold"] = c(((q[:, None] // 32 == q[None, :] // 32) & (q[None, :] % 32 < HD)
                   & (q[:, None] % HD == q[None, :] % HD)).astype(f))
    freq = (1.0 / 10000.0 ** (np.arange(0, HD, 2, dtype=f) / f(HD))).astype(f)
    ang = np.arange(T, dtype=f)[None, :] * np.concatenate([freq, freq])[:, None]
    sign = np.where(np.arange(HD) < HD // 2, -1.0, 1.0).astype(f)[:, None]
    o["rope"] = c(np.tile(np.concatenate([np.cos(ang), np.sin(ang) * sign], 0).astype(f), (HG, 1)))
    j, k = q[:, None], q[None, :]
    masks = [j == k] + [(j // (2 * s) == k // (2 * s)) & (j // s % 2 == 0) & (k // s % 2 == 1)
                        for s in LEVELS[1:]]
    o["masks"] = c(np.stack([np.eye(P, dtype=f), np.where(k > j, NEG, 0.0), np.where(j > k, NEG, 0.0)]
                           + [m.astype(f) for m in masks], 1).astype(f))
    return o


def kernel(**inputs):
    import concourse.bacc as _bacc
    from concourse.bass_utils import run_bass_kernel_spmd as _run

    nc = _bacc.Bacc("TRN2", target_bir_lowering=False, num_devices=1)
    arrays, io = {}, {}
    for name, a in layouts(inputs).items():
        arrays[f"in_{name}"] = np.ascontiguousarray(a)
        io[name] = nc.dram_tensor(f"in_{name}", a.shape, mybir.dt.from_np(a.dtype), kind="ExternalInput").ap()
    out = nc.dram_tensor("out", (B, T, D), F32, kind="ExternalOutput").ap()
    hybrid_kernel(nc, io, out)
    r = _run(nc, [arrays], core_ids=[0])
    return r.results[0]["out"]
```

```python
from contextlib import ExitStack

import numpy as np

import concourse.bass as bass
from concourse import mybir

F32 = mybir.dt.float32
F32R = mybir.dt.float32r
BF16 = mybir.dt.bfloat16
U16 = mybir.dt.uint16
ALU = mybir.AluOpType
ACT = mybir.ActivationFunctionType
AX_X = mybir.AxisListType.X

P = 128
B, T, D = 8, 512, 256
NT = T // P
NC = D // P
H, DK, DV = 4, 128, 64
LR = 64
NMIX, RMIX = 5, 32
NH, HD = 16, 16
HG = 4
NG = NH // HG
FF = 1024
NF = FF // P
EPS = 1e-5
STAGES = 10
LOW = 7
LEVELS = [0, 1, 2, 4, 8, 16, 32, 64]
MIX_ORDER = [1, 2, 0, 3, 4]
AHEAD = [[0, 1], [2], [3], []]
HT = T // 2
RING = 6
NEG = -1e30

COLS = {}
_at = 0
for _name, _n in (("mu", NC), ("xbias", NMIX * NC), ("w_b", H), ("bonus", H), ("gn_w", NC), ("gn_b", NC),
                  ("ln1_g", NC), ("ln1_b", NC), ("ln2_g", NC), ("ln2_b", NC), ("bq", NG), ("bk", NG),
                  ("b1", NF), ("up_b", NF), ("minus_row", 1)):
    COLS[_name] = _at
    _at += _n
NCOLS = _at


def psum_order():
    o = [("zt", "A", 0), ("zt", "A", 1), ("xl", 0), ("xl", 1)]

    def project(n):
        if n == 1:
            return [("wa",)] + [("w", h) for h in range(H)]
        if n == 2:
            return [("k", h) for h in range(H)]
        if n == 0:
            return [("r", h) for h in range(H)]
        if n == 3:
            return [("v", t) for t in range(2)]
        return [("ga",)] + [("g", c) for c in range(NC)]

    for a, n in enumerate(MIX_ORDER):
        o += [("x5", n, c) for c in range(NC)]
        if a >= 1:
            o += project(MIX_ORDER[a - 1])
    o += project(MIX_ORDER[-1])
    o += [("A", lv, h) for lv in range(len(LEVELS)) for h in range(H)]
    o += [("kt", h) for h in range(H)] + [("s", c) for c in range(NT - 1)]
    o += [("o", t) for t in range(2)] + [("ogt", c) for c in range(NC)] + [("ao", t) for t in range(2)]

    def ffn(tag):
        return ([key for hf in range(2)
                 for key in [("zt", tag, hf)] + [("up", tag, hf, m) for m in range(NF // 2)]]
                + [("dn", tag, t) for t in range(2)])

    o += ffn("F")
    o += [("zt", "B", 0), ("vb", 0), ("zt", "B", 1)]
    o += [("q", 0), ("kk", 0)]
    for t in range(NG):
        if t + 1 < NG:
            o += [("q", t + 1), ("kk", t + 1)]
        o += [("qf", t), ("kf", t)]
    o += [("vb", 1)]
    o += [("S", 0, g, i) for g in range(HG) for i in range(3)] + [("mt", 0)]
    for t in range(NG):
        for g in range(HG):
            if t + 1 < NG:
                o += [("S", t + 1, a, i) for a in AHEAD[g] for i in range(3)]
            o += [("ST", t, g, i) for i in range(3)]
            if g == 1 and t >= 1:
                o += [("den", t - 1)]
            if g == HG - 1 and t + 1 < NG:
                o += [("mt", t + 1)]
    o += [("den", NG - 1)] + [("wo", t) for t in range(2)]
    o += ffn("M")
    o += ffn("G")
    return o


def hybrid_kernel(nc, io, out):
    order = psum_order()
    bank_of, use_of, uses = {}, {}, [0] * RING
    for n, key in enumerate(order):
        bank_of[key] = n % RING
        use_of[key] = uses[n % RING]
        uses[n % RING] += 1

    with ExitStack() as ctx:
        def sb(name, shape, dt=F32):
            return ctx.enter_context(nc.sbuf_tensor(name, shape, dt))

        class Sem:

            def __init__(self, name, per):
                self.h = ctx.enter_context(nc.semaphore(name))
                self.name, self.per, self.made = name, per, 0

        sems = []

        def sem(name, per=0):
            s = Sem(name, per)
            sems.append(s)
            return s

        def one(s):
            s.made += 1
            return s.h, 1

        w1 = sb("w_mix1", [P, NC, NMIX * RMIX])
        w2a = sb("w_mix2a", [P, D])
        w2b = sb("w_mix2b", [RMIX, D])
        wr = sb("w_r", [P, NC, H * DK])
        wk = sb("w_k", [P, NC, H * DK])
        wv = sb("w_v", [P, NC, H * DV])
        wwa = sb("w_decay_a", [P, NC, LR])
        wwb = sb("w_decay_b", [LR, H * DK])
        wga = sb("w_gate_a", [P, NC, LR])
        wgb = sb("w_gate_b", [LR + 1, D])
        wo = sb("w_mixer_out", [P, NC, D])
        wup = sb("w_up", [P, NC, FF])
        wdn = sb("w_down", [P, NF, D])
        wq_b = sb("w_q", [P, NC, NG * P])
        wk_b = sb("w_kk", [P, NC, NG * P])
        wv_b = sb("w_vv", [P, NC, D])
        wo_b = sb("w_attn_out", [P, NG, D])
        wm1 = sb("w_mlp1", [P, NC, FF])
        wm2 = sb("w_mlp2", [P, NF, D])
        cols = sb("cols", [P, NCOLS])
        upb = sb("up_bias", [P, NF])
        bias_f = sb("bias_ffn", [P, D])
        bias_o = sb("bias_attn_out", [P, D])
        bias_m = sb("bias_mlp", [P, D])
        bias_v = sb("bias_v", [P, D])
        ident = sb("ident", [P, P])
        masks = sb("masks", [P, 3 + len(LEVELS), P], BF16)
        identb = masks[:, 0, :]
        future = masks[:, 1, :]
        future_t = masks[:, 2, :]
        lmask = masks[:, 3:, :]
        fold = sb("fold", [P, P])
        rope = sb("rope", [P, T])

        x = sb("x", [P, NT, D])
        z = sb("z", [P, NT, D])
        xb = sb("x_plus_bias", [P, NT, D])
        x2 = sb("x_block", [P, NT, D])
        zt = sb("z_t", [P, NC, T + 1])
        delta = sb("delta", [P, NC, T])
        mix = sb("mix", [P, 3, NC, T])
        xl0 = sb("xl0", [P, T])
        xl1 = sb("xl1", [RMIX, T])
        stats = sb("stats", [P, NT, 6])
        mv = sb("mean_var", [P, NT, 2])
        rstd = sb("rstd", [P, 3, NT])
        power = sb("eps_and_power", [P, 2, NT])
        big = sb("big", [P, 16, T])
        dec = sb("decay", [P, H, T])
        dtree = sb("decay_blocks", [P, H, T])
        wat = sb("wa_t", [LR, T])
        gat = sb("ga_t", [LR + 1, T])
        v = sb("v", [P, NT, H * DV])
        scores = sb("scores_t", [P, H, NT, P])
        state = sb("state", [P, NT - 1, H, DV])
        gate = sb("gate", [P, NC, T])
        rqk = sb("qk_rounded", [P, 2, 2, T], F32R)
        vaug = sb("v_ones", [P, NT, NH, 2 * HD])
        den_row = sb("den_row", [P, P])
        maxes = sb("maxes", [P, 2, NT, P])

        qf, qu, kg = big[:, 0:4], big[:, 4:8], big[:, 8:12]
        kt = big[:, 12:16].rearrange("p h (c k) -> p h c k", c=NT)
        gelu = big[:, 0:8]
        qp, kp = big[:, 0:4], big[:, 4:8]
        NPT = 3
        pt = big[:, 8:16].rearrange("p a t -> p (a t)")[:, 0:NPT * 1280].rearrange("p (r n) -> p r n", r=NPT)
        on = mix[:, 0].rearrange("p c t -> p (c t)").rearrange("p (t d) -> p t d", t=NT)
        ogate = mix[:, 1]
        gtanh = mix[:, 2]
        qh = mix[:, 1:3].rearrange("p a c t -> p (a c) t")
        attn_t = mix[:, 0:2].rearrange("p a c t -> p (a c) t")
        osum = delta[:, :, :]
        rden = mix[:, 2]
        z2 = on

        dblk, at = {0: dec[:, :, :]}, 0
        for lv in range(1, 8):
            n = T >> lv
            dblk[lv] = dtree[:, :, at:at + n]
            at += n

        ring = [ctx.enter_context(nc.psum_tensor(f"ring{i}", [P, T], F32)) for i in range(RING)]
        obank = [ctx.enter_context(nc.psum_tensor(f"attn_out{i}", [P, T], F32)) for i in range(2)]

        wload = sem("weights_loaded")
        full = [sem(f"bank_full{i}", uses[i]) for i in range(RING)]
        x_in = sem("x_loaded", 16)
        x_out = sem("x_stored", 16)
        x_ready = sem("x_ready", 2 * 4)
        x2_ready = sem("x2_ready", 2)
        lns = sem("ln_steps", 5 * 2 * NT)
        lnb = sem("ln_block_steps", 4)
        rs_step = sem("rstd_step", 5 * 2 + 1 + 2)
        rs_ready = sem("rstd_ready", 5 * 2 + 1 + 2)
        z_ready = sem("z_ready", 5 * NT)
        z2_ready = sem("z2_ready", NT)
        zt_ready = sem("zt_ready", 5 * 2)
        delta_ready = sem("delta_ready", NC)
        mix0_ready = sem("mix0_ready", NC)
        xl_ready = sem("xl_ready", 2)
        mixd_ready = sem("mix_delta_ready", NMIX * NC)
        mix_ready = sem("mix_ready", NMIX * NC)
        wa_ready = sem("wa_ready", 1)
        ga_ready = sem("ga_ready", 1)
        ew_ready = sem("exp_w_ready", H)
        dec_ready = sem("decay_ready", H)
        tree_ready = sem("tree_ready", 7)
        kg_ready = sem("k_ready", H)
        qf_ready = sem("q_ready", H)
        qu_ready = sem("q_bonus_ready", H)
        kg_level = sem("k_level", 7 * H)
        qf_level = sem("q_level", 7 * H)
        v_ready = sem("v_ready", 2)
        gt_ready = sem("gate_tanh", NC)
        gate_ready = sem("gate_ready", NC)
        a_copied = sem("scores_copied", len(LEVELS) * H)
        gating = sem("dve_gate", 0)
        pool_gate = sem("pool_gate", 0)
        sp_gate = sem("sp_gate", 0)
        kt_ready = sem("k_rows_ready", H)
        state_ready = sem("state_ready", NT - 1)
        gstat = sem("gn_steps", 2 * NT)
        on_ready = sem("o_normed", NT)
        oaff_ready = sem("o_affine", NC)
        og_ready = sem("o_gated", NC)
        xb_ready = sem("xb_ready", 4)
        xs_step = sem("xs_step", 1)
        gelu_ready = sem("gelu_ready", 3 * NF)
        qh_ready = sem("qh_ready", 2 * NG)
        qp_ready = sem("qp_ready", 2 * NG)
        rqk_ready = sem("rounded_ready", 2 * NG)
        vaug_ready = sem("vaug_ready", 2)
        maxs = sem("max_steps", NG * HG * 4)
        qm_ready = sem("q_shifted", NG)
        pt_ready = sem("p_ready", NH * 3)
        pt_used = sem("p_used", NH)
        attn_ready = sem("attn_ready", NG)
        rden_ready = sem("rden_ready", NG)
        osum_ready = sem("osum_ready", NG)
        def copied(key):
            kind, a = key[0], key[1:]
            if kind in ("zt", "dn"):
                layer = "AFBMG".index(a[0])
                return (zt_ready, layer * 2 + a[1] + 1) if kind == "zt" else \
                    (x_ready, {1: 2, 3: 4, 4: 6}[layer] + a[1] + 1)
            return {
                "xl": lambda i: (xl_ready, i + 1),
                "x5": lambda n, c: (mixd_ready, MIX_ORDER.index(n) * NC + c + 1),
                "wa": lambda: (wa_ready, 1),
                "w": lambda h: (ew_ready, h + 1),
                "k": lambda h: (kg_ready, h + 1),
                "r": lambda h: (qf_ready, h + 1),
                "v": lambda t: (v_ready, t + 1),
                "ga": lambda: (ga_ready, 1),
                "g": lambda c: (gate_ready, c + 1),
                "A": lambda lv, h: (a_copied, lv * H + h + 1),
                "kt": lambda h: (kt_ready, h + 1),
                "s": lambda c: (state_ready, c + 1),
                "o": lambda t: (on_ready, 2 * t + 2),
                "ogt": lambda c: (oaff_ready, c + 1),
                "ao": lambda t: (x_ready, t + 1),
                "up": lambda tag, hf, m: (gelu_ready, "FMG".index(tag) * NF + hf * (NF // 2) + m + 1),
                "q": lambda t: (qh_ready, 2 * t + 1),
                "kk": lambda t: (qh_ready, 2 * t + 2),
                "qf": lambda t: (qp_ready, 2 * t + 1),
                "kf": lambda t: (qp_ready, 2 * t + 2),
                "vb": lambda t: (vaug_ready, t + 1),
                "S": lambda t, g, b: (maxs, (t * HG + g) * 4 + (1, 3, 4)[b]),
                "mt": lambda t: (qm_ready, t + 1),
                "ST": lambda t, g, i: (pt_ready, (t * HG + g) * 3 + i + 1),
                "den": lambda t: (rden_ready, t + 1),
                "wo": lambda t: (x2_ready, t + 1),
            }[kind](*a)

        consts = sem("constants_set")
        bl_in = sem("butterfly_tile_in")
        bl_cols = sem("butterfly_cols")
        bl_diag = sem("butterfly_diag")
        bl_mat = sem("butterfly_matrix")
        bl_mm = [sem("butterfly_mm_up"), sem("butterfly_mm_down")]
        bl_ev = [sem("butterfly_evac_up"), sem("butterfly_evac_down")]
        bh_t = sem("butterfly_high_same")
        bh_s = sem("butterfly_high")
        bt_mm = sem("w_up_turned")
        bt_ev = sem("w_up_copied")
        pre = sem("biases_ready")
        seeded = sem("seeded")

        flat = big[:, :, :].rearrange("p a t -> p (a t)")
        UW = D + 1
        y_up = flat[:, 0:NF * UW].rearrange("p (t n) -> p t n", t=NF)
        y_up2 = flat[:, NF * UW:2 * NF * UW].rearrange("p (t n) -> p t n", t=NF)
        dflat = mix[:, :, :, :].rearrange("p a c t -> p (a c t)")
        y_dn = flat[:, 2 * NF * UW:2 * NF * UW + NF * D].rearrange("p (t n) -> p t n", t=NF)
        masks_in = flat[:, 2 * NF * UW + NF * D:2 * NF * UW + NF * D + (3 + len(LEVELS)) * P]
        bw = dflat[:, 0:3 * 2 * NF * STAGES].rearrange("p (k w t s) -> p k w t s", k=3, w=2, t=NF)
        perm = dflat[:, 512:512 + LOW * P].rearrange("p (s n) -> p s n", s=LOW)
        bcol = dflat[:, 1408:1408 + 6 * STAGES].rearrange("p (k w s) -> p k w s", k=3, w=2)
        diag = dflat[:, 1536:1536 + 4 * P].rearrange("p (r n) -> p r n", r=4)
        bmat = dflat[:, 2048:2048 + 4 * P].rearrange("p (r n) -> p r n", r=4)
        ystep = v[:, :, :].rearrange("p a b -> p (a b)")[:, 0:4 * D].rearrange("p (r n) -> p r n", r=4)
        scratch = delta[:, :, :].rearrange("p c t -> p (c t)")
        y_st = [scratch[:, 0:2 * UW].rearrange("p (r n) -> p r n", r=2), ystep[:, 0:2, :]]
        tmp_h = scratch[:, 2 * UW:3 * UW]
        bdn = scores[:, :, :, :].rearrange("p h c n -> p (h c n)")[:, 0:NF * D].rearrange("p (t n) -> p t n", t=NF)

        def col(name, i=0):
            return cols[:, COLS[name] + i:COLS[name] + i + 1]

        block = ctx.enter_context(nc.Block())
        dflt = io

        small_loads = [
            (cols[:, :], dflt["cols"]), (ident[:, :], dflt["ident"]), (perm, dflt["perm"]),
            (masks_in, dflt["masks"].rearrange("p s n -> p (s n)")), (bw, dflt["bw"]), (y_dn, dflt["w_con"].rearrange("(t p) n -> p t n", p=P)),
        ]

        def chunked(a):
            return a.rearrange("(c p) n -> p c n", p=P)

        loads = [
            (w1[:, :, :], chunked(dflt["w1"])), (w2a[:, :], dflt["w2"][0:P, :]),
            (w2b[:, :], dflt["w2"][P:P + RMIX, :]), (wr[:, :, :], chunked(dflt["wr"])),
            (wk[:, :, :], chunked(dflt["wk"])), (wv[:, :, :], chunked(dflt["wv"])),
            (wwa[:, :, :], chunked(dflt["wwa"])), (wwb[:, :], dflt["wwb"]),
            (wga[:, :, :], chunked(dflt["wga"])), (wgb[:, :], dflt["wgb"]),
            (wo[:, :, :], chunked(dflt["wo"])), (wq_b[:, :, :], chunked(dflt["wq_b"])),
            (wk_b[:, :, :], chunked(dflt["wk_b"])), (wv_b[:, :, :], chunked(dflt["wv_b"])),
            (wo_b[:, :, :], chunked(dflt["wo_b"])), (wm1[:, :, :], chunked(dflt["wm1"])),
            (den_row[:, :], dflt["den_row"]),
            (wm2[:, :, :], chunked(dflt["wm2"])), (fold[:, :], dflt["fold"]), (rope[:, :], dflt["rope"]),
        ]
        for tile, name in ((bias_f, "b_con"), (xb[:, 0, :], "down_b"), (bias_o, "bo"), (bias_m, "b2"),
                           (bias_v, "bv")):
            dst = tile[:, :] if name != "down_b" else tile
            loads.append((dst, dflt[name].rearrange("(a n) -> a n", a=1).to_broadcast([P, D])))
        N_SMALL, N_LOADS = len(small_loads), len(loads)
        w_up_dram = dflt["w_exp_t"].rearrange("(t p) n -> t p n", p=P)
        x_dram = dflt["x"].rearrange("b (t p) d -> b p t d", p=P)
        out_dram = out.rearrange("b (t p) d -> b p t d", p=P)

        @block.sync
        def _(sp):
            for dst, src in small_loads:
                sp.dma_start(dst, src).then_inc(wload.h, 16)
            with sp.Fori(0, NF) as t:
                sp.wait_ge(bl_ev[0].h, t * LOW + 1)
                sp.dma_start(y_st[0][:, 0, :], w_up_dram[t]).then_inc(bl_in.h, 16)
            with sp.Fori(0, B) as it:
                sp.dma_start(x[:, :, :], x_dram[it]).then_inc(x_in.h, 16)
                sp.wait_ge(x_ready.h, it * x_ready.per + 8)
                sp.dma_start(out_dram[it], x[:, :, :]).then_inc(x_out.h, 16)
                sp.wait_ge(x_out.h, it * 16 + 16)
                sp.sem_inc(sp_gate.h, 1)

        @block.gpsimd
        def _(pool):
            for n, (dst, src) in enumerate(loads):
                pool.dma_start(dst, src).then_inc(pre.h, 16)
            nc.gpsimd.memset(zt[:, :, :], 0.0).then_inc(*one(consts))
            nc.gpsimd.memset(scores[:, :, :, :], 0.0).then_inc(*one(consts))
            nc.gpsimd.memset(maxes[:, :, :, :], 0.0).then_inc(*one(consts))
            nc.gpsimd.memset(vaug[:, :, :, :], 1.0).then_inc(*one(consts))
            nc.gpsimd.memset(gat[:, :], 1.0).then_inc(*one(consts))
            nc.gpsimd.memset(power[:, 0, :], EPS).then_inc(*one(consts))
            nc.gpsimd.memset(power[:, 1, :], -0.5).then_inc(*one(consts))
            pool.wait_ge(pre.h, 16 * N_LOADS)
            nc.gpsimd.tensor_tensor(bias_f[:, :], bias_f[:, :], xb[:, 0, :], ALU.add).then_inc(*one(consts))
            pool.wait_ge(consts.h, 8)
            pool.wait_ge(bt_ev.h, NC * NF)
            with pool.Fori(0, B) as it:
                def after(s, k):
                    return s.h, it * s.per + k

                def bank_full(key):
                    return after(full[bank_of[key]], use_of[key] + 1)

                def rsqrt(ready, var, dst, lo, hi):
                    pool.wait_ge(*ready)
                    r = rstd[:, dst, lo:hi]
                    nc.gpsimd.tensor_tensor(r, var[:, lo:hi], power[:, 0, lo:hi], ALU.add).then_inc(*one(rs_step))
                    pool.wait_ge(*after(rs_step, rs_step.made))
                    nc.gpsimd.tensor_tensor(r, r, power[:, 1, lo:hi], ALU.pow).then_inc(*one(rs_ready))

                def norm_half(layer, hf):
                    rsqrt(after(lns, layer * 2 * NT + NT * (hf + 1)), mv[:, :, 1], 0, 2 * hf, 2 * hf + 2)

                norm_half(0, 0)
                norm_half(0, 1)
                for c in range(NC):
                    pool.wait_ge(*after(zt_ready, 2))
                    nc.gpsimd.tensor_tensor(delta[:, c, :], zt[:, c, 0:T], zt[:, c, 1:T + 1],
                                            ALU.subtract).then_inc(*one(delta_ready))
                for a, n in enumerate(MIX_ORDER):
                    for c in range(NC):
                        pool.wait_ge(*after(mixd_ready, a * NC + c + 1))
                        nc.gpsimd.tensor_tensor(mix[:, a % 3, c, :], mix[:, a % 3, c, :], zt[:, c, 1:T + 1],
                                                ALU.add).then_inc(*one(mix_ready))
                    if n == 1:
                        for lv in range(1, 8):
                            if lv == 1:
                                pool.wait_ge(*after(dec_ready, H))
                            else:
                                pool.wait_ge(*after(tree_ready, lv - 1))
                            pairs = dblk[lv - 1].rearrange("p h (m two) -> p h m two", two=2)
                            nc.gpsimd.tensor_tensor(dblk[lv], pairs[:, :, :, 0], pairs[:, :, :, 1],
                                                    ALU.mult).then_inc(*one(tree_ready))
                for h in range(H):
                    pool.wait_ge(*after(qf_ready, h + 1))
                    pool.sem_inc(pool_gate.h, 1)
                    nc.gpsimd.tensor_scalar(qu[:, h, :], qf[:, h, :], col("bonus", h), None,
                                            ALU.mult).then_inc(*one(qu_ready))
                pool.wait_ge(*after(tree_ready, 7))
                for lv in range(1, 8):
                    s = LEVELS[lv]
                    for h in range(H):
                        pool.wait_ge(*bank_full(("A", lv, h)))
                        if lv > 1:
                            pool.wait_ge(*after(kg_level, (lv - 2) * H + h + 1))
                        kv = kg[:, h, :].rearrange("p (m two s) -> p m two s", two=2, s=s)[:, :, 0, :]
                        dv = dblk[lv - 1][:, h, :].rearrange("p (m two) -> p m two", two=2)[:, :, 1]
                        nc.gpsimd.tensor_tensor(kv, kv, dv.unsqueeze(2).to_broadcast([P, T // (2 * s), s]),
                                                ALU.mult).then_inc(*one(kg_level))
                rsqrt(after(gstat, 2 * NT), mv[:, :, 1], 0, 0, NT)
                for c in range(NC):
                    pool.wait_ge(*after(oaff_ready, c + 1))
                    pool.wait_ge(*after(gate_ready, c + 1))
                    nc.gpsimd.tensor_tensor(ogate[:, c, :], ogate[:, c, :], gate[:, c, :],
                                            ALU.mult).then_inc(*one(og_ready))

                def plus(out_, a_, bias):
                    return nc.gpsimd.tensor_tensor(out_, a_, bias[:, :].unsqueeze(1).to_broadcast([P, NT, D]),
                                                   ALU.add)

                norm_half(1, 0)
                norm_half(1, 1)
                pool.wait_ge(*after(x_ready, 2))
                plus(xb[:, :, :], x[:, :, :], bias_f).then_inc(*one(xb_ready))
                for hf in range(2):
                    norm_half(2, hf)
                    rsqrt(after(lnb, 2 * hf + 2), rstd[:, 1, :], 2, 2 * hf, 2 * hf + 2)
                pool.wait_ge(*after(z_ready, 3 * NT))
                pool.wait_ge(*after(x_ready, 4))
                plus(xb[:, :, :], z[:, :, :], bias_o).then_inc(*one(xb_ready))
                for t in range(NG):
                    for i, src in enumerate((qp, kp)):
                        pool.wait_ge(*after(qp_ready, 2 * t + i + 1))
                        if t >= 2:
                            pool.wait_ge(*bank_full(("S", t - 2, HG - 1, 2)))
                        pool.sem_inc(pool_gate.h, 1)
                        nc.gpsimd.tensor_copy(rqk[:, t % 2, i, :], src[:, t, :]).then_inc(*one(rqk_ready))
                norm_half(3, 0)
                norm_half(3, 1)
                pool.wait_ge(*after(x2_ready, 2))
                nc.gpsimd.tensor_tensor(xb[:, :, :], x[:, :, :], x2[:, :, :], ALU.add).then_inc(*one(xs_step))
                pool.wait_ge(*after(xs_step, 1))
                plus(xb[:, :, :], xb[:, :, :], bias_m).then_inc(*one(xb_ready))
                norm_half(4, 0)
                norm_half(4, 1)
                pool.wait_ge(*after(x_ready, 6))
                plus(xb[:, :, :], x[:, :, :], bias_f).then_inc(*one(xb_ready))

        @block.scalar
        def _(act):
            with act.Fori(0, NF) as t:
                act.wait_ge(bl_cols.h, t + 1)
                for s in range(LOW):
                    n = t * (2 * LOW) + 2 * s
                    act.wait_ge(bl_mat.h, n + 1)
                    nc.scalar.activation(diag[:, (2 * s) % 4, :], ident[:, :], ACT.Copy,
                                         scale=bcol[:, 0, 0, s:s + 1]).then_inc(bl_diag.h, 1)
                    act.wait_ge(bl_mat.h, n + 2)
                    nc.scalar.activation(diag[:, (2 * s + 1) % 4, :], ident[:, :], ACT.Copy,
                                         scale=bcol[:, 0, 1, LOW - 1 - s:LOW - s]).then_inc(bl_diag.h, 1)
                    act.wait_ge(bl_mm[0].h, t * LOW + s + 1)
                    if s < LOW - 1:
                        nc.scalar.activation(y_st[0][:, (s + 1) % 2, :], ring[s % 2][:, 0:UW],
                                             ACT.Copy).then_inc(bl_ev[0].h, 1)
                    else:
                        nc.scalar.activation(y_up[:, bass.ds(t, 1), :], ring[s % 2][:, 0:UW].unsqueeze(1),
                                             ACT.Copy).then_inc(bl_ev[0].h, 1)
            for m in range(NF):
                for c in range(NC):
                    n = m * NC + c
                    act.wait_ge(bt_mm.h, n + 1)
                    nc.scalar.activation(wup[:, c, m * P:(m + 1) * P], ring[n % 4][:, 0:P],
                                         ACT.Copy).then_inc(*one(bt_ev))
            act.wait_ge(pre.h, 16 * N_LOADS)
            with act.Fori(0, B) as it:
                def after(s, k):
                    return s.h, it * s.per + k

                def bank_full(key):
                    return after(full[bank_of[key]], use_of[key] + 1)

                def bank(key):
                    return ring[bank_of[key]]

                def turned(tag, hf, scale=None, bias=None):
                    key = ("zt", tag, hf)
                    act.wait_ge(*bank_full(key))
                    ps = bank(key)[:, :].rearrange("p (c t) -> p c t", c=NC)
                    dst = zt[:, :, 1 + hf * HT:1 + (hf + 1) * HT]
                    if scale is None:
                        ins = nc.scalar.activation(dst, ps, ACT.Copy)
                    else:
                        for c in range(NC):
                            ins = nc.scalar.activation(dst[:, c, :], ps[:, c, :], ACT.Identity,
                                                       scale=col(scale, c), bias=col(bias, c))
                    ins.then_inc(*one(zt_ready))

                def evac(key, dst, done, func=ACT.Copy, rows=P, **kw):
                    act.wait_ge(*bank_full(key))
                    nc.scalar.activation(dst, bank(key)[0:rows, :], func, **kw).then_inc(*one(done))

                turned("A", 0)
                turned("A", 1)
                evac(("xl", 0), xl0[:, :], xl_ready, ACT.Tanh)
                evac(("xl", 1), xl1[:, :], xl_ready, ACT.Tanh, rows=RMIX)
                evac(("wa",), wat[:, :], wa_ready, ACT.Tanh, rows=LR)
                for h in range(H):
                    evac(("w", h), dec[:, h, :], ew_ready, ACT.Exp, bias=col("w_b", h))
                    act.wait_ge(*after(ew_ready, h + 1))
                    nc.scalar.activation(dec[:, h, :], dec[:, h, :], ACT.Exp, scale=-1.0).then_inc(*one(dec_ready))
                for h in range(H):
                    evac(("k", h), kg[:, h, :], kg_ready)
                for h in range(H):
                    evac(("r", h), qf[:, h, :], qf_ready)
                for t in range(2):
                    evac(("v", t), v[:, 2 * t:2 * t + 2, :].rearrange("p a b -> p (a b)"), v_ready)
                evac(("ga",), gat[0:LR, :], ga_ready, ACT.Tanh, rows=LR)
                for c in range(NC):
                    act.wait_ge(*bank_full(("g", c)))
                    nc.scalar.activation(gtanh[:, c, :], bank(("g", c))[:, :], ACT.Tanh,
                                         scale=0.5).then_inc(*one(gt_ready))
                for h in range(H):
                    act.wait_ge(*bank_full(("kt", h)))
                    nc.scalar.activation(kt[:, h, 0:NT - 1, :],
                                         bank(("kt", h))[:, 0:(NT - 1) * P].rearrange("p (c k) -> p c k", k=P),
                                         ACT.Copy).then_inc(*one(kt_ready))
                for c in range(NC):
                    evac(("ogt", c), ogate[:, c, :], oaff_ready, ACT.Identity, scale=col("gn_w", c),
                         bias=col("gn_b", c))

                def ffn_half(tag, hf, bias, *affine):
                    turned(tag, hf, *affine)
                    for m2 in range(NF // 2):
                        key = ("up", tag, hf, m2)
                        act.wait_ge(*bank_full(key))
                        for a in range(2):
                            m = 2 * m2 + a
                            ins = nc.scalar.activation(gelu[:, m, hf * HT:(hf + 1) * HT],
                                                       bank(key)[:, a * HT:(a + 1) * HT], ACT.Gelu, bias=bias(m))
                        ins.then_inc(*one(gelu_ready))

                for hf in range(2):
                    ffn_half("F", hf, lambda m: upb[:, m:m + 1])
                for hf in range(2):
                    act.wait_ge(*after(rs_ready, 7 + 2 * hf))
                    for t in (2 * hf, 2 * hf + 1):
                        act.wait_ge(*after(z_ready, 2 * NT + t + 1))
                        nc.scalar.activation(z2[:, t, :], z[:, t, :], ACT.Copy,
                                             scale=rstd[:, 2, t:t + 1]).then_inc(*one(z2_ready))
                    turned("B", hf, "ln1_g", "ln1_b")
                for t in range(NG):
                    evac(("qf", t), qp[:, t, :], qp_ready)
                    evac(("kf", t), kp[:, t, :], qp_ready, ACT.Identity, bias=col("minus_row"))

                def weighted(t):
                    act.wait_ge(*after(pt_used, HG * (t + 1)))
                    if t >= 2:
                        act.wait_ge(*after(attn_ready, t - 1))
                    nc.scalar.activation(osum[:, t % 2, :], obank[t % 2][:, :], ACT.Copy) \
                        .then_inc(*one(osum_ready))

                for t in range(NG):
                    for g in range(HG):
                        n = t * HG + g
                        if n >= NPT:
                            act.wait_ge(*after(pt_used, n - NPT + 1))
                        for i, (lo, hi) in enumerate(((0, 512), (512, 1024), (1024, 1280))):
                            key = ("ST", t, g, i)
                            act.wait_ge(*bank_full(key))
                            nc.scalar.activation(pt[:, n % NPT, lo:hi], bank(key)[:, 0:hi - lo], ACT.Exp,
                                                 scale=HD ** -0.5).then_inc(*one(pt_ready))
                        if g == 0 and t >= 1:
                            weighted(t - 1)
                weighted(NG - 1)
                for hf in range(2):
                    ffn_half("M", hf, lambda m: col("b1", m), "ln2_g", "ln2_b")
                for hf in range(2):
                    ffn_half("G", hf, lambda m: upb[:, m:m + 1])

        @block.vector
        def _(dve):
            for i in range(3):
                dve.sem_inc(bl_mat.h, 1)
            dve.wait_ge(wload.h, 16 * N_SMALL)
            nc.vector.tensor_copy(masks[:, :, :].rearrange("p s n -> p (s n)"), masks_in).then_inc(*one(seeded))
            high = [0]

            def high_stage(src, dst, width, which, kind, s):
                m = 1 << (s - LOW)
                for t in range(NF):
                    if high[0] >= 1:
                        dve.wait_ge(bh_s.h, high[0])
                    high[0] += 1
                    nc.vector.tensor_scalar(tmp_h[:, 0:width], src[:, t, 0:width], bw[:, 0, which, t, s:s + 1], None,
                                            ALU.mult).then_inc(bh_t.h, 1)
                    dve.wait_ge(bh_t.h, high[0])
                    nc.vector.scalar_tensor_tensor(out=dst[:, t, 0:width], in0=src[:, t ^ m, 0:width],
                                                   scalar=bw[:, kind, which, t, s:s + 1], in1=tmp_h[:, 0:width],
                                                   op0=ALU.mult, op1=ALU.add).then_inc(bh_s.h, 1)

            dn_tmp = y_up
            dn_cur = y_dn
            for s in range(STAGES - 1, LOW - 1, -1):
                nxt = {STAGES - 1: dn_tmp, STAGES - 2: y_dn, LOW: bdn}[s]
                if s == LOW:
                    dve.wait_ge(consts.h, 2)
                high_stage(dn_cur, nxt, D, 1, 2, s)
                dn_cur = nxt
            dve.wait_ge(bh_s.h, high[0])
            HDN = high[0]
            dve.sem_inc(bl_ev[0].h, 1)
            with dve.Fori(0, NF) as t:
                nc.vector.tensor_copy(bcol.rearrange("p k w s -> p (k w) s"),
                                      bw.rearrange("p k w t s -> p (k w) t s")[:, :, bass.ds(t, 1), :]
                                      .rearrange("p k t s -> p k (t s)")).then_inc(bl_cols.h, 1)
                dve.wait_ge(bl_cols.h, t + 1)
                for s in range(LOW):
                    for w in range(2):
                        n = 2 * s + w
                        st = s if w == 0 else LOW - 1 - s
                        dve.wait_ge(bl_diag.h, t * 2 * LOW + n + 1)
                        if w == 0:
                            if s >= 2:
                                dve.wait_ge(bl_mm[0].h, t * LOW + s - 1)
                        nc.vector.scalar_tensor_tensor(out=bmat[:, n % 4, :], in0=perm[:, st, :],
                                                       scalar=bcol[:, 2 if w == 0 else 1, w, st:st + 1],
                                                       in1=diag[:, n % 4, :], op0=ALU.mult,
                                                       op1=ALU.add).then_inc(bl_mat.h, 1)
                    dve.wait_ge(bl_mm[1].h, t * LOW + s + 1)
                    if s < LOW - 1:
                        nc.vector.tensor_copy(y_st[1][:, (s + 1) % 2, :],
                                              ring[2 + s % 2][:, 0:D]).then_inc(bl_ev[1].h, 1)
                    else:
                        nc.vector.tensor_copy(wdn[:, bass.ds(t, 1), :],
                                              ring[2 + s % 2][:, 0:D].unsqueeze(1)).then_inc(bl_ev[1].h, 1)
            dve.wait_ge(bl_ev[0].h, NF * LOW + 1)
            high_stage(y_up, y_up2, UW, 0, 1, LOW)
            high_stage(y_up2, y_up, UW, 0, 1, LOW + 1)
            high_stage(y_up, y_up2, UW, 0, 1, LOW + 2)
            dve.wait_ge(bh_s.h, high[0])
            for m in range(NF):
                ins = nc.vector.tensor_tensor(upb[:, m:m + 1], y_up2[:, m, D:UW], col("up_b", m), ALU.add)
            ins.then_inc(*one(seeded))
            dve.wait_ge(bt_ev.h, NC * NF)
            dve.wait_ge(consts.h, 8)
            dve.wait_ge(pre.h, 16 * N_LOADS)

            with dve.Fori(0, B) as it:
                def after(s, k):
                    return s.h, it * s.per + k

                def bank_full(key):
                    return after(full[bank_of[key]], use_of[key] + 1)

                def bank(key):
                    return ring[bank_of[key]]

                def norm_half(layer, hf, src, ready):
                    base = layer * 2 * NT + hf * NT
                    tiles = (2 * hf, 2 * hf + 1)
                    dve.wait_ge(*ready)
                    for t in tiles:
                        nc.vector.bn_stats(stats[:, t, :], src[:, t, :]).then_inc(*one(lns))
                    dve.wait_ge(*after(lns, base + 2))
                    dve.sem_inc(gating.h, 1)
                    for t in tiles:
                        nc.vector.bn_aggr(mv[:, t, :], stats[:, t, :]).then_inc(*one(lns))
                    dve.wait_ge(*after(rs_ready, (1, 4, 6, 10, 12)[layer] + hf * (2 if layer == 2 else 1)))
                    for t in tiles:
                        nc.vector.tensor_scalar(z[:, t, :], src[:, t, :], mv[:, t, 0:1], rstd[:, 0, t:t + 1],
                                                ALU.subtract, ALU.mult).then_inc(*one(z_ready))
                    if layer == 2:
                        sl = slice(2 * hf, 2 * hf + 2)
                        nc.vector.tensor_tensor(rstd[:, 1, sl], rstd[:, 0, sl], rstd[:, 0, sl],
                                                ALU.mult).then_inc(*one(lnb))
                        dve.wait_ge(*after(lnb, 2 * hf + 1))
                        nc.vector.tensor_tensor(rstd[:, 1, sl], rstd[:, 1, sl], mv[:, sl, 1],
                                                ALU.mult).then_inc(*one(lnb))

                def add_back(key, t, res, dst, done):
                    dve.wait_ge(*bank_full(key))
                    nc.vector.tensor_tensor(dst[:, 2 * t:2 * t + 2, :].rearrange("p a b -> p (a b)"), bank(key)[:, :],
                                            res[:, 2 * t:2 * t + 2, :].rearrange("p a b -> p (a b)"),
                                            ALU.add).then_inc(*one(done))

                def values(t):
                    dve.wait_ge(*bank_full(("vb", t)))
                    for a in range(2):
                        ins = nc.vector.tensor_tensor(
                            vaug[:, 2 * t + a, :, 0:HD],
                            bank(("vb", t))[:, a * D:(a + 1) * D].rearrange("p (h d) -> p h d", d=HD),
                            bias_v[:, :].rearrange("p (h d) -> p h d", d=HD), ALU.add)
                    ins.then_inc(*one(vaug_ready))

                for hf in range(2):
                    norm_half(0, hf, x, after(x_in, 16))
                for c in range(NC):
                    dve.wait_ge(*after(delta_ready, c + 1))
                    nc.vector.scalar_tensor_tensor(out=mix[:, 2, c, :], in0=delta[:, c, :], scalar=col("mu", c),
                                                   in1=zt[:, c, 1:T + 1], op0=ALU.mult,
                                                   op1=ALU.add).then_inc(*one(mix0_ready))
                for a, n in enumerate(MIX_ORDER):
                    for c in range(NC):
                        key = ("x5", n, c)
                        dve.wait_ge(*bank_full(key))
                        if a == 3:
                            dve.wait_ge(*bank_full(("w", 0)))
                        if a == 4:
                            dve.wait_ge(*bank_full(("k", H - 1)))
                        nc.vector.scalar_tensor_tensor(out=mix[:, a % 3, c, :], in0=bank(key)[:, :],
                                                       scalar=col("xbias", n * NC + c), in1=delta[:, c, :],
                                                       op0=ALU.add, op1=ALU.mult).then_inc(*one(mixd_ready))
                for c in range(NC):
                    dve.wait_ge(*after(gt_ready, c + 1))
                    nc.vector.scalar_tensor_tensor(out=gate[:, c, :], in0=gtanh[:, c, :], scalar=1.0,
                                                   in1=bank(("g", c))[:, :], op0=ALU.add,
                                                   op1=ALU.mult).then_inc(*one(gate_ready))
                dve.wait_ge(*after(tree_ready, 7))
                for lv, s in enumerate(LEVELS):
                    for h in range(H):
                        key = ("A", lv, h)
                        dve.wait_ge(*bank_full(key))
                        if lv >= 1:
                            dve.wait_ge(*after(a_copied, (lv - 1) * H + h + 1))
                        dve.sem_inc(gating.h, 1)
                        nc.vector.copy_predicated(scores[:, h, :, :],
                                                  lmask[:, lv, :].bitcast(U16).unsqueeze(1).to_broadcast([P, NT, P]),
                                                  bank(key)[:, :].rearrange("p (c n) -> p c n", c=NT)) \
                            .then_inc(*one(a_copied))
                        if lv >= 1:
                            if lv > 1:
                                dve.wait_ge(*after(qf_level, (lv - 2) * H + h + 1))
                            qv = qf[:, h, :].rearrange("p (m two s) -> p m two s", two=2, s=s)[:, :, 1, :]
                            dv = dblk[lv - 1][:, h, :].rearrange("p (m two) -> p m two", two=2)[:, :, 0]
                            nc.vector.tensor_tensor(qv, qv, dv.unsqueeze(2).to_broadcast([P, T // (2 * s), s]),
                                                    ALU.mult).then_inc(*one(qf_level))
                for c in range(NT - 1):
                    key = ("s", c)
                    dve.wait_ge(*bank_full(key))
                    if c == 0:
                        nc.vector.tensor_copy(state[:, 0, :, :].rearrange("p h v -> p (h v)"),
                                              bank(key)[:, 0:H * DV]).then_inc(*one(state_ready))
                    else:
                        dve.wait_ge(*after(state_ready, c))
                        for h in range(H):
                            ins = nc.vector.scalar_tensor_tensor(
                                out=state[:, c, h, :], in0=state[:, c - 1, h, :], scalar=dblk[7][:, h, c:c + 1],
                                in1=bank(key)[:, h * DV:(h + 1) * DV], op0=ALU.mult, op1=ALU.add)
                        ins.then_inc(*one(state_ready))
                for t in range(NT):
                    dve.wait_ge(*bank_full(("o", t // 2)))
                    nc.vector.bn_stats(stats[:, t, :], bank(("o", t // 2))[:, (t % 2) * D:(t % 2 + 1) * D]) \
                        .then_inc(*one(gstat))
                dve.wait_ge(*after(gstat, NT))
                dve.sem_inc(gating.h, 1)
                for t in range(NT):
                    nc.vector.bn_aggr(mv[:, t, :], stats[:, t, :]).then_inc(*one(gstat))
                dve.wait_ge(*after(rs_ready, 3))
                for t in range(NT):
                    nc.vector.tensor_scalar(on[:, t, :], bank(("o", t // 2))[:, (t % 2) * D:(t % 2 + 1) * D],
                                            mv[:, t, 0:1], rstd[:, 0, t:t + 1], ALU.subtract,
                                            ALU.mult).then_inc(*one(on_ready))
                for t in range(2):
                    key = ("ao", t)
                    dve.wait_ge(*bank_full(key))
                    xv = x[:, 2 * t:2 * t + 2, :].rearrange("p a b -> p (a b)")
                    nc.vector.scalar_tensor_tensor(out=xv, in0=bank(key)[:, :], scalar=0.5, in1=xv, op0=ALU.mult,
                                                   op1=ALU.add).then_inc(*one(x_ready))
                    norm_half(1, t, x, after(x_ready, t + 1))

                dve.wait_ge(*after(xb_ready, 1))
                for t in range(2):
                    add_back(("dn", "F", t), t, xb, x, x_ready)
                    norm_half(2, t, x, after(x_ready, 2 + t + 1))
                values(0)
                for t in range(NG):
                    for i, (name, b) in enumerate((("q", "bq"), ("kk", "bk"))):
                        n = 2 * t + i
                        dve.wait_ge(*bank_full((name, t)))
                        if n == 0:
                            dve.wait_ge(*after(zt_ready, 6))
                        if n >= 4:
                            dve.wait_ge(*bank_full(("qf" if i == 0 else "kf", t - 2)))
                        nc.vector.scalar_tensor_tensor(out=qh[:, n % 4, :], in0=bank((name, t))[:, :],
                                                       scalar=col(b, t), in1=rope[:, :], op0=ALU.add,
                                                       op1=ALU.mult).then_inc(*one(qh_ready))
                values(1)

                def row_max(t, g):
                    c = 32 * g + HD
                    n = (t * HG + g) * 4
                    if t >= 2 and g == 0:
                        dve.wait_ge(*bank_full(("mt", t - 2)))
                    for i, (qt, lo, hi) in enumerate(((3, 0, 512), (2, 0, 384), (0, 384, 512), (1, 0, 256))):
                        b = (0, 1, 1, 2)[i]
                        key = ("S", t, g, b)
                        dve.wait_ge(*bank_full(key))
                        nc.vector.tensor_reduce(maxes[:, t % 2, qt, c:c + 1], bank(key)[:, lo:hi], AX_X,
                                                ALU.max).then_inc(*one(maxs))

                def normalised(t):
                    dve.wait_ge(*bank_full(("den", t)))
                    if t >= 2:
                        dve.wait_ge(*after(attn_ready, t - 1))
                    nc.vector.reciprocal(rden[:, t % 2, :], bank(("den", t))[:, :]).then_inc(*one(rden_ready))
                    dve.wait_ge(*after(rden_ready, t + 1))
                    nc.vector.tensor_tensor(attn_t[:, t, :], osum[:, t % 2, :], rden[:, t % 2, :], ALU.mult) \
                        .then_inc(*one(attn_ready))

                def shift(t):
                    dve.wait_ge(*bank_full(("mt", t)))
                    nc.vector.tensor_tensor(qp[:, t, :], bank(("mt", t))[:, :], qp[:, t, :],
                                            ALU.add).then_inc(*one(qm_ready))

                for g in range(HG):
                    row_max(0, g)
                shift(0)
                for t in range(NG):
                    for g in range(HG):
                        if t + 1 < NG:
                            for a in AHEAD[g]:
                                row_max(t + 1, a)
                        if g == 1 and t >= 1:
                            normalised(t - 1)
                        if g == HG - 1 and t + 1 < NG:
                            shift(t + 1)
                normalised(NG - 1)
                dve.wait_ge(*after(xb_ready, 2))
                for t in range(2):
                    add_back(("wo", t), t, xb, x2, x2_ready)
                    norm_half(3, t, x2, after(x2_ready, t + 1))
                dve.wait_ge(*after(xb_ready, 3))
                for t in range(2):
                    add_back(("dn", "M", t), t, xb, x, x_ready)
                    norm_half(4, t, x, after(x_ready, 4 + t + 1))
                dve.wait_ge(*after(xb_ready, 4))
                for t in range(2):
                    add_back(("dn", "G", t), t, xb, x, x_ready)

        @block.tensor
        def _(pe):
            mm = nc.tensor.matmul
            with pe.Fori(0, NF) as t:
                for s in range(LOW):
                    pe.wait_ge(bl_mat.h, t * 2 * LOW + 2 * s + 3 + 1)
                    if s == 0:
                        pe.wait_ge(bl_in.h, t * 16 + 16)
                    pe.wait_ge(bl_ev[0].h, t * LOW + s + 1)
                    mm(ring[s % 2][:, 0:UW], bmat[:, (2 * s) % 4, :], y_st[0][:, s % 2, :], start=True,
                       stop=True).then_inc(bl_mm[0].h, 1)
                    pe.wait_ge(bl_mat.h, t * 2 * LOW + 2 * s + 3 + 2)
                    if s:
                        pe.wait_ge(bl_ev[1].h, t * LOW + s)
                        src = y_st[1][:, s % 2, :]
                    else:
                        src = bdn[:, bass.ds(t, 1), :].rearrange("p a n -> p (a n)")
                    mm(ring[2 + s % 2][:, 0:D], bmat[:, (2 * s + 1) % 4, :], src, start=True,
                       stop=True).then_inc(bl_mm[1].h, 1)
            pe.wait_ge(bh_s.h, 2 * 3 * NF)
            for m in range(NF):
                for c in range(NC):
                    n = m * NC + c
                    if n >= 4:
                        pe.wait_ge(bt_ev.h, n - 3)
                    nc.tensor.transpose(ring[n % 4][:, 0:P], y_up2[:, m, c * P:(c + 1) * P],
                                        ident[:, :]).then_inc(*one(bt_mm))
            pe.wait_ge(seeded.h, 2)
            pe.wait_ge(pre.h, 16 * N_LOADS)
            pe.wait_ge(consts.h, 8)

            with pe.Fori(0, B) as it:
                def after(s, k):
                    return s.h, it * s.per + k

                count = [0]

                def take(key):
                    assert order[count[0]] == key, (order[count[0]], key)
                    count[0] += 1
                    if count[0] > RING:
                        pe.wait_ge(*after(*copied(order[count[0] - 1 - RING])))
                    return ring[bank_of[key]]

                def filled(key):
                    return one(full[bank_of[key]])

                def turn(tag, hf, src, ready):
                    ps = take(("zt", tag, hf))
                    for a in range(2):
                        t = 2 * hf + a
                        pe.wait_ge(*ready(t))
                        for c in range(NC):
                            ins = nc.tensor.transpose(ps[:, c * HT + a * P:c * HT + (a + 1) * P],
                                                      src[:, t, c * P:(c + 1) * P], ident[:, :])
                    ins.then_inc(*filled(("zt", tag, hf)))

                def dense(key, w, lo, hi, src, rows=P):
                    ps = take(key)
                    for c in range(NC):
                        ins = mm(ps[0:hi - lo, :], w[:, c, lo:hi], src[:, c, :], start=(c == 0), stop=(c == NC - 1))
                    ins.then_inc(*filled(key))

                def dense_rows(keys, src, w, nk):
                    for key in keys:
                        t2 = key[-1]
                        ps = take(key)
                        for t in range(2):
                            tok = (2 * t2 + t) * P
                            for c in range(nk):
                                ins = mm(ps[:, t * D:(t + 1) * D], src[:, c, tok:tok + P], w[:, c, :],
                                         start=(c == 0), stop=(c == nk - 1))
                        ins.then_inc(*filled(key))

                turn("A", 0, z, lambda t: after(z_ready, t + 1))
                turn("A", 1, z, lambda t: after(z_ready, t + 1))
                for i in range(2):
                    if i == 0:
                        pe.wait_ge(*after(mix0_ready, NC))
                    dense(("xl", i), w1, i * P, P + i * RMIX, mix[:, 2])

                def low_rank(a, n):
                    pe.wait_ge(*after(xl_ready, 1 if n < 4 else 2))
                    for c in range(NC):
                        ps = take(("x5", n, c))
                        if n < 4:
                            ins = mm(ps[:, :], w2a[32 * n:32 * n + 32, c * P:(c + 1) * P], xl0[32 * n:32 * n + 32, :],
                                     start=True, stop=True)
                        else:
                            ins = mm(ps[:, :], w2b[:, c * P:(c + 1) * P], xl1[:, :], start=True, stop=True)
                        ins.then_inc(*filled(("x5", n, c)))

                def project(a, n):
                    pe.wait_ge(*after(mix_ready, (a + 1) * NC))
                    src = mix[:, a % 3]
                    if n == 1:
                        dense(("wa",), wwa, 0, LR, src)
                        pe.wait_ge(*after(wa_ready, 1))
                        for h in range(H):
                            ps = take(("w", h))
                            mm(ps[:, :], wwb[:, h * DK:(h + 1) * DK], wat[:, :], start=True, stop=True) \
                                .then_inc(*filled(("w", h)))
                    elif n == 2:
                        for h in range(H):
                            dense(("k", h), wk, h * DK, (h + 1) * DK, src)
                    elif n == 0:
                        for h in range(H):
                            dense(("r", h), wr, h * DK, (h + 1) * DK, src)
                    elif n == 3:
                        dense_rows([("v", t) for t in range(2)], src, wv, NC)
                    else:
                        dense(("ga",), wga, 0, LR, src)
                        pe.wait_ge(*after(ga_ready, 1))
                        for c in range(NC):
                            ps = take(("g", c))
                            mm(ps[:, :], wgb[:, c * P:(c + 1) * P], gat[:, :], start=True, stop=True) \
                                .then_inc(*filled(("g", c)))

                for a, n in enumerate(MIX_ORDER):
                    low_rank(a, n)
                    if a >= 1:
                        project(a - 1, MIX_ORDER[a - 1])
                project(NMIX - 1, MIX_ORDER[-1])

                for lv in range(len(LEVELS)):
                    for h in range(H):
                        if lv == 0:
                            pe.wait_ge(*after(kg_ready, h + 1))
                            pe.wait_ge(*after(qu_ready, h + 1))
                        if lv >= 2:
                            pe.wait_ge(*after(kg_level, (lv - 2) * H + h + 1))
                            pe.wait_ge(*after(qf_level, (lv - 2) * H + h + 1))
                        ps = take(("A", lv, h))
                        q = qu if lv == 0 else qf
                        for c in range(NT):
                            tok = slice(c * P, (c + 1) * P)
                            ins = mm(ps[:, tok], kg[:, h, tok], q[:, h, tok], start=True, stop=True)
                        ins.then_inc(*filled(("A", lv, h)))
                for h in range(H):
                    pe.wait_ge(*after(kg_level, 6 * H + h + 1))
                    ps = take(("kt", h))
                    for c in range(NT - 1):
                        ins = nc.tensor.transpose(ps[:, c * P:(c + 1) * P], kg[:, h, c * P:(c + 1) * P], ident[:, :])
                    ins.then_inc(*filled(("kt", h)))
                pe.wait_ge(*after(v_ready, 2))
                for c in range(NT - 1):
                    ps = take(("s", c))
                    for h in range(H):
                        if c == 0:
                            pe.wait_ge(*after(kt_ready, h + 1))
                        ins = mm(ps[:, h * DV:(h + 1) * DV], kt[:, h, c, :], v[:, c, h * DV:(h + 1) * DV],
                                 start=True, stop=True)
                    ins.then_inc(*filled(("s", c)))
                pe.wait_ge(*after(a_copied, len(LEVELS) * H))
                pe.wait_ge(*after(qf_level, 7 * H))
                for c in range(NT):
                    if c % 2 == 0:
                        ps = take(("o", c // 2))
                    if c >= 1:
                        pe.wait_ge(*after(state_ready, c))
                    for h in range(H):
                        dst = ps[:, (c % 2) * D + h * DV:(c % 2) * D + (h + 1) * DV]
                        ins = mm(dst, scores[:, h, c, :], v[:, c, h * DV:(h + 1) * DV], start=True, stop=(c == 0))
                        if c >= 1:
                            ins = mm(dst, qf[:, h, c * P:(c + 1) * P], state[:, c - 1, h, :], start=False, stop=True)
                    if c % 2:
                        ins.then_inc(*filled(("o", c // 2)))
                for c in range(NC):
                    ps = take(("ogt", c))
                    for t in range(NT):
                        if c == 0:
                            pe.wait_ge(*after(on_ready, t + 1))
                        ins = nc.tensor.transpose(ps[:, t * P:(t + 1) * P], on[:, t, c * P:(c + 1) * P], ident[:, :])
                    ins.then_inc(*filled(("ogt", c)))
                pe.wait_ge(*after(og_ready, NC))
                dense_rows([("ao", t) for t in range(2)], ogate, wo, NC)

                def ffn(tag, src, layer, wu, wd):
                    for hf in range(2):
                        turn(tag, hf, src, lambda t: after(z_ready, layer * NT + t + 1))
                        pe.wait_ge(*after(zt_ready, 2 * layer + hf + 1))
                        for m2 in range(NF // 2):
                            ps = take(("up", tag, hf, m2))
                            for a in range(2):
                                m = 2 * m2 + a
                                for c in range(NC):
                                    ins = mm(ps[:, a * HT:(a + 1) * HT], wu[:, c, m * P:(m + 1) * P],
                                             zt[:, c, 1 + hf * HT:1 + (hf + 1) * HT], start=(c == 0),
                                             stop=(c == NC - 1))
                            ins.then_inc(*filled(("up", tag, hf, m2)))
                    for t in range(2):
                        pe.wait_ge(*after(gelu_ready, "FMG".index(tag) * NF + (t + 1) * (NF // 2)))
                        dense_rows([("dn", tag, t)], gelu, wd, NF)

                ffn("F", z, 1, wup, wdn)

                turn("B", 0, z2, lambda t: after(z2_ready, t + 1))
                pe.wait_ge(*after(zt_ready, 5))
                dense_rows([("vb", 0)], zt[:, :, 1:T + 1], wv_b, NC)
                turn("B", 1, z2, lambda t: after(z2_ready, t + 1))
                pe.wait_ge(*after(zt_ready, 6))
                nrm = zt[:, :, 1:T + 1]
                dense(("q", 0), wq_b, 0, P, nrm)
                dense(("kk", 0), wk_b, 0, P, nrm)
                for t in range(NG):
                    if t + 1 < NG:
                        dense(("q", t + 1), wq_b, (t + 1) * P, (t + 2) * P, nrm)
                        dense(("kk", t + 1), wk_b, (t + 1) * P, (t + 2) * P, nrm)
                    for i, name in enumerate(("qf", "kf")):
                        pe.wait_ge(*after(qh_ready, 2 * t + i + 1))
                        ps = take((name, t))
                        mm(ps[:, :], fold[:, :], qh[:, (2 * t + i) % 4, :], start=True, stop=True) \
                            .then_inc(*filled((name, t)))
                dense_rows([("vb", 1)], nrm, wv_b, NC)

                def s_max(t, g):
                    r = slice(32 * g, 32 * g + 32)
                    if g == 0:
                        pe.wait_ge(*after(rqk_ready, 2 * t + 2))
                    banks = [take(("S", t, g, b)) for b in range(3)]
                    parts = ((0, 3, 0), (1, 2, 0), (1, 0, 384), (2, 1, 0))
                    for b, qt, lo in parts:
                        n = (qt + 1) * P
                        mm(banks[b][:, lo:lo + n], rqk[r, t % 2, 0, qt * P:(qt + 1) * P], rqk[r, t % 2, 1, 0:n],
                           start=(lo == 0), stop=False)
                    for b, qt, lo in parts:
                        n = (qt + 1) * P
                        ins = mm(banks[b][:, lo + n - P:lo + n], identb, future, start=False, stop=(b, qt) != (1, 2))
                        if (b, qt) != (1, 2):
                            ins.then_inc(*filled(("S", t, g, b)))

                def s_exp(t, g):
                    r = slice(32 * g, 32 * g + 32)
                    banks = [take(("ST", t, g, b)) for b in range(3)]
                    parts = ((0, 0, 0), (1, 1, 0), (1, 3, 384), (2, 2, 0))
                    for b, jt, lo in parts:
                        n = T - jt * P
                        mm(banks[b][:, lo:lo + n], kp[r, t, jt * P:(jt + 1) * P], qp[r, t, jt * P:T],
                           start=(lo == 0), stop=False)
                    for b, jt, lo in parts:
                        ins = mm(banks[b][:, lo:lo + P], identb, future_t, start=False, stop=(b, jt) != (1, 1))
                        if (b, jt) != (1, 1):
                            ins.then_inc(*filled(("ST", t, g, b)))

                def pv(t, g):
                    n = t * HG + g
                    if g == 0 and t >= 2:
                        pe.wait_ge(*after(osum_ready, t - 1))
                    pe.wait_ge(*after(pt_ready, 3 * n + 3))
                    base = {0: 0, 1: 512, 3: 896, 2: 1024}
                    for jt in range(NT):
                        ins = mm(obank[t % 2][32 * g:32 * g + 32, jt * P:T], vaug[:, jt, n, :],
                                 pt[:, n % NPT, base[jt]:base[jt] + T - jt * P], start=(jt == 0), stop=(jt == NT - 1))
                    ins.then_inc(*one(pt_used))

                def spread_sums(t):
                    pe.wait_ge(*after(osum_ready, t + 1))
                    ps = take(("den", t))
                    mm(ps[:, :], den_row[:, :], osum[:, t % 2, :], start=True, stop=True) \
                        .then_inc(*filled(("den", t)))

                def turn_maxima(t):
                    pe.wait_ge(*after(maxs, 4 * HG * (t + 1)))
                    ps = take(("mt", t))
                    for qt in range(NT):
                        ins = nc.tensor.transpose(ps[:, qt * P:(qt + 1) * P], maxes[:, t % 2, qt, :], ident[:, :])
                    ins.then_inc(*filled(("mt", t)))

                for g in range(HG):
                    s_max(0, g)
                turn_maxima(0)
                pe.wait_ge(*after(vaug_ready, 2))
                for t in range(NG):
                    for g in range(HG):
                        if t + 1 < NG:
                            for a in AHEAD[g]:
                                s_max(t + 1, a)
                        if g == 0:
                            pe.wait_ge(*after(qm_ready, t + 1))
                        s_exp(t, g)
                        if g == 1 and t >= 1:
                            spread_sums(t - 1)
                        if g == HG - 1 and t + 1 < NG:
                            turn_maxima(t + 1)
                        if g >= 1:
                            pv(t, g - 1)
                        elif t >= 1:
                            pv(t - 1, HG - 1)
                pv(NG - 1, HG - 1)
                spread_sums(NG - 1)
                pe.wait_ge(*after(attn_ready, NG))
                dense_rows([("wo", t) for t in range(2)], attn_t, wo_b, NG)
                ffn("M", z, 3, wm1, wm2)
                ffn("G", z, 4, wup, wdn)
                assert count[0] == len(order)

        for s in sems:
            assert not s.per or s.made in (s.per, 0), (s.name, s.per, s.made)


def layouts(i):
    def c(a):
        return np.ascontiguousarray(a)

    def tiles(a, n):
        return a.reshape(n, P).T

    A, Bk, Fn = "L0_attn_a_", "L0_attn_b_", "L0_ffn_"
    i = {k: np.asarray(v) for k, v in i.items()}
    f = np.float32
    o = {"x": i[A + "hidden_states"]}
    o["w1"] = c(i[A + "xp_W1"].T)
    o["w2"] = c(i[A + "xp_W2"].T)
    o["wr"], o["wk"], o["wv"] = c(i[A + "r_W"].T), c(i[A + "k_W"].T), c(i[A + "v_W"].T)
    o["wwa"], o["wwb"] = c(i[A + "w_A"].T), c(i[A + "w_B"].T)
    o["wga"] = c(i[A + "g_A"].T)
    o["wgb"] = c(np.concatenate([i[A + "g_B"].T, i[A + "g_b"][None, :]], 0))
    o["wo"] = c(i[A + "o_W"].T)
    src = np.array([h * HD + d if r == 0 else h * HD + (d + HD // 2) % HD
                    for h in range(NH) for r in range(2) for d in range(HD)])
    W, bb = i[Bk + "Wqkv"], i[Bk + "bqkv"]
    o["wq_b"], o["wk_b"], o["wv_b"] = c(W[:, src]), c(W[:, D + src]), c(W[:, 2 * D:3 * D])
    o["bv"], o["bo"], o["b2"] = c(bb[2 * D:3 * D]), i[Bk + "bo"], i[Bk + "b2"]
    o["wm1"], o["wm2"] = i[Bk + "W1"], i[Bk + "W2"]
    o["wo_b"] = np.zeros((NH, 2 * HD, D), f)
    o["wo_b"][:, :HD] = i[Bk + "Wo"].reshape(NH, HD, D)
    o["wo_b"] = o["wo_b"].reshape(NG * P, D)
    minus = np.zeros((P, 1), f)
    minus[HD::32] = -1.0
    o["cols"] = c(np.concatenate([
        tiles(i[A + "xp_mu"], NC), tiles(i[A + "x_bias"], NMIX * NC), tiles(i[A + "w_b"], H), i[A + "bonus"].T,
        tiles(i[A + "gn_w"], NC), tiles(i[A + "gn_b"], NC), tiles(i[Bk + "ln1_g"], NC), tiles(i[Bk + "ln1_b"], NC),
        tiles(i[Bk + "ln2_g"], NC), tiles(i[Bk + "ln2_b"], NC), tiles(bb[src], NG), tiles(bb[D + src], NG),
        tiles(i[Bk + "b1"], NF), tiles(i[Fn + "up_bias"], NF), minus], 1))
    o["b_con"], o["down_b"], o["w_con"] = i[Fn + "b_con"], i[Fn + "down_bias"], i[Fn + "W_con"]
    o["w_exp_t"] = c(np.concatenate([i[Fn + "W_exp"].T, i[Fn + "b_exp"][:, None]], 1))
    n = np.arange(FF)
    parts = []
    for kind in range(3):
        for name in ("up_weights", "down_weights"):
            w = i[Fn + name]
            byst = []
            for s in range(STAGES):
                S = 1 << s
                bit = (n >> s) & 1
                k = (n // (2 * S)) * S + n % S
                a_, b_ = ((bit, bit), (bit, 1 - bit), (1 - bit, bit))[kind]
                byst.append(w[s][k, a_, b_])
            parts.append(np.stack(byst, 1).reshape(NF, P, STAGES).transpose(1, 0, 2))
    o["bw"] = c(np.stack(parts, 1).reshape(P, 3, 2, NF, STAGES))
    q = np.arange(P)
    o["ident"] = np.eye(P, dtype=f)
    o["perm"] = c(np.stack([(q[:, None] == (q[None, :] ^ (1 << s))).astype(f) for s in range(LOW)], 1))
    o["fold"] = c(((q[:, None] // 32 == q[None, :] // 32) & (q[None, :] % 32 < HD)
                   & (q[:, None] % HD == q[None, :] % HD)).astype(f))
    o["den_row"] = (q[:, None] == q[None, :] // 32 * 32 + HD).astype(f)
    freq = (1.0 / 10000.0 ** (np.arange(0, HD, 2, dtype=f) / f(HD))).astype(f)
    ang = np.arange(T, dtype=f)[None, :] * np.concatenate([freq, freq])[:, None]
    sign = np.where(np.arange(HD) < HD // 2, -1.0, 1.0).astype(f)[:, None]
    o["rope"] = c(np.tile(np.concatenate([np.cos(ang), np.sin(ang) * sign], 0).astype(f), (HG, 1)))
    j, k = q[:, None], q[None, :]
    masks = [j == k] + [(j // (2 * s) == k // (2 * s)) & (j // s % 2 == 0) & (k // s % 2 == 1)
                        for s in LEVELS[1:]]
    o["masks"] = c(np.stack([np.eye(P, dtype=f), np.where(k > j, NEG, 0.0), np.where(j > k, NEG, 0.0)]
                           + [m.astype(f) for m in masks], 1).astype(f))
    return o


def kernel(**inputs):
    import concourse.bacc as _bacc
    from concourse.bass_utils import run_bass_kernel_spmd as _run

    nc = _bacc.Bacc("TRN2", target_bir_lowering=False, num_devices=1)
    arrays, io = {}, {}
    for name, a in layouts(inputs).items():
        arrays[f"in_{name}"] = np.ascontiguousarray(a)
        io[name] = nc.dram_tensor(f"in_{name}", a.shape, mybir.dt.from_np(a.dtype), kind="ExternalInput").ap()
    out = nc.dram_tensor("out", (B, T, D), F32, kind="ExternalOutput").ap()
    hybrid_kernel(nc, io, out)
    r = _run(nc, [arrays], core_ids=[0])
    return r.results[0]["out"]
```

```python
from contextlib import ExitStack

import numpy as np

import concourse.bass as bass
from concourse import mybir

F32 = mybir.dt.float32
F32R = mybir.dt.float32r
BF16 = mybir.dt.bfloat16
U16 = mybir.dt.uint16
ALU = mybir.AluOpType
ACT = mybir.ActivationFunctionType
AX_X = mybir.AxisListType.X

P = 128
B, T, D = 8, 512, 256
NT = T // P
NC = D // P
H, DK, DV = 4, 128, 64
LR = 64
NMIX, RMIX = 5, 32
NH, HD = 16, 16
HG = 4
NG = NH // HG
FF = 1024
NF = FF // P
EPS = 1e-5
STAGES = 10
LOW = 7
LEVELS = [0, 1, 2, 4, 8, 16, 32, 64]
MIX_ORDER = [1, 2, 0, 3, 4]
AHEAD = [[0, 1], [2], [3], []]
HT = T // 2
RING = 6
NEG = -1e30

COLS = {}
_at = 0
for _name, _n in (("mu", NC), ("xbias", NMIX * NC), ("w_b", H), ("bonus", H), ("gn_w", NC), ("gn_b", NC),
                  ("ln1_g", NC), ("ln1_b", NC), ("ln2_g", NC), ("ln2_b", NC), ("bq", NG), ("bk", NG),
                  ("b1", NF), ("up_b", NF), ("minus_row", 1)):
    COLS[_name] = _at
    _at += _n
NCOLS = _at


def psum_order():
    o = [("zt", "A", 0), ("zt", "A", 1), ("xl", 0), ("xl", 1)]

    def project(n):
        if n == 1:
            return [("wa",)] + [("w", h) for h in range(H)]
        if n == 2:
            return [("k", h) for h in range(H)]
        if n == 0:
            return [("r", h) for h in range(H)]
        if n == 3:
            return [("v", t) for t in range(2)]
        return [("ga",)] + [("g", c) for c in range(NC)]

    for a, n in enumerate(MIX_ORDER):
        o += [("x5", n, c) for c in range(NC)]
        if a >= 1:
            o += project(MIX_ORDER[a - 1])
    o += project(MIX_ORDER[-1])
    o += [("A", lv, h) for lv in range(len(LEVELS)) for h in range(H)]
    o += [("kt", h) for h in range(H)] + [("s", c) for c in range(NT - 1)]
    o += [("o", t) for t in range(2)] + [("ogt", c) for c in range(NC)] + [("ao", t) for t in range(2)]

    def ffn(tag):
        return ([key for hf in range(2)
                 for key in [("zt", tag, hf)] + [("up", tag, hf, m) for m in range(NF // 2)]]
                + [("dn", tag, t) for t in range(2)])

    o += ffn("F")
    o += [("zt", "B", 0), ("vb", 0), ("zt", "B", 1)]
    o += [("q", 0), ("kk", 0)]
    for t in range(NG):
        if t + 1 < NG:
            o += [("q", t + 1), ("kk", t + 1)]
        o += [("qf", t), ("kf", t)]
    o += [("vb", 1)]
    o += [("S", 0, g, i) for g in range(HG) for i in range(3)] + [("mt", 0)]
    for t in range(NG):
        for g in range(HG):
            if t + 1 < NG:
                o += [("S", t + 1, a, i) for a in AHEAD[g] for i in range(3)]
            o += [("ST", t, g, i) for i in range(3)]
            if g == 1 and t >= 1:
                o += [("den", t - 1)]
            if g == HG - 1 and t + 1 < NG:
                o += [("mt", t + 1)]
    o += [("den", NG - 1)] + [("wo", t) for t in range(2)]
    o += ffn("M")
    o += ffn("G")
    return o


def hybrid_kernel(nc, io, out):
    order = psum_order()
    bank_of, use_of, uses = {}, {}, [0] * RING
    for n, key in enumerate(order):
        bank_of[key] = n % RING
        use_of[key] = uses[n % RING]
        uses[n % RING] += 1

    with ExitStack() as ctx:
        def sb(name, shape, dt=F32):
            return ctx.enter_context(nc.sbuf_tensor(name, shape, dt))

        class Sem:

            def __init__(self, name, per):
                self.h = ctx.enter_context(nc.semaphore(name))
                self.name, self.per, self.made = name, per, 0

        sems = []

        def sem(name, per=0):
            s = Sem(name, per)
            sems.append(s)
            return s

        def one(s):
            s.made += 1
            return s.h, 1

        w1 = sb("w_mix1", [P, NC, NMIX * RMIX])
        w2a = sb("w_mix2a", [P, D])
        w2b = sb("w_mix2b", [RMIX, D])
        wr = sb("w_r", [P, NC, H * DK])
        wk = sb("w_k", [P, NC, H * DK])
        wv = sb("w_v", [P, NC, H * DV])
        wwa = sb("w_decay_a", [P, NC, LR])
        wwb = sb("w_decay_b", [LR, H * DK])
        wga = sb("w_gate_a", [P, NC, LR])
        wgb = sb("w_gate_b", [LR + 1, D])
        wo = sb("w_mixer_out", [P, NC, D])
        wup = sb("w_up", [P, NC, FF])
        wdn = sb("w_down", [P, NF, D])
        wq_b = sb("w_q", [P, NC, NG * P])
        wk_b = sb("w_kk", [P, NC, NG * P])
        wv_b = sb("w_vv", [P, NC, D])
        wo_b = sb("w_attn_out", [P, NG, D])
        wm1 = sb("w_mlp1", [P, NC, FF])
        wm2 = sb("w_mlp2", [P, NF, D])
        cols = sb("cols", [P, NCOLS])
        upb = sb("up_bias", [P, NF])
        bias_f = sb("bias_ffn", [P, D])
        bias_o = sb("bias_attn_out", [P, D])
        bias_m = sb("bias_mlp", [P, D])
        bias_v = sb("bias_v", [P, D])
        ident = sb("ident", [P, P])
        masks = sb("masks", [P, 3 + len(LEVELS), P], BF16)
        identb = masks[:, 0, :]
        future = masks[:, 1, :]
        future_t = masks[:, 2, :]
        lmask = masks[:, 3:, :]
        fold = sb("fold", [P, P])
        rope = sb("rope", [P, T])

        x = sb("x", [P, NT, D])
        z = sb("z", [P, NT, D])
        xb = sb("x_plus_bias", [P, NT, D])
        x2 = sb("x_block", [P, NT, D])
        zt = sb("z_t", [P, NC, T + 1])
        delta = sb("delta", [P, NC, T])
        mix = sb("mix", [P, 3, NC, T])
        xl0 = sb("xl0", [P, T])
        xl1 = sb("xl1", [RMIX, T])
        stats = sb("stats", [P, NT, 6])
        mv = sb("mean_var", [P, NT, 2])
        rstd = sb("rstd", [P, 3, NT])
        power = sb("eps_and_power", [P, 2, NT])
        big = sb("big", [P, 16, T])
        dec = sb("decay", [P, H, T])
        dtree = sb("decay_blocks", [P, H, T])
        wat = sb("wa_t", [LR, T])
        gat = sb("ga_t", [LR + 1, T])
        v = sb("v", [P, NT, H * DV])
        scores = sb("scores_t", [P, H, NT, P])
        state = sb("state", [P, NT - 1, H, DV])
        gate = sb("gate", [P, NC, T])
        rqk = sb("qk_rounded", [P, 2, 2, T], F32R)
        vaug = sb("v_ones", [P, NT, NH, 2 * HD])
        den_row = sb("den_row", [P, P])
        maxes = sb("maxes", [P, 2, NT, P])

        qf, qu, kg = big[:, 0:4], big[:, 4:8], big[:, 8:12]
        kt = big[:, 12:16].rearrange("p h (c k) -> p h c k", c=NT)
        gelu = big[:, 0:8]
        qp, kp = big[:, 0:4], big[:, 4:8]
        NPT = 3
        pt = big[:, 8:16].rearrange("p a t -> p (a t)")[:, 0:NPT * 1280].rearrange("p (r n) -> p r n", r=NPT)
        on = mix[:, 0].rearrange("p c t -> p (c t)").rearrange("p (t d) -> p t d", t=NT)
        ogate = mix[:, 1]
        gtanh = mix[:, 2]
        qh = mix[:, 1:3].rearrange("p a c t -> p (a c) t")
        attn_t = mix[:, 0:2].rearrange("p a c t -> p (a c) t")
        osum = delta[:, :, :]
        rden = mix[:, 2]
        z2 = on

        dblk, at = {0: dec[:, :, :]}, 0
        for lv in range(1, 8):
            n = T >> lv
            dblk[lv] = dtree[:, :, at:at + n]
            at += n

        ring = [ctx.enter_context(nc.psum_tensor(f"ring{i}", [P, T], F32)) for i in range(RING)]
        obank = [ctx.enter_context(nc.psum_tensor(f"attn_out{i}", [P, T], F32)) for i in range(2)]

        wload = sem("weights_loaded")
        full = [sem(f"bank_full{i}", uses[i]) for i in range(RING)]
        x_in = sem("x_loaded", 16)
        x_out = sem("x_stored", 16)
        x_saved = sem("x_saved", 1)
        x_ready = sem("x_ready", 2 * 4)
        x2_ready = sem("x2_ready", 2)
        lns = sem("ln_steps", 5 * 2 * NT)
        lnb = sem("ln_block_steps", 4)
        rs_step = sem("rstd_step", 5 * 2 + 1 + 2)
        rs_ready = sem("rstd_ready", 5 * 2 + 1 + 2)
        z_ready = sem("z_ready", 5 * NT)
        z2_ready = sem("z2_ready", NT)
        zt_ready = sem("zt_ready", 5 * 2)
        delta_ready = sem("delta_ready", NC)
        mix0_ready = sem("mix0_ready", NC)
        xl_ready = sem("xl_ready", 2)
        mixd_ready = sem("mix_delta_ready", NMIX * NC)
        mix_ready = sem("mix_ready", NMIX * NC)
        wa_ready = sem("wa_ready", 1)
        ga_ready = sem("ga_ready", 1)
        ew_ready = sem("exp_w_ready", H)
        dec_ready = sem("decay_ready", H)
        tree_ready = sem("tree_ready", 7)
        kg_ready = sem("k_ready", H)
        qf_ready = sem("q_ready", H)
        qu_ready = sem("q_bonus_ready", H)
        kg_level = sem("k_level", 7 * H)
        qf_level = sem("q_level", 7 * H)
        v_ready = sem("v_ready", 2)
        gt_ready = sem("gate_tanh", NC)
        gate_ready = sem("gate_ready", NC)
        a_copied = sem("scores_copied", len(LEVELS) * H)
        gating = sem("dve_gate", 0)
        pool_gate = sem("pool_gate", 0)
        sp_gate = sem("sp_gate", 0)
        kt_ready = sem("k_rows_ready", H)
        state_ready = sem("state_ready", NT - 1)
        gstat = sem("gn_steps", 2 * NT)
        on_ready = sem("o_normed", NT)
        oaff_ready = sem("o_affine", NC)
        og_ready = sem("o_gated", NC)
        xb_ready = sem("xb_ready", 4)
        xs_step = sem("xs_step", 1)
        gelu_ready = sem("gelu_ready", 3 * NF)
        qh_ready = sem("qh_ready", 2 * NG)
        qp_ready = sem("qp_ready", 2 * NG)
        rqk_ready = sem("rounded_ready", 2 * NG)
        vaug_ready = sem("vaug_ready", 2)
        maxs = sem("max_steps", NG * HG * 4)
        qm_ready = sem("q_shifted", NG)
        pt_ready = sem("p_ready", NH * 3)
        pt_used = sem("p_used", NH)
        attn_ready = sem("attn_ready", NG)
        rden_ready = sem("rden_ready", NG)
        osum_ready = sem("osum_ready", NG)
        def copied(key):
            kind, a = key[0], key[1:]
            if kind in ("zt", "dn"):
                layer = "AFBMG".index(a[0])
                return (zt_ready, layer * 2 + a[1] + 1) if kind == "zt" else \
                    (x_ready, {1: 2, 3: 4, 4: 6}[layer] + a[1] + 1)
            return {
                "xl": lambda i: (xl_ready, i + 1),
                "x5": lambda n, c: (mixd_ready, MIX_ORDER.index(n) * NC + c + 1),
                "wa": lambda: (wa_ready, 1),
                "w": lambda h: (ew_ready, h + 1),
                "k": lambda h: (kg_ready, h + 1),
                "r": lambda h: (qf_ready, h + 1),
                "v": lambda t: (v_ready, t + 1),
                "ga": lambda: (ga_ready, 1),
                "g": lambda c: (gate_ready, c + 1),
                "A": lambda lv, h: (a_copied, lv * H + h + 1),
                "kt": lambda h: (kt_ready, h + 1),
                "s": lambda c: (state_ready, c + 1),
                "o": lambda t: (on_ready, 2 * t + 2),
                "ogt": lambda c: (oaff_ready, c + 1),
                "ao": lambda t: (x_ready, t + 1),
                "up": lambda tag, hf, m: (gelu_ready, "FMG".index(tag) * NF + hf * (NF // 2) + m + 1),
                "q": lambda t: (qh_ready, 2 * t + 1),
                "kk": lambda t: (qh_ready, 2 * t + 2),
                "qf": lambda t: (qp_ready, 2 * t + 1),
                "kf": lambda t: (qp_ready, 2 * t + 2),
                "vb": lambda t: (vaug_ready, t + 1),
                "S": lambda t, g, b: (maxs, (t * HG + g) * 4 + (1, 3, 4)[b]),
                "mt": lambda t: (qm_ready, t + 1),
                "ST": lambda t, g, i: (pt_ready, (t * HG + g) * 3 + i + 1),
                "den": lambda t: (rden_ready, t + 1),
                "wo": lambda t: (x2_ready, t + 1),
            }[kind](*a)

        consts = sem("constants_set")
        bl_in = sem("butterfly_tile_in")
        bl_cols = sem("butterfly_cols")
        bl_diag = sem("butterfly_diag")
        bl_mat = sem("butterfly_matrix")
        bl_mm = [sem("butterfly_mm_up"), sem("butterfly_mm_down")]
        bl_ev = [sem("butterfly_evac_up"), sem("butterfly_evac_down")]
        bh_t = sem("butterfly_high_same")
        bh_s = sem("butterfly_high")
        bt_mm = sem("w_up_turned")
        bt_ev = sem("w_up_copied")
        pre = sem("biases_ready")
        seeded = sem("seeded")

        flat = big[:, :, :].rearrange("p a t -> p (a t)")
        UW = D + 1
        y_up = flat[:, 0:NF * UW].rearrange("p (t n) -> p t n", t=NF)
        y_up2 = flat[:, NF * UW:2 * NF * UW].rearrange("p (t n) -> p t n", t=NF)
        dflat = mix[:, :, :, :].rearrange("p a c t -> p (a c t)")
        y_dn = flat[:, 2 * NF * UW:2 * NF * UW + NF * D].rearrange("p (t n) -> p t n", t=NF)
        masks_in = flat[:, 2 * NF * UW + NF * D:2 * NF * UW + NF * D + (3 + len(LEVELS)) * P]
        bw = dflat[:, 0:3 * 2 * NF * STAGES].rearrange("p (k w t s) -> p k w t s", k=3, w=2, t=NF)
        perm = dflat[:, 512:512 + LOW * P].rearrange("p (s n) -> p s n", s=LOW)
        bcol = dflat[:, 1408:1408 + 12 * STAGES].rearrange("p (k w j s) -> p k w j s", k=3, w=2, j=2)
        NSLOT = 8
        diag = gate[:, :, :].rearrange("p c t -> p (c t)").rearrange("p (r n) -> p r n", r=NSLOT)
        bmat = x[:, :, :].rearrange("p a d -> p (a d)").rearrange("p (r n) -> p r n", r=NSLOT)
        y_st = [dec[:, :, :].rearrange("p h t -> p (h t)")[:, 0:4 * UW].rearrange("p (j r n) -> p j r n", j=2, r=2),
                dtree[:, :, :].rearrange("p h t -> p (h t)")[:, 0:4 * D].rearrange("p (j r n) -> p j r n", j=2, r=2)]
        NTMP = 3
        tmp_h = dtree[:, :, :].rearrange("p h t -> p (h t)")[:, 4 * D:4 * D + NTMP * UW] \
            .rearrange("p (r n) -> p r n", r=NTMP)
        down_stages = [(y_dn, y_up, D, 1, 2, STAGES - 1), (y_up, y_dn, D, 1, 2, STAGES - 2)]
        up_stages = [(y_up, y_up2, UW, 0, 1, LOW), (y_up2, y_up, UW, 0, 1, LOW + 1), (y_up, y_up2, UW, 0, 1, LOW + 2)]
        fold_banks = ring + obank
        bdn = scores[:, :, :, :].rearrange("p h c n -> p (h c n)")[:, 0:NF * D].rearrange("p (t n) -> p t n", t=NF)
        down_stages.append((y_dn, bdn, D, 1, 2, LOW))
        N_DOWN, N_UP = len(down_stages) * NF, len(up_stages) * NF
        N_TURN = NC * NF * P // T

        def chain_count(t, s, w, j):
            return t * 4 * LOW + 4 * s + 2 * w + j + 1

        def step_count(t, s, j):
            return t * 2 * LOW + 2 * s + j + 1

        def col(name, i=0):
            return cols[:, COLS[name] + i:COLS[name] + i + 1]

        block = ctx.enter_context(nc.Block())
        dflt = io

        small_loads = [
            (cols[:, :], dflt["cols"]), (ident[:, :], dflt["ident"]), (perm, dflt["perm"]),
            (masks_in, dflt["masks"].rearrange("p s n -> p (s n)")), (bw, dflt["bw"]), (y_dn, dflt["w_con"].rearrange("(t p) n -> p t n", p=P)),
        ]

        def chunked(a):
            return a.rearrange("(c p) n -> p c n", p=P)

        loads = [
            (w1[:, :, :], chunked(dflt["w1"])), (w2a[:, :], dflt["w2"][0:P, :]),
            (w2b[:, :], dflt["w2"][P:P + RMIX, :]), (wr[:, :, :], chunked(dflt["wr"])),
            (wk[:, :, :], chunked(dflt["wk"])), (wv[:, :, :], chunked(dflt["wv"])),
            (wwa[:, :, :], chunked(dflt["wwa"])), (wwb[:, :], dflt["wwb"]),
            (wga[:, :, :], chunked(dflt["wga"])), (wgb[:, :], dflt["wgb"]),
            (wo[:, :, :], chunked(dflt["wo"])), (wq_b[:, :, :], chunked(dflt["wq_b"])),
            (wk_b[:, :, :], chunked(dflt["wk_b"])), (wv_b[:, :, :], chunked(dflt["wv_b"])),
            (wo_b[:, :, :], chunked(dflt["wo_b"])), (wm1[:, :, :], chunked(dflt["wm1"])),
            (den_row[:, :], dflt["den_row"]),
            (wm2[:, :, :], chunked(dflt["wm2"])), (fold[:, :], dflt["fold"]), (rope[:, :], dflt["rope"]),
        ]
        for tile, name in ((bias_f, "b_con"), (xb[:, 0, :], "down_b"), (bias_o, "bo"), (bias_m, "b2"),
                           (bias_v, "bv")):
            dst = tile[:, :] if name != "down_b" else tile
            loads.append((dst, dflt[name].rearrange("(a n) -> a n", a=1).to_broadcast([P, D])))
        N_SMALL, N_LOADS = len(small_loads), len(loads)
        w_up_dram = dflt["w_exp_t"].rearrange("(t p) n -> p t n", p=P)
        x_dram = dflt["x"].rearrange("b (t p) d -> b p t d", p=P)
        out_dram = out.rearrange("b (t p) d -> b p t d", p=P)

        @block.sync
        def _(sp):
            for dst, src in small_loads:
                sp.dma_start(dst, src).then_inc(wload.h, 16)
            sp.dma_start(y_up2, w_up_dram).then_inc(bl_in.h, 16)
            sp.dma_start(x2[:, :, :], x_dram[0]).then_inc(x_in.h, 16)
            sp.sem_inc(x_saved.h, 1)
            with sp.Fori(0, B) as it:
                sp.wait_ge(z_ready.h, it * z_ready.per + 4 * NT)
                sp.sem_inc(sp_gate.h, 1)
                sp.wait_ge(xs_step.h, it * xs_step.per + 1)
                sp.sem_inc(sp_gate.h, 1)
                sp.dma_start(x2[:, :, :], x_dram[it + 1]).then_inc(x_in.h, 16)
                sp.wait_ge(x_ready.h, it * x_ready.per + 8)
                sp.sem_inc(sp_gate.h, 1)
                sp.dma_start(out_dram[it], x[:, :, :]).then_inc(x_out.h, 16)
                sp.wait_ge(x_out.h, it * 16 + 16)
                sp.sem_inc(sp_gate.h, 1)
                sp.sem_inc(x_saved.h, 1)

        @block.gpsimd
        def _(pool):
            for n, (dst, src) in enumerate(loads):
                pool.dma_start(dst, src).then_inc(pre.h, 16)
            nc.gpsimd.memset(zt[:, :, :], 0.0).then_inc(*one(consts))
            nc.gpsimd.memset(scores[:, :, :, :], 0.0).then_inc(*one(consts))
            nc.gpsimd.memset(maxes[:, :, :, :], 0.0).then_inc(*one(consts))
            nc.gpsimd.memset(vaug[:, :, :, :], 1.0).then_inc(*one(consts))
            nc.gpsimd.memset(gat[:, :], 1.0).then_inc(*one(consts))
            nc.gpsimd.memset(power[:, 0, :], EPS).then_inc(*one(consts))
            nc.gpsimd.memset(power[:, 1, :], -0.5).then_inc(*one(consts))
            pool.wait_ge(pre.h, 16 * N_LOADS)
            nc.gpsimd.tensor_tensor(bias_f[:, :], bias_f[:, :], xb[:, 0, :], ALU.add).then_inc(*one(consts))
            pool.wait_ge(consts.h, 8)
            for hf in range(2):
                pool.wait_ge(lns.h, NT * (hf + 1))
                r = rstd[:, 0, 2 * hf:2 * hf + 2]
                nc.gpsimd.tensor_tensor(r, mv[:, 2 * hf:2 * hf + 2, 1], power[:, 0, 2 * hf:2 * hf + 2],
                                        ALU.add).then_inc(*one(rs_step))
                pool.wait_ge(rs_step.h, hf + 1)
                nc.gpsimd.tensor_tensor(r, r, power[:, 1, 2 * hf:2 * hf + 2], ALU.pow).then_inc(rs_ready.h, 1)
            pool.wait_ge(bt_ev.h, N_TURN)
            with pool.Fori(0, B) as it:
                def after(s, k):
                    return s.h, it * s.per + k

                def bank_full(key):
                    return after(full[bank_of[key]], use_of[key] + 1)

                def rsqrt(ready, var, dst, lo, hi):
                    pool.wait_ge(*ready)
                    r = rstd[:, dst, lo:hi]
                    nc.gpsimd.tensor_tensor(r, var[:, lo:hi], power[:, 0, lo:hi], ALU.add).then_inc(*one(rs_step))
                    pool.wait_ge(*after(rs_step, rs_step.made))
                    nc.gpsimd.tensor_tensor(r, r, power[:, 1, lo:hi], ALU.pow).then_inc(*one(rs_ready))

                def norm_half(layer, hf):
                    rsqrt(after(lns, layer * 2 * NT + NT * (hf + 1)), mv[:, :, 1], 0, 2 * hf, 2 * hf + 2)

                for a, n in enumerate(MIX_ORDER):
                    for c in range(NC):
                        pool.wait_ge(*after(mixd_ready, a * NC + c + 1))
                        nc.gpsimd.tensor_tensor(mix[:, a % 3, c, :], mix[:, a % 3, c, :], zt[:, c, 1:T + 1],
                                                ALU.add).then_inc(*one(mix_ready))
                for h in range(H):
                    pool.wait_ge(*after(qf_ready, h + 1))
                    pool.sem_inc(pool_gate.h, 1)
                    nc.gpsimd.tensor_scalar(qu[:, h, :], qf[:, h, :], col("bonus", h), None,
                                            ALU.mult).then_inc(*one(qu_ready))
                for lv in range(1, 8):
                    if lv == 1:
                        pool.wait_ge(*after(dec_ready, H))
                    else:
                        pool.wait_ge(*after(tree_ready, lv - 1))
                    pairs = dblk[lv - 1].rearrange("p h (m two) -> p h m two", two=2)
                    nc.gpsimd.tensor_tensor(dblk[lv], pairs[:, :, :, 0], pairs[:, :, :, 1],
                                            ALU.mult).then_inc(*one(tree_ready))
                pool.wait_ge(*after(tree_ready, 7))
                for lv in range(1, 8):
                    s = LEVELS[lv]
                    for h in range(H):
                        pool.wait_ge(*bank_full(("A", lv, h)))
                        if lv > 1:
                            pool.wait_ge(*after(kg_level, (lv - 2) * H + h + 1))
                        kv = kg[:, h, :].rearrange("p (m two s) -> p m two s", two=2, s=s)[:, :, 0, :]
                        dv = dblk[lv - 1][:, h, :].rearrange("p (m two) -> p m two", two=2)[:, :, 1]
                        nc.gpsimd.tensor_tensor(kv, kv, dv.unsqueeze(2).to_broadcast([P, T // (2 * s), s]),
                                                ALU.mult).then_inc(*one(kg_level))
                rsqrt(after(gstat, 2 * NT), mv[:, :, 1], 0, 0, NT)
                for c in range(NC):
                    pool.wait_ge(*after(oaff_ready, c + 1))
                    pool.wait_ge(*after(gate_ready, c + 1))
                    nc.gpsimd.tensor_tensor(ogate[:, c, :], ogate[:, c, :], gate[:, c, :],
                                            ALU.mult).then_inc(*one(og_ready))

                def plus(out_, a_, bias):
                    return nc.gpsimd.tensor_tensor(out_, a_, bias[:, :].unsqueeze(1).to_broadcast([P, NT, D]),
                                                   ALU.add)

                norm_half(1, 0)
                norm_half(1, 1)
                pool.wait_ge(*after(x_ready, 2))
                plus(xb[:, :, :], x[:, :, :], bias_f).then_inc(*one(xb_ready))
                for hf in range(2):
                    norm_half(2, hf)
                    rsqrt(after(lnb, 2 * hf + 2), rstd[:, 1, :], 2, 2 * hf, 2 * hf + 2)
                pool.wait_ge(*after(z_ready, 3 * NT))
                pool.wait_ge(*after(x_ready, 4))
                plus(xb[:, :, :], z[:, :, :], bias_o).then_inc(*one(xb_ready))
                for t in range(NG):
                    for i, src in enumerate((qp, kp)):
                        pool.wait_ge(*after(qp_ready, 2 * t + i + 1))
                        if t >= 2:
                            pool.wait_ge(*bank_full(("S", t - 2, HG - 1, 2)))
                        pool.sem_inc(pool_gate.h, 1)
                        nc.gpsimd.tensor_copy(rqk[:, t % 2, i, :], src[:, t, :]).then_inc(*one(rqk_ready))
                norm_half(3, 0)
                norm_half(3, 1)
                pool.wait_ge(*after(x2_ready, 2))
                nc.gpsimd.tensor_tensor(xb[:, :, :], x[:, :, :], x2[:, :, :], ALU.add).then_inc(*one(xs_step))
                pool.wait_ge(*after(xs_step, 1))
                plus(xb[:, :, :], xb[:, :, :], bias_m).then_inc(*one(xb_ready))
                norm_half(4, 0)
                norm_half(4, 1)
                pool.wait_ge(*after(x_ready, 6))
                plus(xb[:, :, :], x[:, :, :], bias_f).then_inc(*one(xb_ready))
                norm_half(5, 0)
                norm_half(5, 1)

        rs_step.made -= 2

        @block.scalar
        def _(act):
            def high_stages(first, stages):
                n = first
                for src, dst, width, which, kind, s in stages:
                    for t in range(NF):
                        if n >= NTMP:
                            act.wait_ge(bh_s.h, n - NTMP + 1)
                        nc.scalar.activation(tmp_h[:, n % NTMP, 0:width], src[:, t, 0:width], ACT.Copy,
                                             scale=bw[:, 0, which, t, s:s + 1]).then_inc(bh_t.h, 1)
                        n += 1

            act.wait_ge(wload.h, 16 * N_SMALL)
            high_stages(0, down_stages)
            with act.Fori(0, NF // 2) as t:
                def diagonals(s):
                    for w in range(2):
                        for j in range(2):
                            if s >= 2:
                                act.wait_ge(bl_mat.h, chain_count(t, s - 2, w, j))
                            st = s if w == 0 else LOW - 1 - s
                            nc.scalar.activation(diag[:, (4 * s + 2 * w + j) % NSLOT, :], ident[:, :], ACT.Copy,
                                                 scale=bcol[:, 0, w, j, st:st + 1]).then_inc(bl_diag.h, 1)

                act.wait_ge(bl_cols.h, t + 1)
                diagonals(0)
                for s in range(LOW):
                    if s + 1 < LOW:
                        diagonals(s + 1)
                    for j in range(2):
                        act.wait_ge(bl_mm[0].h, step_count(t, s, j))
                        ps = fold_banks[2 * j + s % 2][:, 0:UW]
                        if s < LOW - 1:
                            nc.scalar.activation(y_st[0][:, j, (s + 1) % 2, :], ps, ACT.Copy).then_inc(bl_ev[0].h, 1)
                        else:
                            nc.scalar.activation(y_up[:, bass.ds(t * 2 + j, 1), :], ps.unsqueeze(1),
                                                 ACT.Copy).then_inc(bl_ev[0].h, 1)
            act.wait_ge(bl_ev[0].h, NF * LOW + 1)
            high_stages(N_DOWN, up_stages)
            for n in range(N_TURN):
                act.wait_ge(bt_mm.h, n + 1)
                c, q = n % NC, n // NC
                nc.scalar.activation(wup[:, c, q * T:(q + 1) * T], ring[n][:, :], ACT.Copy).then_inc(*one(bt_ev))
            act.wait_ge(pre.h, 16 * N_LOADS)
            with act.Fori(0, B) as it:
                def after(s, k):
                    return s.h, it * s.per + k

                def bank_full(key):
                    return after(full[bank_of[key]], use_of[key] + 1)

                def bank(key):
                    return ring[bank_of[key]]

                def turned(tag, hf, scale=None, bias=None):
                    key = ("zt", tag, hf)
                    act.wait_ge(*bank_full(key))
                    ps = bank(key)[:, :].rearrange("p (c t) -> p c t", c=NC)
                    dst = zt[:, :, 1 + hf * HT:1 + (hf + 1) * HT]
                    if scale is None:
                        ins = nc.scalar.activation(dst, ps, ACT.Copy)
                    else:
                        for c in range(NC):
                            ins = nc.scalar.activation(dst[:, c, :], ps[:, c, :], ACT.Identity,
                                                       scale=col(scale, c), bias=col(bias, c))
                    ins.then_inc(*one(zt_ready))

                def evac(key, dst, done, func=ACT.Copy, rows=P, **kw):
                    act.wait_ge(*bank_full(key))
                    nc.scalar.activation(dst, bank(key)[0:rows, :], func, **kw).then_inc(*one(done))

                turned("A", 0)
                turned("A", 1)
                evac(("xl", 0), xl0[:, :], xl_ready, ACT.Tanh)
                evac(("xl", 1), xl1[:, :], xl_ready, ACT.Tanh, rows=RMIX)
                evac(("wa",), wat[:, :], wa_ready, ACT.Tanh, rows=LR)
                for h in range(H):
                    evac(("w", h), dec[:, h, :], ew_ready, ACT.Exp, bias=col("w_b", h))
                    act.wait_ge(*after(ew_ready, h + 1))
                    nc.scalar.activation(dec[:, h, :], dec[:, h, :], ACT.Exp, scale=-1.0).then_inc(*one(dec_ready))
                for h in range(H):
                    evac(("k", h), kg[:, h, :], kg_ready)
                for h in range(H):
                    evac(("r", h), qf[:, h, :], qf_ready)
                for t in range(2):
                    evac(("v", t), v[:, 2 * t:2 * t + 2, :].rearrange("p a b -> p (a b)"), v_ready)
                evac(("ga",), gat[0:LR, :], ga_ready, ACT.Tanh, rows=LR)
                for c in range(NC):
                    act.wait_ge(*bank_full(("g", c)))
                    nc.scalar.activation(gtanh[:, c, :], bank(("g", c))[:, :], ACT.Tanh,
                                         scale=0.5).then_inc(*one(gt_ready))
                for h in range(H):
                    act.wait_ge(*bank_full(("kt", h)))
                    nc.scalar.activation(kt[:, h, 0:NT - 1, :],
                                         bank(("kt", h))[:, 0:(NT - 1) * P].rearrange("p (c k) -> p c k", k=P),
                                         ACT.Copy).then_inc(*one(kt_ready))
                for c in range(NC):
                    evac(("ogt", c), ogate[:, c, :], oaff_ready, ACT.Identity, scale=col("gn_w", c),
                         bias=col("gn_b", c))

                def ffn_half(tag, hf, bias, *affine):
                    turned(tag, hf, *affine)
                    for m2 in range(NF // 2):
                        key = ("up", tag, hf, m2)
                        act.wait_ge(*bank_full(key))
                        for a in range(2):
                            m = 2 * m2 + a
                            ins = nc.scalar.activation(gelu[:, m, hf * HT:(hf + 1) * HT],
                                                       bank(key)[:, a * HT:(a + 1) * HT], ACT.Gelu, bias=bias(m))
                        ins.then_inc(*one(gelu_ready))

                for hf in range(2):
                    ffn_half("F", hf, lambda m: upb[:, m:m + 1])
                for hf in range(2):
                    act.wait_ge(*after(rs_ready, 7 + 2 * hf))
                    for t in (2 * hf, 2 * hf + 1):
                        act.wait_ge(*after(z_ready, 2 * NT + t + 1))
                        nc.scalar.activation(z2[:, t, :], z[:, t, :], ACT.Copy,
                                             scale=rstd[:, 2, t:t + 1]).then_inc(*one(z2_ready))
                    turned("B", hf, "ln1_g", "ln1_b")
                for t in range(NG):
                    evac(("qf", t), qp[:, t, :], qp_ready)
                    evac(("kf", t), kp[:, t, :], qp_ready, ACT.Identity, bias=col("minus_row"))

                def weighted(t):
                    act.wait_ge(*after(pt_used, HG * (t + 1)))
                    if t >= 2:
                        act.wait_ge(*after(attn_ready, t - 1))
                    nc.scalar.activation(osum[:, t % 2, :], obank[t % 2][:, :], ACT.Copy) \
                        .then_inc(*one(osum_ready))

                for t in range(NG):
                    for g in range(HG):
                        n = t * HG + g
                        if n >= NPT:
                            act.wait_ge(*after(pt_used, n - NPT + 1))
                        for i, (lo, hi) in enumerate(((0, 512), (512, 1024), (1024, 1280))):
                            key = ("ST", t, g, i)
                            act.wait_ge(*bank_full(key))
                            nc.scalar.activation(pt[:, n % NPT, lo:hi], bank(key)[:, 0:hi - lo], ACT.Exp,
                                                 scale=HD ** -0.5).then_inc(*one(pt_ready))
                        if g == 0 and t >= 1:
                            weighted(t - 1)
                weighted(NG - 1)
                for hf in range(2):
                    ffn_half("M", hf, lambda m: col("b1", m), "ln2_g", "ln2_b")
                for hf in range(2):
                    ffn_half("G", hf, lambda m: upb[:, m:m + 1])

        @block.vector
        def _(dve):
            dve.wait_ge(wload.h, 16 * N_SMALL)
            nc.vector.tensor_copy(masks[:, :, :].rearrange("p s n -> p (s n)"), masks_in).then_inc(*one(seeded))

            def high_stages(first, stages):
                n = first
                for src, dst, width, which, kind, s in stages:
                    if dst is bdn:
                        dve.wait_ge(consts.h, 2)
                    for t in range(NF):
                        if t == 0 and n > first:
                            dve.wait_ge(bh_s.h, n)
                        dve.wait_ge(bh_t.h, n + 1)
                        nc.vector.scalar_tensor_tensor(out=dst[:, t, 0:width], in0=src[:, t ^ (1 << (s - LOW)), 0:width],
                                                       scalar=bw[:, kind, which, t, s:s + 1],
                                                       in1=tmp_h[:, n % NTMP, 0:width], op0=ALU.mult,
                                                       op1=ALU.add).then_inc(bh_s.h, 1)
                        n += 1

            high_stages(0, down_stages)
            dve.wait_ge(bh_s.h, N_DOWN)
            for w in range(2):
                dve.sem_inc(bl_ev[w].h, 1)
            with dve.Fori(0, NF // 2) as t:
                def matrices(s):
                    for w in range(2):
                        st = s if w == 0 else LOW - 1 - s
                        for j in range(2):
                            dve.wait_ge(bl_diag.h, chain_count(t, s, w, j))
                            if s >= 2:
                                dve.wait_ge(bl_mm[w].h, step_count(t, s - 2, j))
                            slot = (4 * s + 2 * w + j) % NSLOT
                            nc.vector.scalar_tensor_tensor(out=bmat[:, slot, :], in0=perm[:, st, :],
                                                           scalar=bcol[:, 2 if w == 0 else 1, w, j, st:st + 1],
                                                           in1=diag[:, slot, :], op0=ALU.mult,
                                                           op1=ALU.add).then_inc(bl_mat.h, 1)

                nc.vector.tensor_copy(bcol.rearrange("p k w j s -> p (k w) (j s)"),
                                      bw.rearrange("p k w t s -> p (k w) t s")[:, :, bass.ds(t * 2, 2), :]
                                      .rearrange("p k t s -> p k (t s)")).then_inc(bl_cols.h, 1)
                dve.wait_ge(bl_cols.h, t + 1)
                matrices(0)
                for s in range(LOW):
                    if s + 1 < LOW:
                        matrices(s + 1)
                    for j in range(2):
                        dve.wait_ge(bl_mm[1].h, step_count(t, s, j))
                        ps = fold_banks[4 + 2 * j + s % 2][:, 0:D]
                        if s < LOW - 1:
                            nc.vector.tensor_copy(y_st[1][:, j, (s + 1) % 2, :], ps).then_inc(bl_ev[1].h, 1)
                        else:
                            nc.vector.tensor_copy(wdn[:, bass.ds(t * 2 + j, 1), :],
                                                  ps.unsqueeze(1)).then_inc(bl_ev[1].h, 1)
                dve.wait_ge(bl_mm[0].h, step_count(t, LOW - 1, 1))
            dve.wait_ge(x_in.h, 16)
            for hf in range(2):
                for t in (2 * hf, 2 * hf + 1):
                    nc.vector.bn_stats(stats[:, t, :], x2[:, t, :]).then_inc(lns.h, 1)
                dve.wait_ge(lns.h, NT * hf + 2)
                for t in (2 * hf, 2 * hf + 1):
                    nc.vector.bn_aggr(mv[:, t, :], stats[:, t, :]).then_inc(lns.h, 1)
                dve.wait_ge(rs_ready.h, hf + 1)
                for t in (2 * hf, 2 * hf + 1):
                    nc.vector.tensor_scalar(z[:, t, :], x2[:, t, :], mv[:, t, 0:1], rstd[:, 0, t:t + 1],
                                            ALU.subtract, ALU.mult).then_inc(z_ready.h, 1)
            dve.wait_ge(bl_ev[0].h, NF * LOW + 1)
            high_stages(N_DOWN, up_stages)
            dve.wait_ge(bh_s.h, N_DOWN + N_UP)
            for m in range(NF):
                ins = nc.vector.tensor_tensor(upb[:, m:m + 1], y_up2[:, m, D:UW], col("up_b", m), ALU.add)
            ins.then_inc(*one(seeded))
            dve.wait_ge(bt_ev.h, N_TURN)
            dve.wait_ge(consts.h, 8)
            dve.wait_ge(pre.h, 16 * N_LOADS)

            with dve.Fori(0, B) as it:
                def after(s, k):
                    return s.h, it * s.per + k

                def bank_full(key):
                    return after(full[bank_of[key]], use_of[key] + 1)

                def bank(key):
                    return ring[bank_of[key]]

                def norm_half(layer, hf, src, ready):
                    base = layer * 2 * NT + hf * NT
                    tiles = (2 * hf, 2 * hf + 1)
                    dve.wait_ge(*ready)
                    for t in tiles:
                        nc.vector.bn_stats(stats[:, t, :], src[:, t, :]).then_inc(*one(lns))
                    dve.wait_ge(*after(lns, base + 2))
                    dve.sem_inc(gating.h, 1)
                    for t in tiles:
                        nc.vector.bn_aggr(mv[:, t, :], stats[:, t, :]).then_inc(*one(lns))
                    dve.wait_ge(*after(rs_ready, (1, 4, 6, 10, 12, 14)[layer] + hf * (2 if layer == 2 else 1)))
                    for t in tiles:
                        nc.vector.tensor_scalar(z[:, t, :], src[:, t, :], mv[:, t, 0:1], rstd[:, 0, t:t + 1],
                                                ALU.subtract, ALU.mult).then_inc(*one(z_ready))
                    if layer == 2:
                        sl = slice(2 * hf, 2 * hf + 2)
                        nc.vector.tensor_tensor(rstd[:, 1, sl], rstd[:, 0, sl], rstd[:, 0, sl],
                                                ALU.mult).then_inc(*one(lnb))
                        dve.wait_ge(*after(lnb, 2 * hf + 1))
                        nc.vector.tensor_tensor(rstd[:, 1, sl], rstd[:, 1, sl], mv[:, sl, 1],
                                                ALU.mult).then_inc(*one(lnb))

                def add_back(key, t, res, dst, done):
                    dve.wait_ge(*bank_full(key))
                    nc.vector.tensor_tensor(dst[:, 2 * t:2 * t + 2, :].rearrange("p a b -> p (a b)"), bank(key)[:, :],
                                            res[:, 2 * t:2 * t + 2, :].rearrange("p a b -> p (a b)"),
                                            ALU.add).then_inc(*one(done))

                def values(t):
                    dve.wait_ge(*bank_full(("vb", t)))
                    for a in range(2):
                        ins = nc.vector.tensor_tensor(
                            vaug[:, 2 * t + a, :, 0:HD],
                            bank(("vb", t))[:, a * D:(a + 1) * D].rearrange("p (h d) -> p h d", d=HD),
                            bias_v[:, :].rearrange("p (h d) -> p h d", d=HD), ALU.add)
                    ins.then_inc(*one(vaug_ready))

                for c in range(NC):
                    dve.wait_ge(*after(zt_ready, 2))
                    nc.vector.tensor_tensor(delta[:, c, :], zt[:, c, 0:T], zt[:, c, 1:T + 1],
                                            ALU.subtract).then_inc(*one(delta_ready))
                for c in range(NC):
                    dve.wait_ge(*after(delta_ready, c + 1))
                    nc.vector.scalar_tensor_tensor(out=mix[:, 2, c, :], in0=delta[:, c, :], scalar=col("mu", c),
                                                   in1=zt[:, c, 1:T + 1], op0=ALU.mult,
                                                   op1=ALU.add).then_inc(*one(mix0_ready))
                for a, n in enumerate(MIX_ORDER):
                    for c in range(NC):
                        key = ("x5", n, c)
                        dve.wait_ge(*bank_full(key))
                        if a == 3:
                            dve.wait_ge(*bank_full(("w", 0)))
                        if a == 4:
                            dve.wait_ge(*bank_full(("k", H - 1)))
                        nc.vector.scalar_tensor_tensor(out=mix[:, a % 3, c, :], in0=bank(key)[:, :],
                                                       scalar=col("xbias", n * NC + c), in1=delta[:, c, :],
                                                       op0=ALU.add, op1=ALU.mult).then_inc(*one(mixd_ready))
                for c in range(NC):
                    dve.wait_ge(*after(gt_ready, c + 1))
                    nc.vector.scalar_tensor_tensor(out=gate[:, c, :], in0=gtanh[:, c, :], scalar=1.0,
                                                   in1=bank(("g", c))[:, :], op0=ALU.add,
                                                   op1=ALU.mult).then_inc(*one(gate_ready))
                dve.wait_ge(*after(tree_ready, 7))
                for lv, s in enumerate(LEVELS):
                    for h in range(H):
                        key = ("A", lv, h)
                        dve.wait_ge(*bank_full(key))
                        if lv >= 1:
                            dve.wait_ge(*after(a_copied, (lv - 1) * H + h + 1))
                        dve.sem_inc(gating.h, 1)
                        nc.vector.copy_predicated(scores[:, h, :, :],
                                                  lmask[:, lv, :].bitcast(U16).unsqueeze(1).to_broadcast([P, NT, P]),
                                                  bank(key)[:, :].rearrange("p (c n) -> p c n", c=NT)) \
                            .then_inc(*one(a_copied))
                        if lv >= 1:
                            if lv > 1:
                                dve.wait_ge(*after(qf_level, (lv - 2) * H + h + 1))
                            qv = qf[:, h, :].rearrange("p (m two s) -> p m two s", two=2, s=s)[:, :, 1, :]
                            dv = dblk[lv - 1][:, h, :].rearrange("p (m two) -> p m two", two=2)[:, :, 0]
                            nc.vector.tensor_tensor(qv, qv, dv.unsqueeze(2).to_broadcast([P, T // (2 * s), s]),
                                                    ALU.mult).then_inc(*one(qf_level))
                for c in range(NT - 1):
                    key = ("s", c)
                    dve.wait_ge(*bank_full(key))
                    if c == 0:
                        nc.vector.tensor_copy(state[:, 0, :, :].rearrange("p h v -> p (h v)"),
                                              bank(key)[:, 0:H * DV]).then_inc(*one(state_ready))
                    else:
                        dve.wait_ge(*after(state_ready, c))
                        for h in range(H):
                            ins = nc.vector.scalar_tensor_tensor(
                                out=state[:, c, h, :], in0=state[:, c - 1, h, :], scalar=dblk[7][:, h, c:c + 1],
                                in1=bank(key)[:, h * DV:(h + 1) * DV], op0=ALU.mult, op1=ALU.add)
                        ins.then_inc(*one(state_ready))
                for t in range(NT):
                    dve.wait_ge(*bank_full(("o", t // 2)))
                    nc.vector.bn_stats(stats[:, t, :], bank(("o", t // 2))[:, (t % 2) * D:(t % 2 + 1) * D]) \
                        .then_inc(*one(gstat))
                dve.wait_ge(*after(gstat, NT))
                dve.sem_inc(gating.h, 1)
                for t in range(NT):
                    nc.vector.bn_aggr(mv[:, t, :], stats[:, t, :]).then_inc(*one(gstat))
                dve.wait_ge(*after(rs_ready, 3))
                for t in range(NT):
                    nc.vector.tensor_scalar(on[:, t, :], bank(("o", t // 2))[:, (t % 2) * D:(t % 2 + 1) * D],
                                            mv[:, t, 0:1], rstd[:, 0, t:t + 1], ALU.subtract,
                                            ALU.mult).then_inc(*one(on_ready))
                for t in range(2):
                    key = ("ao", t)
                    dve.wait_ge(*bank_full(key))
                    if t == 0:
                        dve.wait_ge(*after(x_saved, 1))
                    xv = x[:, 2 * t:2 * t + 2, :].rearrange("p a b -> p (a b)")
                    nc.vector.scalar_tensor_tensor(out=xv, in0=bank(key)[:, :], scalar=0.5,
                                                   in1=x2[:, 2 * t:2 * t + 2, :].rearrange("p a b -> p (a b)"),
                                                   op0=ALU.mult,
                                                   op1=ALU.add).then_inc(*one(x_ready))
                    norm_half(1, t, x, after(x_ready, t + 1))

                dve.wait_ge(*after(xb_ready, 1))
                for t in range(2):
                    add_back(("dn", "F", t), t, xb, x, x_ready)
                    norm_half(2, t, x, after(x_ready, 2 + t + 1))
                values(0)
                for t in range(NG):
                    for i, (name, b) in enumerate((("q", "bq"), ("kk", "bk"))):
                        n = 2 * t + i
                        dve.wait_ge(*bank_full((name, t)))
                        if n == 0:
                            dve.wait_ge(*after(zt_ready, 6))
                        if n >= 4:
                            dve.wait_ge(*bank_full(("qf" if i == 0 else "kf", t - 2)))
                        nc.vector.scalar_tensor_tensor(out=qh[:, n % 4, :], in0=bank((name, t))[:, :],
                                                       scalar=col(b, t), in1=rope[:, :], op0=ALU.add,
                                                       op1=ALU.mult).then_inc(*one(qh_ready))
                values(1)

                def row_max(t, g):
                    c = 32 * g + HD
                    n = (t * HG + g) * 4
                    if t >= 2 and g == 0:
                        dve.wait_ge(*bank_full(("mt", t - 2)))
                    for i, (qt, lo, hi) in enumerate(((3, 0, 512), (2, 0, 384), (0, 384, 512), (1, 0, 256))):
                        b = (0, 1, 1, 2)[i]
                        key = ("S", t, g, b)
                        dve.wait_ge(*bank_full(key))
                        nc.vector.tensor_reduce(maxes[:, t % 2, qt, c:c + 1], bank(key)[:, lo:hi], AX_X,
                                                ALU.max).then_inc(*one(maxs))

                def normalised(t):
                    dve.wait_ge(*bank_full(("den", t)))
                    if t >= 2:
                        dve.wait_ge(*after(attn_ready, t - 1))
                    nc.vector.reciprocal(rden[:, t % 2, :], bank(("den", t))[:, :]).then_inc(*one(rden_ready))
                    dve.wait_ge(*after(rden_ready, t + 1))
                    nc.vector.tensor_tensor(attn_t[:, t, :], osum[:, t % 2, :], rden[:, t % 2, :], ALU.mult) \
                        .then_inc(*one(attn_ready))

                def shift(t):
                    dve.wait_ge(*bank_full(("mt", t)))
                    nc.vector.tensor_tensor(qp[:, t, :], bank(("mt", t))[:, :], qp[:, t, :],
                                            ALU.add).then_inc(*one(qm_ready))

                for g in range(HG):
                    row_max(0, g)
                shift(0)
                for t in range(NG):
                    for g in range(HG):
                        if t + 1 < NG:
                            for a in AHEAD[g]:
                                row_max(t + 1, a)
                        if g == 1 and t >= 1:
                            normalised(t - 1)
                        if g == HG - 1 and t + 1 < NG:
                            shift(t + 1)
                normalised(NG - 1)
                dve.wait_ge(*after(xb_ready, 2))
                for t in range(2):
                    add_back(("wo", t), t, xb, x2, x2_ready)
                    norm_half(3, t, x2, after(x2_ready, t + 1))
                dve.wait_ge(*after(xb_ready, 3))
                for t in range(2):
                    add_back(("dn", "M", t), t, xb, x, x_ready)
                    norm_half(4, t, x, after(x_ready, 4 + t + 1))
                dve.wait_ge(*bank_full(("zt", "G", 1)))
                for hf in range(2):
                    norm_half(5, hf, x2, after(x_in, 32))
                dve.wait_ge(*after(xb_ready, 4))
                for t in range(2):
                    add_back(("dn", "G", t), t, xb, x, x_ready)

        @block.tensor
        def _(pe):
            mm = nc.tensor.matmul
            pe.wait_ge(bl_in.h, 16)
            with pe.Fori(0, NF // 2) as t:
                for s in range(LOW):
                    for w in range(2):
                        for j in range(2):
                            pe.wait_ge(bl_mat.h, chain_count(t, s, w, j))
                            pe.wait_ge(bl_ev[w].h, t * 2 * LOW + 1 if s == 0 else step_count(t, s - 1, j) + 1)
                            if s == 0:
                                src = (y_up2 if w == 0 else bdn)[:, bass.ds(t * 2 + j, 1), :] \
                                    .rearrange("p a n -> p (a n)")
                            else:
                                src = y_st[w][:, j, s % 2, :]
                            mm(fold_banks[4 * w + 2 * j + s % 2][:, 0:(UW, D)[w]],
                               bmat[:, (4 * s + 2 * w + j) % NSLOT, :], src, start=True,
                               stop=True).then_inc(bl_mm[w].h, 1)
            pe.wait_ge(bh_s.h, N_DOWN + N_UP)
            for n in range(N_TURN):
                c, q = n % NC, n // NC
                for m in range(T // P):
                    ins = nc.tensor.transpose(ring[n][:, m * P:(m + 1) * P],
                                              y_up2[:, q * (T // P) + m, c * P:(c + 1) * P], ident[:, :])
                ins.then_inc(*one(bt_mm))
            pe.wait_ge(bt_ev.h, N_TURN)
            pe.wait_ge(seeded.h, 2)
            pe.wait_ge(pre.h, 16 * N_LOADS)
            pe.wait_ge(consts.h, 8)

            with pe.Fori(0, B) as it:
                def after(s, k):
                    return s.h, it * s.per + k

                count = [0]

                waited = {}

                def take(*keys):
                    need = {}
                    for key in keys:
                        assert order[count[0]] == key, (order[count[0]], key)
                        count[0] += 1
                        if count[0] > RING:
                            s, k = copied(order[count[0] - 1 - RING])
                            need[s] = max(need.get(s, 0), k)
                    for s, k in need.items():
                        if waited.get(s, 0) < k:
                            waited[s] = k
                            pe.wait_ge(*after(s, k))
                    banks = [ring[bank_of[key]] for key in keys]
                    return banks if len(keys) > 1 else banks[0]

                def filled(key):
                    return one(full[bank_of[key]])

                def turn(tag, hf, src, ready):
                    ps = take(("zt", tag, hf))
                    for a in range(2):
                        t = 2 * hf + a
                        pe.wait_ge(*ready(t))
                        for c in range(NC):
                            ins = nc.tensor.transpose(ps[:, c * HT + a * P:c * HT + (a + 1) * P],
                                                      src[:, t, c * P:(c + 1) * P], ident[:, :])
                    ins.then_inc(*filled(("zt", tag, hf)))

                def dense(key, w, lo, hi, src, rows=P):
                    ps = take(key)
                    for c in range(NC):
                        ins = mm(ps[0:hi - lo, :], w[:, c, lo:hi], src[:, c, :], start=(c == 0), stop=(c == NC - 1))
                    ins.then_inc(*filled(key))

                def dense_rows(keys, src, w, nk):
                    for key in keys:
                        t2 = key[-1]
                        ps = take(key)
                        for t in range(2):
                            tok = (2 * t2 + t) * P
                            for c in range(nk):
                                ins = mm(ps[:, t * D:(t + 1) * D], src[:, c, tok:tok + P], w[:, c, :],
                                         start=(c == 0), stop=(c == nk - 1))
                        ins.then_inc(*filled(key))

                turn("A", 0, z, lambda t: after(z_ready, t + 1))
                turn("A", 1, z, lambda t: after(z_ready, t + 1))
                for i in range(2):
                    if i == 0:
                        pe.wait_ge(*after(mix0_ready, NC))
                    dense(("xl", i), w1, i * P, P + i * RMIX, mix[:, 2])

                def low_rank(a, n):
                    pe.wait_ge(*after(xl_ready, 1 if n < 4 else 2))
                    for c in range(NC):
                        ps = take(("x5", n, c))
                        if n < 4:
                            ins = mm(ps[:, :], w2a[32 * n:32 * n + 32, c * P:(c + 1) * P], xl0[32 * n:32 * n + 32, :],
                                     start=True, stop=True)
                        else:
                            ins = mm(ps[:, :], w2b[:, c * P:(c + 1) * P], xl1[:, :], start=True, stop=True)
                        ins.then_inc(*filled(("x5", n, c)))

                def project(a, n):
                    pe.wait_ge(*after(mix_ready, (a + 1) * NC))
                    src = mix[:, a % 3]
                    if n == 1:
                        dense(("wa",), wwa, 0, LR, src)
                        pe.wait_ge(*after(wa_ready, 1))
                        for h in range(H):
                            ps = take(("w", h))
                            mm(ps[:, :], wwb[:, h * DK:(h + 1) * DK], wat[:, :], start=True, stop=True) \
                                .then_inc(*filled(("w", h)))
                    elif n == 2:
                        for h in range(H):
                            dense(("k", h), wk, h * DK, (h + 1) * DK, src)
                    elif n == 0:
                        for h in range(H):
                            dense(("r", h), wr, h * DK, (h + 1) * DK, src)
                    elif n == 3:
                        dense_rows([("v", t) for t in range(2)], src, wv, NC)
                    else:
                        dense(("ga",), wga, 0, LR, src)
                        pe.wait_ge(*after(ga_ready, 1))
                        for c in range(NC):
                            ps = take(("g", c))
                            mm(ps[:, :], wgb[:, c * P:(c + 1) * P], gat[:, :], start=True, stop=True) \
                                .then_inc(*filled(("g", c)))

                for a, n in enumerate(MIX_ORDER):
                    low_rank(a, n)
                    if a >= 1:
                        project(a - 1, MIX_ORDER[a - 1])
                project(NMIX - 1, MIX_ORDER[-1])

                for lv in range(len(LEVELS)):
                    for h in range(H):
                        if lv == 0:
                            pe.wait_ge(*after(kg_ready, h + 1))
                            pe.wait_ge(*after(qu_ready, h + 1))
                        if lv >= 2:
                            pe.wait_ge(*after(kg_level, (lv - 2) * H + h + 1))
                            pe.wait_ge(*after(qf_level, (lv - 2) * H + h + 1))
                        ps = take(("A", lv, h))
                        q = qu if lv == 0 else qf
                        for c in range(NT):
                            tok = slice(c * P, (c + 1) * P)
                            ins = mm(ps[:, tok], kg[:, h, tok], q[:, h, tok], start=True, stop=True)
                        ins.then_inc(*filled(("A", lv, h)))
                for h in range(H):
                    pe.wait_ge(*after(kg_level, 6 * H + h + 1))
                    ps = take(("kt", h))
                    for c in range(NT - 1):
                        ins = nc.tensor.transpose(ps[:, c * P:(c + 1) * P], kg[:, h, c * P:(c + 1) * P], ident[:, :])
                    ins.then_inc(*filled(("kt", h)))
                pe.wait_ge(*after(v_ready, 2))
                for c in range(NT - 1):
                    ps = take(("s", c))
                    for h in range(H):
                        if c == 0:
                            pe.wait_ge(*after(kt_ready, h + 1))
                        ins = mm(ps[:, h * DV:(h + 1) * DV], kt[:, h, c, :], v[:, c, h * DV:(h + 1) * DV],
                                 start=True, stop=True)
                    ins.then_inc(*filled(("s", c)))
                pe.wait_ge(*after(a_copied, len(LEVELS) * H))
                pe.wait_ge(*after(qf_level, 7 * H))
                for c in range(NT):
                    if c % 2 == 0:
                        ps = take(("o", c // 2))
                    if c >= 1:
                        pe.wait_ge(*after(state_ready, c))
                    for h in range(H):
                        dst = ps[:, (c % 2) * D + h * DV:(c % 2) * D + (h + 1) * DV]
                        ins = mm(dst, scores[:, h, c, :], v[:, c, h * DV:(h + 1) * DV], start=True, stop=(c == 0))
                        if c >= 1:
                            ins = mm(dst, qf[:, h, c * P:(c + 1) * P], state[:, c - 1, h, :], start=False, stop=True)
                    if c % 2:
                        ins.then_inc(*filled(("o", c // 2)))
                for c in range(NC):
                    ps = take(("ogt", c))
                    for t in range(NT):
                        if c == 0:
                            pe.wait_ge(*after(on_ready, t + 1))
                        ins = nc.tensor.transpose(ps[:, t * P:(t + 1) * P], on[:, t, c * P:(c + 1) * P], ident[:, :])
                    ins.then_inc(*filled(("ogt", c)))
                pe.wait_ge(*after(og_ready, NC))
                dense_rows([("ao", t) for t in range(2)], ogate, wo, NC)

                def ffn(tag, src, layer, wu, wd):
                    for hf in range(2):
                        turn(tag, hf, src, lambda t: after(z_ready, layer * NT + t + 1))
                        pe.wait_ge(*after(zt_ready, 2 * layer + hf + 1))
                        for m2 in range(NF // 2):
                            ps = take(("up", tag, hf, m2))
                            for a in range(2):
                                m = 2 * m2 + a
                                for c in range(NC):
                                    ins = mm(ps[:, a * HT:(a + 1) * HT], wu[:, c, m * P:(m + 1) * P],
                                             zt[:, c, 1 + hf * HT:1 + (hf + 1) * HT], start=(c == 0),
                                             stop=(c == NC - 1))
                            ins.then_inc(*filled(("up", tag, hf, m2)))
                    for t in range(2):
                        pe.wait_ge(*after(gelu_ready, "FMG".index(tag) * NF + (t + 1) * (NF // 2)))
                        dense_rows([("dn", tag, t)], gelu, wd, NF)

                ffn("F", z, 1, wup, wdn)

                turn("B", 0, z2, lambda t: after(z2_ready, t + 1))
                pe.wait_ge(*after(zt_ready, 5))
                dense_rows([("vb", 0)], zt[:, :, 1:T + 1], wv_b, NC)
                turn("B", 1, z2, lambda t: after(z2_ready, t + 1))
                pe.wait_ge(*after(zt_ready, 6))
                nrm = zt[:, :, 1:T + 1]
                dense(("q", 0), wq_b, 0, P, nrm)
                dense(("kk", 0), wk_b, 0, P, nrm)
                for t in range(NG):
                    if t + 1 < NG:
                        dense(("q", t + 1), wq_b, (t + 1) * P, (t + 2) * P, nrm)
                        dense(("kk", t + 1), wk_b, (t + 1) * P, (t + 2) * P, nrm)
                    for i, name in enumerate(("qf", "kf")):
                        pe.wait_ge(*after(qh_ready, 2 * t + i + 1))
                        ps = take((name, t))
                        mm(ps[:, :], fold[:, :], qh[:, (2 * t + i) % 4, :], start=True, stop=True) \
                            .then_inc(*filled((name, t)))
                dense_rows([("vb", 1)], nrm, wv_b, NC)

                def s_max(t, g):
                    r = slice(32 * g, 32 * g + 32)
                    if g == 0:
                        pe.wait_ge(*after(rqk_ready, 2 * t + 2))
                    banks = take(*[("S", t, g, b) for b in range(3)])
                    parts = ((0, 3, 0), (1, 2, 0), (1, 0, 384), (2, 1, 0))
                    for b, qt, lo in parts:
                        n = (qt + 1) * P
                        mm(banks[b][:, lo:lo + n], rqk[r, t % 2, 0, qt * P:(qt + 1) * P], rqk[r, t % 2, 1, 0:n],
                           start=(lo == 0), stop=False)
                    for b, qt, lo in parts:
                        n = (qt + 1) * P
                        ins = mm(banks[b][:, lo + n - P:lo + n], identb, future, start=False, stop=(b, qt) != (1, 2))
                        if (b, qt) != (1, 2):
                            ins.then_inc(*filled(("S", t, g, b)))

                def s_exp(t, g):
                    r = slice(32 * g, 32 * g + 32)
                    banks = take(*[("ST", t, g, b) for b in range(3)])
                    parts = ((0, 0, 0), (1, 1, 0), (1, 3, 384), (2, 2, 0))
                    for b, jt, lo in parts:
                        n = T - jt * P
                        mm(banks[b][:, lo:lo + n], kp[r, t, jt * P:(jt + 1) * P], qp[r, t, jt * P:T],
                           start=(lo == 0), stop=False)
                    for b, jt, lo in parts:
                        ins = mm(banks[b][:, lo:lo + P], identb, future_t, start=False, stop=(b, jt) != (1, 1))
                        if (b, jt) != (1, 1):
                            ins.then_inc(*filled(("ST", t, g, b)))

                def pv(t, g):
                    n = t * HG + g
                    if g == 0 and t >= 2:
                        pe.wait_ge(*after(osum_ready, t - 1))
                    pe.wait_ge(*after(pt_ready, 3 * n + 3))
                    base = {0: 0, 1: 512, 3: 896, 2: 1024}
                    for jt in range(NT):
                        ins = mm(obank[t % 2][32 * g:32 * g + 32, jt * P:T], vaug[:, jt, n, :],
                                 pt[:, n % NPT, base[jt]:base[jt] + T - jt * P], start=(jt == 0), stop=(jt == NT - 1))
                    ins.then_inc(*one(pt_used))

                def spread_sums(t):
                    pe.wait_ge(*after(osum_ready, t + 1))
                    ps = take(("den", t))
                    mm(ps[:, :], den_row[:, :], osum[:, t % 2, :], start=True, stop=True) \
                        .then_inc(*filled(("den", t)))

                def turn_maxima(t):
                    pe.wait_ge(*after(maxs, 4 * HG * (t + 1)))
                    ps = take(("mt", t))
                    for qt in range(NT):
                        ins = nc.tensor.transpose(ps[:, qt * P:(qt + 1) * P], maxes[:, t % 2, qt, :], ident[:, :])
                    ins.then_inc(*filled(("mt", t)))

                for g in range(HG):
                    s_max(0, g)
                turn_maxima(0)
                pe.wait_ge(*after(vaug_ready, 2))
                for t in range(NG):
                    for g in range(HG):
                        if t + 1 < NG:
                            for a in AHEAD[g]:
                                s_max(t + 1, a)
                        if g == 0:
                            pe.wait_ge(*after(qm_ready, t + 1))
                        s_exp(t, g)
                        if g == 1 and t >= 1:
                            spread_sums(t - 1)
                        if g == HG - 1 and t + 1 < NG:
                            turn_maxima(t + 1)
                        if g >= 1:
                            pv(t, g - 1)
                        elif t >= 1:
                            pv(t - 1, HG - 1)
                pv(NG - 1, HG - 1)
                spread_sums(NG - 1)
                pe.wait_ge(*after(attn_ready, NG))
                dense_rows([("wo", t) for t in range(2)], attn_t, wo_b, NG)
                ffn("M", z, 3, wm1, wm2)
                ffn("G", z, 4, wup, wdn)
                assert count[0] == len(order)

        for s in sems:
            assert not s.per or s.made in (s.per, 0), (s.name, s.per, s.made)


def layouts(i):
    def c(a):
        return np.ascontiguousarray(a)

    def tiles(a, n):
        return a.reshape(n, P).T

    A, Bk, Fn = "L0_attn_a_", "L0_attn_b_", "L0_ffn_"
    i = {k: np.asarray(v) for k, v in i.items()}
    f = np.float32
    x = i[A + "hidden_states"]
    o = {"x": c(np.concatenate([x, np.zeros_like(x[:1])], 0))}
    o["w1"] = c(i[A + "xp_W1"].T)
    o["w2"] = c(i[A + "xp_W2"].T)
    o["wr"], o["wk"], o["wv"] = c(i[A + "r_W"].T), c(i[A + "k_W"].T), c(i[A + "v_W"].T)
    o["wwa"], o["wwb"] = c(i[A + "w_A"].T), c(i[A + "w_B"].T)
    o["wga"] = c(i[A + "g_A"].T)
    o["wgb"] = c(np.concatenate([i[A + "g_B"].T, i[A + "g_b"][None, :]], 0))
    o["wo"] = c(i[A + "o_W"].T)
    src = np.array([h * HD + d if r == 0 else h * HD + (d + HD // 2) % HD
                    for h in range(NH) for r in range(2) for d in range(HD)])
    W, bb = i[Bk + "Wqkv"], i[Bk + "bqkv"]
    o["wq_b"], o["wk_b"], o["wv_b"] = c(W[:, src]), c(W[:, D + src]), c(W[:, 2 * D:3 * D])
    o["bv"], o["bo"], o["b2"] = c(bb[2 * D:3 * D]), i[Bk + "bo"], i[Bk + "b2"]
    o["wm1"], o["wm2"] = i[Bk + "W1"], i[Bk + "W2"]
    o["wo_b"] = np.zeros((NH, 2 * HD, D), f)
    o["wo_b"][:, :HD] = i[Bk + "Wo"].reshape(NH, HD, D)
    o["wo_b"] = o["wo_b"].reshape(NG * P, D)
    minus = np.zeros((P, 1), f)
    minus[HD::32] = -1.0
    o["cols"] = c(np.concatenate([
        tiles(i[A + "xp_mu"], NC), tiles(i[A + "x_bias"], NMIX * NC), tiles(i[A + "w_b"], H), i[A + "bonus"].T,
        tiles(i[A + "gn_w"], NC), tiles(i[A + "gn_b"], NC), tiles(i[Bk + "ln1_g"], NC), tiles(i[Bk + "ln1_b"], NC),
        tiles(i[Bk + "ln2_g"], NC), tiles(i[Bk + "ln2_b"], NC), tiles(bb[src], NG), tiles(bb[D + src], NG),
        tiles(i[Bk + "b1"], NF), tiles(i[Fn + "up_bias"], NF), minus], 1))
    o["b_con"], o["down_b"], o["w_con"] = i[Fn + "b_con"], i[Fn + "down_bias"], i[Fn + "W_con"]
    o["w_exp_t"] = c(np.concatenate([i[Fn + "W_exp"].T, i[Fn + "b_exp"][:, None]], 1))
    n = np.arange(FF)
    parts = []
    for kind in range(3):
        for name in ("up_weights", "down_weights"):
            w = i[Fn + name]
            byst = []
            for s in range(STAGES):
                S = 1 << s
                bit = (n >> s) & 1
                k = (n // (2 * S)) * S + n % S
                a_, b_ = ((bit, bit), (bit, 1 - bit), (1 - bit, bit))[kind]
                byst.append(w[s][k, a_, b_])
            parts.append(np.stack(byst, 1).reshape(NF, P, STAGES).transpose(1, 0, 2))
    o["bw"] = c(np.stack(parts, 1).reshape(P, 3, 2, NF, STAGES))
    q = np.arange(P)
    o["ident"] = np.eye(P, dtype=f)
    o["perm"] = c(np.stack([(q[:, None] == (q[None, :] ^ (1 << s))).astype(f) for s in range(LOW)], 1))
    o["fold"] = c(((q[:, None] // 32 == q[None, :] // 32) & (q[None, :] % 32 < HD)
                   & (q[:, None] % HD == q[None, :] % HD)).astype(f))
    o["den_row"] = (q[:, None] == q[None, :] // 32 * 32 + HD).astype(f)
    freq = (1.0 / 10000.0 ** (np.arange(0, HD, 2, dtype=f) / f(HD))).astype(f)
    ang = np.arange(T, dtype=f)[None, :] * np.concatenate([freq, freq])[:, None]
    sign = np.where(np.arange(HD) < HD // 2, -1.0, 1.0).astype(f)[:, None]
    o["rope"] = c(np.tile(np.concatenate([np.cos(ang), np.sin(ang) * sign], 0).astype(f), (HG, 1)))
    j, k = q[:, None], q[None, :]
    masks = [j == k] + [(j // (2 * s) == k // (2 * s)) & (j // s % 2 == 0) & (k // s % 2 == 1)
                        for s in LEVELS[1:]]
    o["masks"] = c(np.stack([np.eye(P, dtype=f), np.where(k > j, NEG, 0.0), np.where(j > k, NEG, 0.0)]
                           + [m.astype(f) for m in masks], 1).astype(f))
    return o


def kernel(**inputs):
    import concourse.bacc as _bacc
    from concourse.bass_utils import run_bass_kernel_spmd as _run

    nc = _bacc.Bacc("TRN2", target_bir_lowering=False, num_devices=1)
    arrays, io = {}, {}
    for name, a in layouts(inputs).items():
        arrays[f"in_{name}"] = np.ascontiguousarray(a)
        io[name] = nc.dram_tensor(f"in_{name}", a.shape, mybir.dt.from_np(a.dtype), kind="ExternalInput").ap()
    out = nc.dram_tensor("out", (B, T, D), F32, kind="ExternalOutput").ap()
    hybrid_kernel(nc, io, out)
    r = _run(nc, [arrays], core_ids=[0])
    return r.results[0]["out"]
```
